# Optimizing a Trainium2 kernel written in Bass

```python
import numpy as np
import jax
import jax.numpy as jnp

def _softmax(x, axis=-1):
    return jax.nn.softmax(x, axis=axis)

def _gelu(x):
    return jax.nn.gelu(x, approximate=True)

def _silu(x):
    return jax.nn.silu(x)

def _sigmoid(x):
    return jax.nn.sigmoid(x)

def _layernorm(x, axis=-1, eps=1e-05):
    m = jnp.mean(x, axis=axis, keepdims=True)
    v = jnp.var(x, axis=axis, keepdims=True)
    return (x - m) / jnp.sqrt(v + eps)

def _scatter_add(tgt, idx, src, axis=0):
    return tgt.at[idx].add(src)

def _segment_sum(src, seg, n):
    return jax.ops.segment_sum(src, seg, n)
kernel_name = 'mk_gnn_ffn_d1_gnn_r32_027c42'

def setup_inputs(seed: int=0):
    np.random.seed(seed)
    _w = jnp.asarray

    def _rec_inputs():
        import jax
        import jax.numpy as jnp
        _gk = jax.random.key(seed)
        x = -8.776e-05 + 1 * jax.random.normal(jax.random.fold_in(_gk, 1), (3125, 256), jnp.float32)
        src = jax.random.randint(jax.random.fold_in(_gk, 2), (50000,), 0, 3125, jnp.int32)
        dst = jax.random.randint(jax.random.fold_in(_gk, 3), (50000,), 0, 3125, jnp.int32)
        _o = jnp.argsort(dst, stable=True)
        src = src[_o]
        dst = dst[_o]
        return (x, src, dst)
    x, src, dst = _rec_inputs()

    def _L0_gnn_setup():
        import jax, jax.numpy as jnp
        import numpy as np
        N = 625
        E = 10000
        HID = 256
        HEADS = 8
        HD = HID // HEADS
        key = jax.random.key(seed)
        ks = jax.random.split(key, 12)
        scale = 1.0 / np.sqrt(HID).astype(np.float32)

        def lin_w(k):
            return jax.random.normal(k, (HID, HID), jnp.float32) * scale

        def lin_b(k):
            return jax.random.normal(k, (HID,), jnp.float32) * 0.01
        return {'h': jax.random.normal(ks[0], (N, HID), jnp.float32), 'Wq': lin_w(ks[1]), 'bq': lin_b(ks[2]), 'Wk': lin_w(ks[3]), 'bk': lin_b(ks[4]), 'Wv': lin_w(ks[5]), 'bv': lin_b(ks[6]), 'Wo': lin_w(ks[7]), 'bo': lin_b(ks[8]), 'rows': jax.random.randint(ks[9], (E,), 0, N), 'cols': jax.random.randint(ks[10], (E,), 0, N)}
    _L0_gnn_all = _L0_gnn_setup()
    _L0_gnn_in = {k: v for k, v in _L0_gnn_all.items() if k in ('Wq', 'bq', 'Wk', 'bk', 'Wv', 'bv', 'Wo', 'bo')}
    del _L0_gnn_all

    def _L0_ffn_setup():
        import jax, jax.numpy as jnp
        import numpy as np
        TOP_K = 2
        LN_EPS = 1e-05
        key = jax.random.key(seed)
        ks = jax.random.split(key, 8)
        B, S, D, E, H = (16, 1024, 256, 8, 1024)
        x = jax.random.normal(ks[0], (B, S, D), dtype=jnp.float32)
        Wr = jax.random.normal(ks[1], (D, E), dtype=jnp.float32) * 0.1
        br = jnp.zeros((E,), dtype=jnp.float32)
        ln_g = jnp.ones((E, D), dtype=jnp.float32)
        ln_b = jnp.zeros((E, D), dtype=jnp.float32)
        W1 = jax.random.normal(ks[2], (E, D, H), dtype=jnp.float32) * (1.0 / np.sqrt(D))
        b1 = jnp.zeros((E, H), dtype=jnp.float32)
        W2 = jax.random.normal(ks[3], (E, H, D), dtype=jnp.float32) * (1.0 / np.sqrt(H))
        b2 = jnp.zeros((E, D), dtype=jnp.float32)
        return {'x': x, 'Wr': Wr, 'br': br, 'ln_g': ln_g, 'ln_b': ln_b, 'W1': W1, 'b1': b1, 'W2': W2, 'b2': b2}
    _L0_ffn_all = _L0_ffn_setup()
    _L0_ffn_in = {k: v for k, v in _L0_ffn_all.items() if k in ('Wr', 'br', 'ln_g', 'ln_b', 'W1', 'b1', 'W2', 'b2')}
    del _L0_ffn_all
    return {'x': x, 'src': src, 'dst': dst, 'L0_gnn_Wq': _L0_gnn_in['Wq'], 'L0_gnn_bq': _L0_gnn_in['bq'], 'L0_gnn_Wk': _L0_gnn_in['Wk'], 'L0_gnn_bk': _L0_gnn_in['bk'], 'L0_gnn_Wv': _L0_gnn_in['Wv'], 'L0_gnn_bv': _L0_gnn_in['bv'], 'L0_gnn_Wo': _L0_gnn_in['Wo'], 'L0_gnn_bo': _L0_gnn_in['bo'], 'L0_ffn_Wr': _L0_ffn_in['Wr'], 'L0_ffn_br': _L0_ffn_in['br'], 'L0_ffn_ln_g': _L0_ffn_in['ln_g'], 'L0_ffn_ln_b': _L0_ffn_in['ln_b'], 'L0_ffn_W1': _L0_ffn_in['W1'], 'L0_ffn_b1': _L0_ffn_in['b1'], 'L0_ffn_W2': _L0_ffn_in['W2'], 'L0_ffn_b2': _L0_ffn_in['b2']}

def reference(x, src, dst, L0_gnn_Wq, L0_gnn_bq, L0_gnn_Wk, L0_gnn_bk, L0_gnn_Wv, L0_gnn_bv, L0_gnn_Wo, L0_gnn_bo, L0_ffn_Wr, L0_ffn_br, L0_ffn_ln_g, L0_ffn_ln_b, L0_ffn_W1, L0_ffn_b1, L0_ffn_W2, L0_ffn_b2):
    import jax
    import jax.numpy as jnp

    def _L0_gnn_ref(h, Wq, bq, Wk, bk, Wv, bv, Wo, bo, rows, cols):
        import jax, jax.numpy as jnp
        import numpy as np
        N = 625
        E = 10000
        HID = 256
        HEADS = 8
        HD = HID // HEADS
        n = h.shape[0]
        scaling = HD ** (-0.5)
        q = (h @ Wq + bq).reshape(n, HD, HEADS) * scaling
        k = (h @ Wk + bk).reshape(n, HD, HEADS)
        v = (h @ Wv + bv).reshape(n, HD, HEADS)
        s = jnp.einsum('edh,edh->eh', q[rows], k[cols])
        m = jax.ops.segment_max(s, rows, num_segments=n)
        e = jnp.exp(s - m[rows])
        z = jax.ops.segment_sum(e, rows, num_segments=n)
        attn = e / z[rows]
        out = jax.ops.segment_sum(attn[:, None, :] * v[cols], rows, num_segments=n)
        return out.reshape(n, -1) @ Wo + bo

    def _L0_ffn_ref(x, Wr, br, ln_g, ln_b, W1, b1, W2, b2):
        import jax, jax.numpy as jnp
        import numpy as np
        TOP_K = 2
        LN_EPS = 1e-05
        B, S, D = x.shape
        N = B * S
        xt = x.reshape(N, D)
        logits = xt @ Wr + br
        probs = jax.nn.softmax(logits, axis=-1)
        top_p, top_idx = jax.lax.top_k(probs, TOP_K)
        weights = top_p / top_p.sum(axis=-1, keepdims=True)
        mu = xt.mean(axis=-1, keepdims=True)
        var = ((xt - mu) ** 2).mean(axis=-1, keepdims=True)
        xn = (xt - mu) * jax.lax.rsqrt(var + LN_EPS)
        xe = xn[None, :, :] * ln_g[:, None, :] + ln_b[:, None, :]
        h = jax.nn.gelu(jnp.einsum('end,edh->enh', xe, W1) + b1[:, None, :], approximate=False)
        y = jnp.einsum('enh,ehd->end', h, W2) + b2[:, None, :]
        y_tok = jnp.transpose(y, (1, 0, 2))
        sel = jnp.take_along_axis(y_tok, top_idx[:, :, None], axis=1)
        out = (weights[:, :, None] * sel).sum(axis=1)
        return out.reshape(B, S, D)
    x = x + _L0_gnn_ref(_layernorm(x, axis=-1), L0_gnn_Wq, L0_gnn_bq, L0_gnn_Wk, L0_gnn_bk, L0_gnn_Wv, L0_gnn_bv, L0_gnn_Wo, L0_gnn_bo, src, dst)
    x = x + _L0_ffn_ref(_layernorm(x, axis=-1)[None], L0_ffn_Wr, L0_ffn_br, L0_ffn_ln_g, L0_ffn_ln_b, L0_ffn_W1, L0_ffn_b1, L0_ffn_W2, L0_ffn_b2)[0]
    return x

_drawn_inputs = setup_inputs


def setup_inputs(seed=0):
    import zlib

    import numpy as np

    out = dict(_drawn_inputs(seed))
    spreads = {'L0_ffn_br': (0.0, 0.1),
     'L0_ffn_ln_g': (1.0, 0.2),
     'L0_ffn_ln_b': (0.0, 0.1),
     'L0_ffn_b1': (0.0, 0.1),
     'L0_ffn_b2': (0.0, 0.1)}
    factors = {'L0_gnn_bq': 4.407, 'L0_gnn_bk': 8.0}
    for name, (base, spread) in spreads.items():
        noise = np.random.default_rng([zlib.crc32(name.encode()), seed]).standard_normal(out[name].shape)
        drawn = base * np.exp(spread * noise) if base else spread * noise
        out[name] = jnp.asarray(drawn.astype(out[name].dtype))
    for name, factor in factors.items():
        out[name] = (out[name] * factor).astype(out[name].dtype)
    return out
```

```python
from contextlib import ExitStack

import concourse.bass as bass
from concourse import mybir

F32 = mybir.dt.float32
I32 = mybir.dt.int32
U32 = mybir.dt.uint32
ALU = mybir.AluOpType
ACT = mybir.ActivationFunctionType
AX = mybir.AxisListType

P = 128
BIG = 1.0e30
EPS = 1e-5


def gnn_moe_kernel(nc, x, src, dst, Wq, bq, Wk, bk, Wv, bv, Wo, bo, Wr, br, ln_g, ln_b, W1, b1, W2, b2, out):
    N, D = x.shape
    E = src.shape[0]
    NX, H = W1.shape[0], W1.shape[2]
    HEADS, HD = 8, D // 8
    KC = D // P
    HC = H // P
    SCALE = float(HD) ** -0.5

    NBF = N // P
    TAIL = N - NBF * P
    NBR = NBF + 1
    NB = NBR + 1
    NT = 416
    assert NT % 16 == 0 and NT * P >= E + NBR * (P - 1) and NB % 2 == 0
    SORT = 1 << 16
    SC = SORT // P
    LOGN, LOGP = 16, 7
    SHIFT = 12
    RADIX = 1 << SHIFT
    PAD_DST = RADIX - 1
    FILL = ((NB - 1) * P + P - 1) * RADIX + PAD_DST
    assert N < PAD_DST and FILL < 1 << 24 and SORT >= NT * P
    ER = 125
    EC = E // ER
    assert ER * EC == E and EC + NBR <= SC

    TE = (2 * N + NX * (P - 1)) // P
    UE = 4
    NS = (TE + UE) * P
    assert TE % UE == 0

    ctx = ExitStack()
    with ctx:
        def sem(name):
            return ctx.enter_context(nc.semaphore(name))

        def dram(name, shape):
            return nc.dram_tensor(name, shape, F32, kind="Internal").ap()

        k_table = dram("k_table", [NB * P, D])
        v_table = dram("v_table", [NB * P, D])

        def sb(name, shape, dt=F32, c=ctx):
            return c.enter_context(nc.sbuf_tensor(name, shape, dt))

        def psum(name, shape, c, dt=F32):
            return c.enter_context(nc.psum_tensor(name, shape, dt))

        ident = sb("ident", [P, P])
        ones = sb("ones", [P, P])
        ones_row = ones[0:1, :]
        wts = sb("wts", [P, 2, NB])
        row_i = sb("row_i", [P, 2, NB], I32)
        tile_ex = sb("tile_ex", [P, NS // P], I32)
        lane = sb("lane", [P, 1], I32)
        lane_f = sb("lane_f", [P, 1])
        stats = sb("stats", [P, NB, 6])
        mean = sb("mean", [P, NB])
        var = sb("var", [P, NB])
        half_diff = sb("half_diff", [P, NB])
        rstd = sb("rstd", [P, NB])
        minus_half = sb("minus_half", [P, NB])

        def block_of(table, b):
            return table[:, bass.ds(b, 1), :].rearrange("p a d -> p (a d)")

        def mean_and_variance(link):
            link(nc.vector.tensor_tensor(mean[:, :], stats[:, :, 1], stats[:, :, 4], ALU.add))
            link(nc.vector.tensor_tensor(half_diff[:, :], stats[:, :, 1], stats[:, :, 4], ALU.subtract))
            link(nc.vector.tensor_tensor(var[:, :], stats[:, :, 2], stats[:, :, 5], ALU.add))
            link(nc.vector.tensor_scalar(mean[:, :], mean[:, :], 0.5, None, ALU.mult))
            link(nc.vector.tensor_scalar(half_diff[:, :], half_diff[:, :], 0.5, None, ALU.mult))
            link(nc.vector.tensor_scalar(var[:, :], var[:, :], 1.0 / D, EPS, ALU.mult, ALU.add))
            link(nc.vector.tensor_tensor(half_diff[:, :], half_diff[:, :], half_diff[:, :], ALU.mult))
            link(nc.vector.tensor_tensor(var[:, :], var[:, :], half_diff[:, :], ALU.add))

        gnn = ExitStack()
        gnn.__enter__()
        xres = sb("xres", [P, NB, D], F32, gnn)
        q_table = sb("q_table", [P, NB, D], F32, gnn)
        key_i = sb("key_i", [P, SC], I32, gnn)
        dst_i = sb("dst_i", [P, SC], I32, gnn)
        src_f = sb("src_f", [P, SC], F32, gnn)
        rel_f = sb("rel_f", [P, SC], F32, gnn)
        real_f = sb("real_f", [P, SC], F32, gnn)
        blk_i = sb("blk_i", [P, SC], I32, gnn)
        with ExitStack() as st:
            srcs = sb("srcs", [ER, EC], I32, st)
            dsts = sb("dsts", [ER, EC], I32, st)
            blkf = sb("blkf", [ER, EC], F32, st)
            tmp_i = sb("tmp_i", [P, SC], I32, st)
            tmp_f = sb("tmp_f", [P, SC], F32, st)
            blkno_i = sb("blkno_i", [P, NBR], I32, st)
            blkno = sb("blkno", [P, NBR], F32, st)
            inblk = sb("inblk", [ER, NBR, EC], F32, st)
            cnt = sb("cnt", [ER, NBR], F32, st)
            need_i = sb("need_i", [P, NBR], I32, st)
            need = sb("need", [P, NBR], F32, st)
            padkey = sb("padkey", [P, NBR], F32, st)
            dir_i = sb("dir_i", [P, LOGP], I32, st)
            dirs = sb("dirs", [P, LOGP], F32, st)
            keys = [sb(f"keys{i}", [P, SC], F32, st) for i in range(2)]
            half = sb("half", [P, SC // 2], F32, st)
            xhat = sb("xhat", [P, NB, D], F32, st)
            xin = sb("xin", [P, 2, D], F32, st)
            xT = sb("xT", [P, 2, KC, P], F32, st)
            wq_sb = sb("wq_sb", [P, KC, D], F32, st)
            wkv_sb = sb("wkv_sb", [P, KC, 2 * D], F32, st)
            bq_sb = sb("bq_sb", [1, D], F32, st)
            bkv_sb = sb("bkv_sb", [1, 2 * D], F32, st)
            kv_out = sb("kv_out", [P, 2, 2 * D], F32, st)
            xT_ps = psum("xT_ps", [P, 2, KC, P], st)
            q_ps = psum("q_ps", [P, 2, D], st)
            kv_ps = [psum(f"kv_ps{i}", [P, 2 * D], st) for i in range(2)]
            cnt_ps = psum("cnt_ps", [P, NBR], st)
            swap_ps = [psum(f"swap_ps{i}", [P, SC], st) for i in range(2)]

            edges_in = sem("edges_in")
            x_in = sem("x_in")
            w_in = sem("w_in")
            consts = sem("consts")
            cdone = sem("cdone")
            cleared = sem("cleared")
            counted = sem("counted")
            cnt_sum = sem("cnt_sum")
            stats_made = sem("stats_made")
            var_ready = sem("var_ready")
            rstd_ready = sem("rstd_ready")
            xhat_ready = sem("xhat_ready")
            xin_ready = sem("xin_ready")
            xin_free = sem("xin_free")
            xT_made = sem("xT_made")
            xT_ready = sem("xT_ready")
            q_made = sem("q_made")
            kv_made = sem("kv_made")
            q_kept = sem("q_kept")
            kv_ready = sem("kv_ready")
            k_stored = [sem(f"k_stored{i}") for i in range(2)]
            sort_step = sem("sort_step")
            to_swap = sem("to_swap")
            swapped = sem("swapped")
            decoded = sem("decoded")

            with nc.Block() as block:
                @block.sync
                def _(sp):
                    for j in range(2):
                        sp.sem_inc(k_stored[j], 32)
                    sp.dma_start(srcs[:, :], src.rearrange("(p t) -> p t", p=ER)).then_inc(edges_in, 16)
                    sp.dma_start(dsts[:, :], dst.rearrange("(p t) -> p t", p=ER)).then_inc(edges_in, 16)
                    sp.wait_ge(cleared, 1)
                    sp.dma_start(xres[:, 0:NBF, :],
                                 x[0:NBF * P, :].rearrange("(b p) d -> p b d", p=P)).then_inc(x_in, 16)
                    sp.dma_start(xres[0:TAIL, NBF, :], x[NBF * P:N, :]).then_inc(x_in, 16)
                    sp.dma_start(wq_sb[:, :, :], Wq.rearrange("(c p) n -> p c n", p=P)).then_inc(w_in, 16)
                    sp.dma_start(wkv_sb[:, :, 0:D], Wk.rearrange("(c p) n -> p c n", p=P)).then_inc(w_in, 16)
                    sp.dma_start(wkv_sb[:, :, D:2 * D], Wv.rearrange("(c p) n -> p c n", p=P)).then_inc(w_in, 16)
                    sp.dma_start(bq_sb[:, :], bq.rearrange("(a n) -> a n", a=1)).then_inc(w_in, 16)
                    sp.dma_start(bkv_sb[:, 0:D], bk.rearrange("(a n) -> a n", a=1)).then_inc(w_in, 16)
                    sp.dma_start(bkv_sb[:, D:2 * D], bv.rearrange("(a n) -> a n", a=1)).then_inc(w_in, 16)
                    with sp.Fori(0, NB // 2) as i:
                        for j in range(2):
                            rows = bass.ds((i * 2 + j) * P, P)
                            sp.wait_ge(kv_ready, i * 2 + j + 1)
                            sp.dma_start(k_table[rows, :], kv_out[:, j, 0:D]).then_inc(k_stored[j], 16)
                            sp.dma_start(v_table[rows, :], kv_out[:, j, D:2 * D]).then_inc(k_stored[j], 16)
                    for j in range(2):
                        sp.wait_ge(k_stored[j], 16 * NB + 32)

                @block.gpsimd
                def _(pool):
                    nc.gpsimd.memset(ident[:, :], 0.0).then_inc(consts, 1)
                    nc.gpsimd.memset(ones[:, :], 1.0).then_inc(consts, 1)
                    pool.wait_ge(consts, 2)
                    nc.gpsimd.affine_select(out=ident[:, :], in_=ident[:, :], compare_op=ALU.not_equal, fill=1.0,
                                            base=0, pattern=[[-1, P]], channel_multiplier=1).then_inc(consts, 1)
                    nc.gpsimd.iota(lane[:, :], [[0, 1]], base=0, channel_multiplier=1).then_inc(consts, 1)
                    nc.gpsimd.iota(blkno_i[:, :], [[1, NBR]], base=0, channel_multiplier=0).then_inc(consts, 1)
                    nc.gpsimd.memset(minus_half[:, :], -0.5).then_inc(consts, 1)
                    pool.wait_ge(consts, 6)
                    pool.wait_ge(var_ready, 1)
                    nc.gpsimd.tensor_tensor(rstd[:, :], var[:, :], minus_half[:, :], ALU.pow).then_inc(rstd_ready, 1)
                    with pool.Fori(0, NB // 2) as i:
                        for j in range(2):
                            b = i * 2 + j
                            pool.wait_ge(xhat_ready, b + 1)
                            pool.wait_ge(xin_free, b + 1)
                            nc.gpsimd.tensor_copy(xin[:, j, :], block_of(xhat, b)).then_inc(xin_ready, 1)

                @block.vector
                def _(dve):
                    steps = [0]

                    def link(ins):
                        steps[0] += 1
                        ins.then_inc(cdone, 1)
                        dve.wait_ge(cdone, steps[0])

                    nc.vector.memset(xres[:, NBF:NB, :], 0.0).then_inc(cleared, 1)
                    dve.wait_ge(x_in, 32)
                    with dve.Fori(0, NB // 2) as i:
                        for j in range(2):
                            b = i * 2 + j
                            nc.vector.bn_stats(stats[:, bass.ds(b, 1), :].rearrange("p a s -> p (a s)"),
                                               block_of(xres, b)).then_inc(stats_made, 1)
                    dve.wait_ge(stats_made, NB)
                    mean_and_variance(link)
                    nc.vector.tensor_copy(var[:, :], var[:, :]).then_inc(var_ready, 1)
                    dve.wait_ge(rstd_ready, 1)
                    with dve.Fori(0, NB // 2) as i:
                        for j in range(2):
                            b = i * 2 + j
                            nc.vector.tensor_scalar(block_of(xhat, b), block_of(xres, b), mean[:, bass.ds(b, 1)],
                                                    rstd[:, bass.ds(b, 1)], ALU.subtract,
                                                    ALU.mult).then_inc(xhat_ready, 1)

                    dve.wait_ge(edges_in, 32)
                    dve.wait_ge(consts, 5)
                    link(nc.vector.tensor_copy(lane_f[:, :], lane[:, :]))
                    link(nc.vector.tensor_copy(blkno[:, :], blkno_i[:, :]))
                    link(nc.vector.tensor_scalar(tmp_i[0:ER, 0:EC], srcs[:, :], LOGP, None, ALU.logical_shift_right))
                    link(nc.vector.tensor_copy(blkf[:, :], tmp_i[0:ER, 0:EC]))
                    for b in range(NBR):
                        nc.vector.tensor_scalar(inblk[:, b, :], blkf[:, :], float(b), None, ALU.is_equal)
                    link(nc.vector.tensor_scalar(padkey[:, :], blkno[:, :], float(P * RADIX),
                                                 float((P - 1) * RADIX + PAD_DST - FILL), ALU.mult, ALU.add))
                    nc.vector.tensor_reduce(cnt[:, :], inblk[:, :, :], AX.X, ALU.add).then_inc(counted, 1)
                    for j in range(LOGP):
                        nc.vector.tensor_scalar(dir_i[:, j:j + 1], lane[:, :], j, 1, ALU.logical_shift_right,
                                                ALU.bitwise_and)
                    link(nc.vector.memset(keys[1][:, :], float(FILL)))
                    link(nc.vector.tensor_copy(dirs[:, :], dir_i[:, :]))
                    link(nc.vector.tensor_scalar(dirs[:, :], dirs[:, :], -2.0, 1.0, ALU.mult, ALU.add))
                    link(nc.vector.scalar_tensor_tensor(out=keys[1][0:ER, 0:EC], in0=srcs[:, :], scalar=float(RADIX),
                                                        in1=dsts[:, :], op0=ALU.mult, op1=ALU.add))
                    dve.wait_ge(cnt_sum, 1)
                    link(nc.vector.tensor_scalar(need[:, :], cnt_ps[:, :], -1.0, float(SORT), ALU.mult, ALU.add))
                    link(nc.vector.tensor_copy(need_i[:, :], need[:, :]))
                    link(nc.vector.tensor_scalar(need_i[:, :], need_i[:, :], P - 1, None, ALU.bitwise_and))
                    link(nc.vector.tensor_copy(need[:, :], need_i[:, :]))
                    link(nc.vector.scalar_tensor_tensor(out=need[:, :], in0=need[:, :], scalar=lane_f[:, 0:1],
                                                        in1=padkey[:, :], op0=ALU.is_gt, op1=ALU.mult))
                    link(nc.vector.tensor_scalar(keys[1][:, EC:EC + NBR], need[:, :], float(FILL), None, ALU.add))

                    n, swaps = 0, 0
                    source = keys[1]

                    def column_bit(bit, low):
                        if low:
                            return bit if bit < LOGP else (bit - LOGP if bit >= 2 * LOGP else None)
                        return bit - LOGP

                    def settle(ins):
                        nonlocal n
                        n += 1
                        ins.then_inc(sort_step, 1)
                        dve.wait_ge(sort_step, n)

                    def exchanges(bits, low, after_swap, swap_next, to_come=0):
                        nonlocal n, source
                        for left, bit in zip(range(len(bits) - 1, -1, -1), bits):
                            w = 1 << column_bit(bit, low)
                            target = keys[1 - (left + to_come) % 2]
                            s = source[:, :].rearrange("p (h t w) -> p h t w", t=2, w=w)
                            d = target[:, :].rearrange("p (h t w) -> p h t w", t=2, w=w)
                            first, second = s[:, :, 0, :], s[:, :, 1, :]
                            if left == len(bits) - 1 and after_swap:
                                second = half[:, :].rearrange("p (h w) -> p h w", w=w)
                                settle(nc.vector.tensor_copy(second, s[:, :, 1, :]))
                            lesser = nc.vector.tensor_tensor(d[:, :, 0, :], first, second, ALU.min)
                            if left == 0 and swap_next:
                                settle(lesser)
                            greater = nc.vector.tensor_tensor(d[:, :, 1, :], first, second, ALU.max)
                            if left == 0 and swap_next:
                                greater.then_inc(to_swap, 1)
                            else:
                                settle(greater)
                            source = target

                    def negate(bit, swap_next=False):
                        col = column_bit(bit, True)
                        s = source[:, :]
                        by = dirs[:, bit - LOGP:bit - LOGP + 1] if col is None else -1.0
                        if col is not None:
                            s = s.rearrange("p (h t w) -> p h t w", t=2, w=1 << col)[:, :, 1, :]
                        ins = nc.vector.tensor_scalar(s, s, by, None, ALU.mult)
                        if swap_next:
                            ins.then_inc(to_swap, 1)
                        else:
                            settle(ins)

                    def swap_layout():
                        nonlocal swaps, source
                        swaps += 1
                        dve.wait_ge(swapped, swaps)
                        source = swap_ps[(swaps - 1) % 2]

                    low_bits = list(range(LOGP - 1, -1, -1))
                    for k in range(1, LOGP + 1):
                        if k > 1:
                            negate(k - 1)
                        negate(k)
                        exchanges(list(range(k - 1, -1, -1)), True, False, False,
                                  to_come=sum(range(k + 1, LOGP + 1)))
                    for k in range(LOGP + 1, LOGN + 1):
                        negate(k - 1, swap_next=(k == LOGN))
                        if k < LOGN:
                            negate(k, swap_next=True)
                        swap_layout()
                        exchanges(list(range(k - 1, LOGP - 1, -1)), False, True, True)
                        swap_layout()
                        exchanges(low_bits, True, True, k == LOGN)
                    swap_layout()

                    n = 0

                    def then(ins):
                        nonlocal n
                        n += 1
                        ins.then_inc(decoded, 1)
                        dve.wait_ge(decoded, n)

                    then(nc.vector.tensor_copy(key_i[:, :], source[:, :]))
                    then(nc.vector.tensor_scalar(tmp_i[:, :], key_i[:, :], SHIFT, None, ALU.logical_shift_right))
                    then(nc.vector.tensor_copy(src_f[:, :], tmp_i[:, :]))
                    then(nc.vector.tensor_scalar(blk_i[:, :], tmp_i[:, :], LOGP, None, ALU.logical_shift_right))
                    then(nc.vector.tensor_scalar(tmp_i[:, :], tmp_i[:, :], P - 1, None, ALU.bitwise_and))
                    then(nc.vector.tensor_copy(rel_f[:, :], tmp_i[:, :]))
                    then(nc.vector.tensor_scalar(tmp_i[:, :], key_i[:, :], RADIX - 1, None, ALU.bitwise_and))
                    then(nc.vector.tensor_copy(tmp_f[:, :], tmp_i[:, :]))
                    then(nc.vector.tensor_scalar(real_f[:, :], tmp_f[:, :], float(PAD_DST), None, ALU.is_lt))
                    then(nc.vector.tensor_scalar(dst_i[:, :], tmp_f[:, :], float(N - 1), None, ALU.min))

                @block.tensor
                def _(pe):
                    pe.wait_ge(consts, 3)
                    pe.sem_inc(xin_free, 2)

                    def project(b, j):
                        pe.wait_ge(xin_ready, b + 1)
                        for c in range(KC):
                            ins = nc.tensor.transpose(xT_ps[:, j, c, :], xin[:, j, c * P:(c + 1) * P], ident[:, :])
                        ins.then_inc(xT_made, 1)
                        pe.wait_ge(xT_ready, b + 1)
                        pe.wait_ge(w_in, 96)
                        for c in range(KC):
                            nc.tensor.matmul(q_ps[:, j, :], xT[:, j, c, :], wq_sb[:, c, :], start=(c == 0), stop=False)
                        nc.tensor.matmul(q_ps[:, j, :], ones_row, bq_sb[:, :], start=False, stop=True).then_inc(q_made, 1)
                        for c in range(KC):
                            ins = nc.tensor.matmul(kv_ps[j][:, :], xT[:, j, c, :], wkv_sb[:, c, :], start=(c == 0), stop=False)
                        ins.then_inc(xin_free, 1)
                        nc.tensor.matmul(kv_ps[j][:, :], ones_row, bkv_sb[:, :], start=False, stop=True).then_inc(kv_made, 1)

                    def swap(i, j):
                        pe.wait_ge(to_swap, i + 1)
                        for g in range(SC // P):
                            ins = nc.tensor.transpose(swap_ps[j][:, g * P:(g + 1) * P], keys[1][:, g * P:(g + 1) * P], ident[:, :])
                        ins.then_inc(swapped, 1)

                    HEAD = NB - 2 * (LOGN - LOGP)
                    with pe.Fori(0, HEAD // 2) as i:
                        project(i * 2, 0)
                        project(i * 2 + 1, 1)
                    pe.wait_ge(counted, 1)
                    nc.tensor.matmul(cnt_ps[:, :], ones[0:ER, :], cnt[:, :], start=True, stop=True).then_inc(cnt_sum, 1)
                    with pe.Fori(0, LOGN - LOGP) as i:
                        swap(i * 2, 0)
                        project(i * 2 + HEAD, 0)
                        swap(i * 2 + 1, 1)
                        project(i * 2 + HEAD + 1, 1)
                    swap(2 * (LOGN - LOGP), 0)

                @block.scalar
                def _(act):
                    with act.Fori(0, NB // 2) as i:
                        for j in range(2):
                            b = i * 2 + j
                            act.wait_ge(xT_made, b + 1)
                            nc.scalar.activation(xT[:, j, :, :], xT_ps[:, j, :, :], ACT.Copy).then_inc(xT_ready, 1)
                            act.wait_ge(q_made, b + 1)
                            nc.scalar.activation(block_of(q_table, b), q_ps[:, j, :], ACT.Copy,
                                                 scale=SCALE).then_inc(q_kept, 1)
                            act.wait_ge(kv_made, b + 1)
                            act.wait_ge(k_stored[j], i * 32 + 32)
                            nc.scalar.activation(kv_out[:, j, :], kv_ps[j][:, :], ACT.Copy).then_inc(kv_ready, 1)

        U = 16
        TR = NT // U
        scores = sb("scores", [P, NT, HEADS], F32, gnn)
        weights = sb("weights", [P, NT + 2, HEADS], F32, gnn)
        lane_row = sb("lane_row", [P, P], F32, gnn)
        lane_row_i = sb("lane_row_i", [P, P], I32, gnn)
        idx_ring = sb("idx_ring", [P, 2, U // 2], I32, gnn)
        row_ring = sb("row_ring", [P, U, D], F32, gnn)
        onehot = sb("onehot", [P, 4, P], F32, gnn)

        def gather_rows(pool, table, fetched, used, copied, turns, extra):
            H8 = U // 2

            def copy_indices(first, s, count):
                nc.gpsimd.tensor_copy(idx_ring[:, s, :], dst_i[:, bass.ds(first, H8)]).then_inc(copied, 1)

            def gather(slot, free):
                pool.wait_ge(used, free)
                pool.sem_inc(turns, 1)
                nc.gpsimd.indirect_dma_start(
                    row_ring[:, slot, :], None, table,
                    bass.IndirectOffsetOnAxis(idx_ring[:, slot // H8, slot % H8:slot % H8 + 1].bitcast(U32), 0)).then_inc(fetched[slot], 16)

            nc.gpsimd.tensor_copy(idx_ring[:, 0, :], dst_i[:, 0:H8]).then_inc(copied, 1)
            with pool.Fori(0, TR) as i:
                for half in range(2):
                    pool.wait_ge(copied, i * 2 + half + 1)
                    for j in range(H8):
                        gather(half * H8 + j, i * U + half * H8 + j + 1)
                        if j == H8 - 2:
                            pool.wait_ge(used, i * U + half * H8 + U)
                            copy_indices(i * U + (half + 1) * H8, 1 - half, None)
            pool.wait_ge(copied, TR * 2 + 1)
            for slot in range(extra):
                gather(slot, NT + slot + 1)
            for slot in range(U):
                pool.wait_ge(fetched[slot], 16 * (TR + (slot < extra)))

        with ExitStack() as st:
            onehotT = sb("onehotT", [P, 2, P], F32, st)
            prod = sb("prod", [P, 2, D], F32, st)
            oT_ps = [psum(f"oT_ps{i}", [P, 512], st) for i in range(2)]
            qe_ps = [psum(f"qe_ps{i}", [P, 512], st) for i in range(2)]
            k_in = [sem(f"k_in{i}") for i in range(U)]
            k_copied = sem("k_copied")
            k_turns = sem("k_turns")
            lane_made = sem("lane_made")
            hot_ready = sem("hot_ready")
            hotT_made = sem("hotT_made")
            hotT_ready = sem("hotT_ready")
            qe_made = sem("qe_made")
            qk_done = sem("qk_done")
            scored = sem("scored")
            with nc.Block() as block:
                @block.gpsimd
                def _(pool):
                    nc.gpsimd.iota(lane_row_i[:, :], [[1, P]], base=0, channel_multiplier=0).then_inc(lane_made, 1)
                    gather_rows(pool, k_table, k_in, qk_done, k_copied, k_turns, 0)

                @block.vector
                def _(dve):
                    dve.sem_inc(qk_done, U)
                    dve.wait_ge(lane_made, 1)
                    nc.vector.tensor_copy(lane_row[:, :], lane_row_i[:, :]).then_inc(lane_made, 1)
                    dve.wait_ge(lane_made, 2)

                    def hot(t, slot):
                        nc.vector.tensor_scalar(onehot[:, slot, :], lane_row[:, :], rel_f[:, bass.ds(t, 1)], None,
                                                ALU.is_equal).then_inc(hot_ready, 1)

                    hot(0, 0)
                    hot(1, 1)
                    with dve.Fori(0, TR) as i:
                        for j in range(U):
                            t = i * U + j
                            hot(t + 2, (j + 2) % 4)
                            dve.wait_ge(k_in[j], i * 16 + 16)
                            dve.wait_ge(qe_made, t + 1)
                            nc.vector.tensor_tensor(prod[:, j % 2, :], qe_ps[j % 2][:, 0:D], row_ring[:, j, :],
                                                    ALU.mult).then_inc(qk_done, 1)
                            dve.wait_ge(qk_done, t + 1 + U)
                            nc.vector.tensor_reduce(scores[:, bass.ds(t, 1), :].rearrange("p a h -> p (a h)"),
                                                    prod[:, j % 2, :].rearrange("p (d h) -> p h d", h=HEADS),
                                                    AX.X, ALU.add).then_inc(scored, 1)

                @block.tensor
                def _(pe):
                    def turn(t, j):
                        pe.wait_ge(hot_ready, t + 1)
                        nc.tensor.transpose(oT_ps[j % 2][:, 0:P], onehot[:, j % 4, :], ident[:, :]).then_inc(hotT_made, 1)

                    turn(0, 0)
                    with pe.Fori(0, TR) as i:
                        for j in range(U):
                            t = i * U + j
                            turn(t + 1, j + 1)
                            b = pe.value_load(blk_i[0:1, bass.ds(t, 1)], min_val=0, max_val=NB - 1)
                            pe.wait_ge(hotT_ready, t + 1)
                            pe.wait_ge(qk_done, t + U - 1)
                            nc.tensor.matmul(qe_ps[j % 2][:, 0:D], onehotT[:, j % 2, :], block_of(q_table, b),
                                             start=True, stop=True).then_inc(qe_made, 1)

                @block.scalar
                def _(act):
                    def keep(t, j):
                        act.wait_ge(hotT_made, t + 1)
                        nc.scalar.activation(onehotT[:, j % 2, :], oT_ps[j % 2][:, 0:P], ACT.Copy).then_inc(hotT_ready, 1)

                    with act.Fori(0, TR) as i:
                        for j in range(U):
                            keep(i * U + j, j)
                    keep(NT, 0)

        W = TR * P
        PER = 4
        with ExitStack() as st:
            perm = sb("perm", [P, TR, U, HEADS], F32, st)
            sT = sb("sT", [P, W], F32, st)
            off = sb("off", [P, W + 1], F32, st)
            fwd = sb("fwd", [P, W], F32, st)
            bwd = sb("bwd", [P, W], F32, st)
            pen = sb("pen", [P, NT], F32, st)
            ends = sb("ends", [P, 4], F32, st)
            rows = sb("rows", [1, 4, HEADS, U], F32, st)
            f_row, l_row, lf_row, lb_row = (rows[:, k] for k in range(4))
            whole = sb("whole", [1, HEADS, U], F32, st)
            cont = sb("cont", [1, 2, HEADS, U], F32, st)
            step_off = sb("step_off", [1, HEADS, U], F32, st)
            run = sb("run", [1, 2, HEADS, U], F32, st)
            carry = sb("carry", [1, 2, U, HEADS], F32, st)
            carry_col = sb("carry_col", [P, 2], F32, st)
            turn_ps = [psum(f"turn_ps{i}", [P, PER * P], st) for i in range(4)]
            small_ps = psum("small_ps", [1, 4, P], st)
            carry_ps = psum("carry_ps", [P, 2], st)
            GROUPS = [list(range(g, min(g + PER, TR))) for g in range(0, TR, PER)]
            NG = len(GROUPS)
            sm = sem("sm")
            perm_ready = sem("perm_ready")
            turned = sem("turned")
            evacuated = sem("evacuated")
            ends_ready = sem("ends_ready")
            rows_made = sem("rows_made")
            carry_ready = sem("carry_ready")
            carry_made = sem("carry_made")
            diff_ready = sem("diff_ready")
            exp_ready = sem("exp_ready")
            with nc.Block() as block:
                @block.vector
                def _(dve):
                    n = [0]

                    def then(ins):
                        n[0] += 1
                        ins.then_inc(sm, 1)
                        dve.wait_ge(sm, n[0])

                    by_row = scores[:, :, :].rearrange("p (r q) h -> p q r h", q=TR)
                    then(nc.vector.tensor_scalar(pen[:, :], real_f[:, 0:NT], BIG, -BIG, ALU.mult, ALU.add))
                    pens = pen[:, :].rearrange("p (r q) -> p q r", q=TR).unsqueeze(3).to_broadcast([P, TR, U, HEADS])
                    for q in range(TR):
                        ins = nc.vector.tensor_tensor(perm[:, q], by_row[:, q], pens[:, q], ALU.add)
                    ins.then_inc(perm_ready, 1)
                    dve.wait_ge(turned, NG)
                    srcs_by_row = src_f[:, 0:NT].rearrange("p (r q) -> p q r", q=TR).unsqueeze(3)\
                        .to_broadcast([P, TR, U, HEADS])
                    for q in range(TR):
                        ins = nc.vector.tensor_copy(perm[:, q], srcs_by_row[:, q])
                    ins.then_inc(perm_ready, 1)
                    dve.wait_ge(evacuated, 2 * NG)
                    then(nc.vector.tensor_copy(ends[:, 0:1], fwd[:, 0:1]))
                    then(nc.vector.tensor_copy(ends[:, 1:2], fwd[:, W - 1:W]))
                    then(nc.vector.tensor_tensor(off[:, 1:W], fwd[:, 1:W], fwd[:, 0:W - 1], ALU.not_equal))
                    then(nc.vector.memset(off[:, 0:1], 0.0))
                    then(nc.vector.memset(off[:, W:W + 1], 0.0))
                    then(nc.vector.tensor_scalar(off[:, 1:W], off[:, 1:W], -BIG, None, ALU.mult))

                    def scans(first_f, first_b):
                        then(nc.vector.tensor_tensor_scan(fwd[:, :], off[:, 0:W], sT[:, :], first_f, ALU.add, ALU.max))
                        then(nc.vector.tensor_tensor_scan(bwd[:, ::-1], off[:, W:0:-1], sT[:, ::-1], first_b,
                                                          ALU.add, ALU.max))

                    scans(-BIG, -BIG)
                    then(nc.vector.tensor_copy(ends[:, 2:3], fwd[:, W - 1:W]))
                    nc.vector.tensor_copy(ends[:, 3:4], bwd[:, 0:1]).then_inc(ends_ready, 1)
                    dve.wait_ge(rows_made, 1)
                    then(nc.vector.tensor_copy(rows[:, :, :, :],
                                               small_ps[:, :, :].rearrange("a k (r h) -> a k h r", h=HEADS)))
                    then(nc.vector.tensor_tensor(whole[:, :, :], f_row, l_row, ALU.is_equal))
                    then(nc.vector.memset(cont[:, :, :, :], 0.0))
                    then(nc.vector.tensor_tensor(cont[:, 0, :, 1:U], f_row[:, :, 1:U], l_row[:, :, 0:U - 1],
                                                 ALU.is_equal))
                    then(nc.vector.tensor_tensor(cont[:, 1, :, 0:U - 1], l_row[:, :, 0:U - 1], f_row[:, :, 1:U],
                                                 ALU.is_equal))

                    def flat(ap):
                        return ap.rearrange("a h r -> a (h r)")

                    for k, last in ((0, lf_row), (1, lb_row)):
                        back = slice(None) if k == 0 else slice(None, None, -1)
                        then(nc.vector.tensor_tensor(step_off[:, :, :], cont[:, k], whole[:, :, :], ALU.mult))
                        then(nc.vector.tensor_scalar(step_off[:, :, :], step_off[:, :, :], BIG, -BIG, ALU.mult, ALU.add))
                        then(nc.vector.tensor_tensor_scan(flat(run[:, k])[:, back], flat(step_off[:, :, :])[:, back],
                                                          flat(last)[:, back], -BIG, ALU.add, ALU.max))
                        then(nc.vector.tensor_scalar(cont[:, k], cont[:, k], BIG, -BIG, ALU.mult, ALU.add))
                    then(nc.vector.memset(carry[:, :, :, :], -BIG))
                    fc = carry[:, 0].rearrange("a r h -> a h r")
                    bc = carry[:, 1].rearrange("a r h -> a h r")
                    then(nc.vector.tensor_tensor(fc[:, :, 1:U], run[:, 0, :, 0:U - 1], cont[:, 0, :, 1:U], ALU.add))
                    nc.vector.tensor_tensor(bc[:, :, 0:U - 1], run[:, 1, :, 1:U], cont[:, 1, :, 0:U - 1],
                                            ALU.add).then_inc(carry_ready, 1)
                    dve.wait_ge(carry_made, 1)
                    then(nc.vector.tensor_copy(carry_col[:, :], carry_ps[:, :]))
                    scans(carry_col[:, 0:1], carry_col[:, 1:2])
                    for g, qs in enumerate(GROUPS):
                        cols = slice(qs[0] * P, (qs[-1] + 1) * P)
                        then(nc.vector.tensor_tensor(fwd[:, cols], fwd[:, cols], bwd[:, cols], ALU.max))
                        nc.vector.tensor_tensor(sT[:, cols], sT[:, cols], fwd[:, cols], ALU.subtract).then_inc(diff_ready, 1)
                    then(nc.vector.memset(weights[:, NT:NT + 2, :], 0.0))
                    w_rows = weights[:, 0:NT, :].rearrange("p (r q) h -> p q r h", q=TR)
                    real_rows = real_f[:, 0:NT].rearrange("p (r q) -> p q r", q=TR).unsqueeze(3)\
                        .to_broadcast([P, TR, U, HEADS])
                    for g, qs in enumerate(GROUPS):
                        dve.wait_ge(turned, 2 * NG + g + 1)
                        for k, q in enumerate(qs):
                            nc.vector.tensor_tensor(
                                w_rows[:, q], turn_ps[g % 4][:, k * P:(k + 1) * P].rearrange("p (r h) -> p r h", h=HEADS),
                                real_rows[:, q], ALU.mult).then_inc(evacuated, 1)

                @block.tensor
                def _(pe):
                    for what in range(2):
                        pe.wait_ge(perm_ready, what + 1)
                        for g, qs in enumerate(GROUPS):
                            bank = what * NG + g
                            if bank >= 4:
                                pe.wait_ge(evacuated, bank - 3)
                            for k, q in enumerate(qs):
                                ins = nc.tensor.transpose(turn_ps[bank % 4][:, k * P:(k + 1) * P],
                                                          perm[:, q].rearrange("p r h -> p (r h)"), ident[:, :])
                            ins.then_inc(turned, 1)
                    pe.wait_ge(ends_ready, 1)
                    for k in range(4):
                        ins = nc.tensor.transpose(small_ps[:, k, :], ends[:, k:k + 1], ident[:, :])
                    ins.then_inc(rows_made, 1)
                    pe.wait_ge(carry_ready, 1)
                    for k in range(2):
                        ins = nc.tensor.transpose(carry_ps[:, k:k + 1], carry[:, k].rearrange("a r h -> a (r h)"),
                                                  ident[0:1, 0:1])
                    ins.then_inc(carry_made, 1)
                    for g, qs in enumerate(GROUPS):
                        pe.wait_ge(exp_ready, g + 1)
                        if g >= 4:
                            pe.wait_ge(evacuated, 2 * NG + (g - 3) * PER)
                        for k, q in enumerate(qs):
                            ins = nc.tensor.transpose(turn_ps[g % 4][:, k * P:(k + 1) * P], sT[:, q * P:(q + 1) * P],
                                                      ident[:, :])
                        ins.then_inc(turned, 1)

                @block.scalar
                def _(act):
                    for what, target in enumerate((sT, fwd)):
                        for g, qs in enumerate(GROUPS):
                            act.wait_ge(turned, what * NG + g + 1)
                            nc.scalar.activation(target[:, qs[0] * P:(qs[-1] + 1) * P],
                                                 turn_ps[(what * NG + g) % 4][:, 0:len(qs) * P],
                                                 ACT.Copy).then_inc(evacuated, 1)
                    for g, qs in enumerate(GROUPS):
                        act.wait_ge(diff_ready, g + 1)
                        cols = slice(qs[0] * P, (qs[-1] + 1) * P)
                        nc.scalar.activation(sT[:, cols], sT[:, cols], ACT.Exp).then_inc(exp_ready, 1)

        DZ = D + HEADS
        acc = sb("acc", [P, NB + 1, DZ], F32, gnn)
        with ExitStack() as st:
            pv = sb("pv", [P, 4, D], F32, st)
            agg_ps = [psum(f"agg_ps{i}", [P, 512], st) for i in range(4)]
            v_in = [sem(f"v_in{i}") for i in range(U)]
            v_copied = sem("v_copied")
            v_turns = sem("v_turns")
            acc_clear = sem("acc_clear")
            pv_ready = sem("pv_ready")
            agg_made = sem("agg_made")
            acc_done = sem("acc_done")
            with nc.Block() as block:
                @block.gpsimd
                def _(pool):
                    gather_rows(pool, v_table, v_in, pv_ready, v_copied, v_turns, 2)

                @block.vector
                def _(dve):
                    dve.sem_inc(pv_ready, U)
                    dve.sem_inc(acc_done, 1)
                    nc.vector.memset(acc[:, :, :], 0.0).then_inc(acc_clear, 1)

                    def weigh(t, slot, in_round):
                        nc.vector.tensor_scalar(onehot[:, slot % 4, :], lane_row[:, :], rel_f[:, bass.ds(t, 1)], None,
                                                ALU.is_equal)
                        dve.wait_ge(v_in[slot], in_round)
                        w = weights[:, bass.ds(t, 1), :].to_broadcast([P, HD, HEADS])
                        nc.vector.tensor_tensor(pv[:, slot % 4, :].rearrange("p (d h) -> p d h", h=HEADS),
                                                row_ring[:, slot, :].rearrange("p (d h) -> p d h", h=HEADS), w,
                                                ALU.mult).then_inc(pv_ready, 1)

                    weigh(0, 0, 16)
                    weigh(1, 1, 16)
                    dve.wait_ge(acc_clear, 1)
                    with dve.Fori(0, TR) as i:
                        for j in range(U):
                            t = i * U + j
                            weigh(t + 2, (j + 2) % U, i * 16 + 16 + 16 * ((j + 2) // U))
                            b = dve.value_load(blk_i[0:1, bass.ds(t, 1)], min_val=0, max_val=NB - 1)
                            dve.wait_ge(agg_made, t + 1)
                            dve.wait_ge(acc_done, t + 1)
                            nc.vector.tensor_tensor(block_of(acc, b), block_of(acc, b), agg_ps[j % 4][:, 0:DZ],
                                                    ALU.add).then_inc(acc_done, 1)

                @block.tensor
                def _(pe):
                    def aggregate(t, j):
                        pe.wait_ge(pv_ready, t + 1 + U)
                        nc.tensor.matmul(agg_ps[j % 4][:, 0:D], onehot[:, j % 4, :], pv[:, j % 4, :],
                                         start=True, stop=True)
                        nc.tensor.matmul(agg_ps[j % 4][:, D:DZ], onehot[:, j % 4, :], block_of(weights, t),
                                         start=True, stop=True).then_inc(agg_made, 1)

                    with pe.Fori(0, TR) as i:
                        for j in range(U):
                            aggregate(i * U + j, j)
                    aggregate(NT, 0)
                    aggregate(NT + 1, 1)


        x1_dram = dram("x1_dram", [NB * P, D])
        xs_dram = dram("xs_dram", [NS, D])
        ys_dram = dram("ys_dram", [TE * P, D])
        logits = sb("logits", [P, NB, NX], F32, gnn)
        xn = sb("xn", [P, NB, D], F32, gnn)
        with ExitStack() as st:
            att = sb("att", [P, 2, D], F32, st)
            attT = sb("attT", [P, 2, KC, P], F32, st)
            zinv = sb("zinv", [P, NB + 1, HEADS], F32, st)
            wo_sb = sb("wo_sb", [P, KC, D], F32, st)
            bo_sb = sb("bo_sb", [1, D], F32, st)
            wr_sb = sb("wr_sb", [P, KC, NX], F32, st)
            br_sb = sb("br_sb", [1, NX], F32, st)
            uin = sb("uin", [P, 2, D], F32, st)
            uT = sb("uT", [P, 2, KC, P], F32, st)
            zeros = sb("zeros", [P, D], F32, st)
            aT_ps = [psum(f"aT_ps{i}", [P, KC, P], st) for i in range(2)]
            o_ps = [psum(f"o_ps{i}", [P, D], st) for i in range(2)]
            uT_ps = [psum(f"uT_ps{i}", [P, KC, P], st) for i in range(2)]
            lg_ps = psum("lg_ps", [P, 2, NX], st)
            wo_in = sem("wo_in")
            zeroed = sem("zeroed")
            xs_zero = sem("xs_zero")
            nd = sem("nd")
            att_ready = sem("att_ready")
            att_turned = sem("att_turned")
            attT_ready = sem("attT_ready")
            o_made = sem("o_made")
            x1_ready = sem("x1_ready")
            x1_stored = sem("x1_stored")
            stats1 = sem("stats1")
            var1 = sem("var1")
            rstd1 = sem("rstd1")
            u_ready = sem("u_ready")
            uin_ready = sem("uin_ready")
            uin_free = sem("uin_free")
            u_turned = sem("u_turned")
            uT_ready = sem("uT_ready")
            lg_made = sem("lg_made")
            lg_kept = sem("lg_kept")
            xn_ready = sem("xn_ready")
            with nc.Block() as block:
                @block.sync
                def _(sp):
                    sp.dma_start(wo_sb[:, :, :], Wo.rearrange("(c p) n -> p c n", p=P)).then_inc(wo_in, 16)
                    sp.dma_start(bo_sb[:, :], bo.rearrange("(a n) -> a n", a=1)).then_inc(wo_in, 16)
                    sp.dma_start(wr_sb[:, :, :], Wr.rearrange("(c p) n -> p c n", p=P)).then_inc(wo_in, 16)
                    sp.dma_start(br_sb[:, :], br.rearrange("(a n) -> a n", a=1)).then_inc(wo_in, 16)
                    sp.wait_ge(zeroed, 1)
                    sp.dma_start(xs_dram.rearrange("(t p) d -> p t d", p=P),
                                 zeros[:, :].unsqueeze(1).to_broadcast([P, NS // P, D])).then_inc(xs_zero, 16)
                    sp.wait_ge(x1_ready, NB)
                    sp.dma_start(x1_dram.rearrange("(b p) d -> p b d", p=P), xres[:, :, :]).then_inc(x1_stored, 16)
                    sp.wait_ge(x1_stored, 16)
                    sp.wait_ge(xs_zero, 16)

                @block.gpsimd
                def _(pool):
                    nc.gpsimd.memset(zeros[:, :], 0.0).then_inc(zeroed, 1)
                    pool.wait_ge(var1, 1)
                    nc.gpsimd.tensor_tensor(rstd[:, :], var[:, :], minus_half[:, :], ALU.pow).then_inc(rstd1, 1)
                    with pool.Fori(0, NB // 2) as i:
                        for j in range(2):
                            b = i * 2 + j
                            pool.wait_ge(u_ready, b + 1)
                            pool.wait_ge(uin_free, b + 1)
                            nc.gpsimd.tensor_copy(uin[:, j, :], block_of(xn, b)).then_inc(uin_ready, 1)
                    pool.wait_ge(var1, 2)
                    pool.wait_ge(uin_ready, NB)
                    nc.gpsimd.tensor_tensor(rstd[:, :], var[:, :], minus_half[:, :], ALU.pow).then_inc(rstd1, 1)

                @block.vector
                def _(dve):
                    n = [0]

                    def link(ins):
                        n[0] += 1
                        ins.then_inc(nd, 1)
                        dve.wait_ge(nd, n[0])

                    link(nc.vector.tensor_scalar(zinv[:, :, :], acc[:, :, D:DZ], 0.5, None, ALU.max))
                    link(nc.vector.reciprocal(zinv[:, :, :], zinv[:, :, :]))

                    def normalise(b, j):
                        z = zinv[:, bass.ds(b, 1), :].to_broadcast([P, HD, HEADS])
                        sums = acc[:, bass.ds(b, 1), 0:D].rearrange("p a (d h) -> p (a d) h", h=HEADS)
                        nc.vector.tensor_tensor(att[:, j, :].rearrange("p (d h) -> p d h", h=HEADS), sums, z,
                                                ALU.mult).then_inc(att_ready, 1)

                    normalise(0, 0)
                    with dve.Fori(0, NB // 2) as i:
                        for j in range(2):
                            b = i * 2 + j
                            normalise(b + 1, 1 - j)
                            dve.wait_ge(o_made, b + 1)
                            nc.vector.tensor_tensor(block_of(xres, b), block_of(xres, b), o_ps[j][:, :],
                                                    ALU.add).then_inc(x1_ready, 1)
                            dve.wait_ge(x1_ready, b + 1)
                            nc.vector.bn_stats(stats[:, bass.ds(b, 1), :].rearrange("p a s -> p (a s)"),
                                               block_of(xres, b)).then_inc(stats1, 1)
                    dve.wait_ge(stats1, NB)
                    mean_and_variance(link)
                    nc.vector.tensor_copy(var[:, :], var[:, :]).then_inc(var1, 1)
                    dve.wait_ge(rstd1, 1)
                    with dve.Fori(0, NB // 2) as i:
                        for j in range(2):
                            b = i * 2 + j
                            nc.vector.tensor_scalar(block_of(xn, b), block_of(xres, b), mean[:, bass.ds(b, 1)],
                                                    rstd[:, bass.ds(b, 1)], ALU.subtract, ALU.mult).then_inc(u_ready, 1)
                            dve.wait_ge(u_ready, b + 1)
                            nc.vector.bn_stats(stats[:, bass.ds(b, 1), :].rearrange("p a s -> p (a s)"),
                                               block_of(xn, b)).then_inc(stats1, 1)
                    dve.wait_ge(stats1, 2 * NB)
                    mean_and_variance(link)
                    nc.vector.tensor_copy(var[:, :], var[:, :]).then_inc(var1, 1)
                    dve.wait_ge(rstd1, 2)
                    with dve.Fori(0, NB // 2) as i:
                        for j in range(2):
                            b = i * 2 + j
                            nc.vector.tensor_scalar(block_of(xn, b), block_of(xn, b), mean[:, bass.ds(b, 1)],
                                                    rstd[:, bass.ds(b, 1)], ALU.subtract, ALU.mult).then_inc(xn_ready, 1)

                @block.tensor
                def _(pe):
                    pe.sem_inc(uin_free, 2)
                    pe.wait_ge(wo_in, 64)
                    with pe.Fori(0, NB // 2) as i:
                        for j in range(2):
                            b = i * 2 + j
                            pe.wait_ge(att_ready, b + 1)
                            for c in range(KC):
                                ins = nc.tensor.transpose(aT_ps[j][:, c, :], att[:, j, c * P:(c + 1) * P], ident[:, :])
                            ins.then_inc(att_turned, 1)
                            pe.wait_ge(attT_ready, b + 1)
                            for c in range(KC):
                                nc.tensor.matmul(o_ps[j][:, :], attT[:, j, c, :], wo_sb[:, c, :], start=(c == 0),
                                                 stop=False)
                            nc.tensor.matmul(o_ps[j][:, :], ones_row, bo_sb[:, :], start=False,
                                             stop=True).then_inc(o_made, 1)
                    with pe.Fori(0, NB // 2) as i:
                        for j in range(2):
                            b = i * 2 + j
                            pe.wait_ge(uin_ready, b + 1)
                            for c in range(KC):
                                ins = nc.tensor.transpose(uT_ps[j][:, c, :], uin[:, j, c * P:(c + 1) * P], ident[:, :])
                            ins.then_inc(u_turned, 1)
                            pe.wait_ge(uT_ready, b + 1)
                            for c in range(KC):
                                ins = nc.tensor.matmul(lg_ps[:, j, :], uT[:, j, c, :], wr_sb[:, c, :], start=(c == 0),
                                                       stop=False)
                            ins.then_inc(uin_free, 1)
                            nc.tensor.matmul(lg_ps[:, j, :], ones_row, br_sb[:, :], start=False,
                                             stop=True).then_inc(lg_made, 1)

                @block.scalar
                def _(act):
                    with act.Fori(0, NB // 2) as i:
                        for j in range(2):
                            act.wait_ge(att_turned, i * 2 + j + 1)
                            nc.scalar.activation(attT[:, j, :, :], aT_ps[j][:, :, :], ACT.Copy).then_inc(attT_ready, 1)
                    with act.Fori(0, NB // 2) as i:
                        for j in range(2):
                            b = i * 2 + j
                            act.wait_ge(u_turned, b + 1)
                            nc.scalar.activation(uT[:, j, :, :], uT_ps[j][:, :, :], ACT.Copy).then_inc(uT_ready, 1)
                            act.wait_ge(lg_made, b + 1)
                            nc.scalar.activation(block_of(logits, b), lg_ps[:, j, :], ACT.Copy).then_inc(lg_kept, 1)

        with ExitStack() as st:
            top = sb("top", [P, NB, 8], F32, st)
            top_i = sb("top_i", [P, NB, 8], U32, st)
            ids = sb("ids", [P, 2, NB], F32, st)
            ex_no = sb("ex_no", [P, NX], F32, st)
            ex_no_i = sb("ex_no_i", [P, NX], I32, st)
            token_i = sb("token_i", [P, NB], I32, st)
            token_ok = sb("token_ok", [P, NB], F32, st)
            tile_no_i = sb("tile_no_i", [P, NS // P], I32, st)
            tile_no = sb("tile_no", [P, NS // P], F32, st)
            pick = sb("pick", [P, 2, NB, NX], F32, st)
            both = sb("both", [P, NB, NX], F32, st)
            before = sb("before", [P, P], F32, st)
            inc = sb("inc", [P, NX, NB], F32, st)
            keep = sb("keep", [P, NX, NB], F32, st)
            total = sb("total", [P, NX, NB], F32, st)
            tiles_i = sb("tiles_i", [P, NX], I32, st)
            tiles = sb("tiles", [P, NX], F32, st)
            tile_end = sb("tile_end", [P, NX], F32, st)
            base = sb("base", [P, NX], F32, st)
            one_x = sb("one_x", [P, NX], F32, st)
            place = sb("place", [P, NB, NX], F32, st)
            picked = sb("picked", [P, 2, NB, NX], F32, st)
            rowf = sb("rowf", [P, 2, NB], F32, st)
            ended = sb("ended", [P, NS // P, NX], F32, st)
            tile_f = sb("tile_f", [P, NS // P], F32, st)
            low = sb("low", [P, 2, NB], F32, st)
            pre_ps = psum("pre_ps", [P, NB, NX], st)
            tot_ps = psum("tot_ps", [P, NB, NX], st)
            rt = sem("rt")
            r_const = sem("r_const")
            gap_ready = sem("gap_ready")
            gap_exp = sem("gap_exp")
            both_ready = sem("both_ready")
            pre_made = sem("pre_made")
            rows_ready = sem("rows_ready")
            scattered = sem("scattered")
            with nc.Block() as block:
                @block.gpsimd
                def _(pool):
                    nc.gpsimd.iota(ex_no_i[:, :], [[1, NX]], base=0, channel_multiplier=0).then_inc(r_const, 1)
                    nc.gpsimd.iota(token_i[:, :], [[P, NB]], base=0, channel_multiplier=1).then_inc(r_const, 1)
                    nc.gpsimd.iota(tile_no_i[:, :], [[1, NS // P]], base=0, channel_multiplier=0).then_inc(r_const, 1)
                    nc.gpsimd.affine_select(out=before[:, :], in_=ones[:, :], compare_op=ALU.is_gt, fill=0.0,
                                            base=0, pattern=[[1, P]], channel_multiplier=-1).then_inc(r_const, 1)
                    pool.wait_ge(rows_ready, 1)
                    for b in range(NBR):
                        live = P if b < NBF else TAIL
                        for k in range(2):
                            nc.gpsimd.indirect_dma_start(
                                xs_dram, bass.IndirectOffsetOnAxis(row_i[0:live, k, b:b + 1].bitcast(U32), 0),
                                xn[0:live, b, :], None).then_inc(scattered, 16)
                    pool.wait_ge(scattered, 32 * NBR)

                @block.vector
                def _(dve):
                    n = [0]

                    def link(ins):
                        n[0] += 1
                        ins.then_inc(rt, 1)
                        dve.wait_ge(rt, n[0])

                    dve.wait_ge(r_const, 3)
                    nc.vector.tensor_copy(ex_no[:, :], ex_no_i[:, :])
                    nc.vector.tensor_copy(tile_no[:, :], tile_no_i[:, :])
                    link(nc.vector.tensor_copy(token_ok[:, :], token_i[:, :]))
                    link(nc.vector.tensor_scalar(token_ok[:, :], token_ok[:, :], float(N), None, ALU.is_lt))
                    for b in range(NB):
                        ins = nc.vector.max(top[:, b, :], logits[:, b, :])
                    link(ins)
                    for b in range(NB):
                        ins = nc.vector.max_index(top_i[:, b, :], top[:, b, :], logits[:, b, :])
                    link(ins)
                    nc.vector.tensor_tensor(low[:, 0, :], top[:, :, 1], top[:, :, 0], ALU.subtract).then_inc(gap_ready, 1)
                    for k in range(2):
                        link(nc.vector.tensor_copy(ids[:, k, :], top_i[:, :, k]))
                    for k in range(2):
                        for b in range(NB):
                            ins = nc.vector.tensor_scalar(pick[:, k, b, :], ex_no[:, :], ids[:, k, b:b + 1],
                                                          token_ok[:, b:b + 1], ALU.is_equal, ALU.mult)
                    link(ins)
                    nc.vector.tensor_tensor(both[:, :, :], pick[:, 0], pick[:, 1], ALU.add).then_inc(both_ready, 1)
                    dve.wait_ge(gap_exp, 1)
                    link(nc.vector.tensor_scalar(wts[:, 0, :], low[:, 1, :], 1.0, None, ALU.add))
                    link(nc.vector.reciprocal(wts[:, 0, :], wts[:, 0, :]))
                    link(nc.vector.tensor_tensor(wts[:, 1, :], wts[:, 0, :], low[:, 1, :], ALU.mult))
                    link(nc.vector.memset(keep[:, :, :], 1.0))
                    link(nc.vector.memset(keep[:, :, 0:1], 0.0))
                    link(nc.vector.memset(one_x[:, :], 1.0))
                    dve.wait_ge(pre_made, 1)
                    link(nc.vector.tensor_copy(total[:, :, :], tot_ps[:, :, :].rearrange("p b e -> p e b")))
                    link(nc.vector.tensor_tensor_scan(inc[:, :, :].rearrange("p e b -> p (e b)"),
                                                      keep[:, :, :].rearrange("p e b -> p (e b)"),
                                                      total[:, :, :].rearrange("p e b -> p (e b)"), 0.0,
                                                      ALU.mult, ALU.add))
                    link(nc.vector.tensor_scalar(tiles[:, :], inc[:, :, NB - 1], float(P - 1), None, ALU.add))
                    link(nc.vector.tensor_copy(tiles_i[:, :], tiles[:, :]))
                    link(nc.vector.tensor_scalar(tiles_i[:, :], tiles_i[:, :], LOGP, None, ALU.logical_shift_right))
                    link(nc.vector.tensor_copy(tiles[:, :], tiles_i[:, :]))
                    link(nc.vector.tensor_tensor_scan(tile_end[:, :], one_x[:, :], tiles[:, :], 0.0, ALU.mult, ALU.add))
                    link(nc.vector.tensor_tensor(base[:, :], tile_end[:, :], tiles[:, :], ALU.subtract))
                    link(nc.vector.tensor_scalar(base[:, :], base[:, :], float(P), None, ALU.mult))
                    link(nc.vector.tensor_tensor(inc[:, :, :], inc[:, :, :], total[:, :, :], ALU.subtract))
                    link(nc.vector.tensor_tensor(inc[:, :, :], inc[:, :, :],
                                                 base[:, :].unsqueeze(2).to_broadcast([P, NX, NB]), ALU.add))
                    link(nc.vector.tensor_tensor(place[:, :, :], inc[:, :, :].rearrange("p e b -> p b e"),
                                                 pre_ps[:, :, :], ALU.add))
                    for k in range(2):
                        link(nc.vector.tensor_tensor(picked[:, k], pick[:, k], place[:, :, :], ALU.mult))
                        link(nc.vector.tensor_reduce(rowf[:, k], picked[:, k], AX.X, ALU.add))
                    nc.vector.tensor_copy(row_i[:, :, :], rowf[:, :, :]).then_inc(rows_ready, 1)
                    for e in range(NX):
                        ins = nc.vector.tensor_scalar(ended[:, :, e], tile_no[:, :], tile_end[:, e:e + 1], None,
                                                      ALU.is_ge)
                    link(ins)
                    link(nc.vector.tensor_reduce(tile_f[:, :], ended[:, :, :], AX.X, ALU.add))
                    link(nc.vector.tensor_scalar(tile_f[:, :], tile_f[:, :], float(NX - 1), None, ALU.min))
                    link(nc.vector.tensor_copy(tile_ex[:, :], tile_f[:, :]))

                @block.scalar
                def _(act):
                    act.wait_ge(gap_ready, 1)
                    nc.scalar.activation(low[:, 1, :], low[:, 0, :], ACT.Exp).then_inc(gap_exp, 1)

                @block.tensor
                def _(pe):
                    pe.wait_ge(both_ready, 1)
                    pe.wait_ge(r_const, 4)
                    nc.tensor.matmul(pre_ps[:, :, :].rearrange("p b e -> p (b e)"), before[:, :],
                                     both[:, :, :].rearrange("p b e -> p (b e)"), start=True, stop=True)
                    nc.tensor.matmul(tot_ps[:, :, :].rearrange("p b e -> p (b e)"), ones[:, :],
                                     both[:, :, :].rearrange("p b e -> p (b e)"), start=True,
                                     stop=True).then_inc(pre_made, 1)

        gnn.close()
        with ExitStack() as st:
            w1_sb = sb("w1_sb", [P, NX, KC, H], F32, st)
            w2_sb = sb("w2_sb", [P, NX, HC, D], F32, st)
            b1_sb = sb("b1_sb", [P, NX, H], F32, st)
            b2_sb = sb("b2_sb", [P, NX, D], F32, st)
            g_sb = sb("g_sb", [P, NX * KC], F32, st)
            be_sb = sb("be_sb", [P, NX * KC], F32, st)
            xs = sb("xs", [P, UE, D], F32, st)
            xeT = sb("xeT", [P, KC, P], F32, st)
            h_sb = sb("h_sb", [P, H], F32, st)
            hT = sb("hT", [P, HC, P], F32, st)
            ys = sb("ys", [P, UE, D], F32, st)
            xsT_ps = psum("xsT_ps", [P, KC, P], st)
            h_ps = psum("h_ps", [P, H], st)
            hT_ps = psum("hT_ps", [P, HC, P], st)
            y_ps = psum("y_ps", [P, D], st)
            HB = 512
            we_in = sem("we_in")
            xs_in = [sem(f"xs_in{j}") for j in range(UE)]
            ys_out = [sem(f"ys_out{j}") for j in range(UE)]
            xs_turned = sem("xs_turned")
            xeT_ready = sem("xeT_ready")
            h_made = sem("h_made")
            h_biased = sem("h_biased")
            h_ready = sem("h_ready")
            h_turned = sem("h_turned")
            hT_ready = sem("hT_ready")
            y_made = sem("y_made")
            ys_ready = sem("ys_ready")
            with nc.Block() as block:
                @block.sync
                def _(sp):
                    for j in range(UE):
                        sp.sem_inc(ys_out[j], 16)
                        sp.dma_start(xs[:, j, :], xs_dram[j * P:(j + 1) * P, :]).then_inc(xs_in[j], 16)
                    with sp.Fori(0, TE // UE) as i:
                        for j in range(UE):
                            t = i * UE + j
                            sp.wait_ge(xs_turned, t + 1)
                            sp.dma_start(xs[:, j, :], xs_dram[bass.ds((t + UE) * P, P), :]).then_inc(xs_in[j], 16)
                            sp.wait_ge(ys_ready, t + 1)
                            sp.dma_start(ys_dram[bass.ds(t * P, P), :], ys[:, j, :]).then_inc(ys_out[j], 16)
                    for j in range(UE):
                        sp.wait_ge(xs_in[j], 16 * (TE // UE + 1))
                        sp.wait_ge(ys_out[j], 16 * (TE // UE + 1))

                @block.scalar
                def _(act):
                    act.dma_start(g_sb[:, :], ln_g.rearrange("e (c p) -> p (e c)", p=P),
                                  allow_slow_non_contiguous=True).then_inc(we_in, 16)
                    act.dma_start(be_sb[:, :], ln_b.rearrange("e (c p) -> p (e c)", p=P),
                                  allow_slow_non_contiguous=True).then_inc(we_in, 16)
                    for e in range(NX):
                        act.dma_start(w1_sb[:, e], W1[e].rearrange("(c p) h -> p c h", p=P)).then_inc(we_in, 16)
                        act.dma_start(w2_sb[:, e], W2[e].rearrange("(c p) d -> p c d", p=P)).then_inc(we_in, 16)
                    act.dma_start(b1_sb[:, :, :], b1.unsqueeze(0).to_broadcast([P, NX, H])).then_inc(we_in, 16)
                    act.dma_start(b2_sb[:, :, :], b2.unsqueeze(0).to_broadcast([P, NX, D])).then_inc(we_in, 16)

                    with act.Fori(0, TE // UE) as i:
                        for j in range(UE):
                            t = i * UE + j
                            act.wait_ge(h_biased, t + 1)
                            nc.scalar.activation(h_sb[:, :], h_sb[:, :], ACT.Gelu).then_inc(h_ready, 1)
                            for half in range(2):
                                ks = slice(half * HC // 2, (half + 1) * HC // 2)
                                act.wait_ge(h_turned, t * 2 + half + 1)
                                nc.scalar.activation(hT[:, ks, :], hT_ps[:, ks, :], ACT.Copy).then_inc(hT_ready, 1)

                @block.vector
                def _(dve):
                    def scale_and_bias(t, e):
                        for c in range(KC):
                            at = bass.ds(e * KC + c, 1)
                            ins = nc.vector.tensor_scalar(xeT[:, c, :], xsT_ps[:, c, :], g_sb[:, at], be_sb[:, at],
                                                          ALU.mult, ALU.add)
                        ins.then_inc(xeT_ready, 1)

                    def add_b1(t, e):
                        dve.wait_ge(h_made, t + 1)
                        for half in range(H // HB):
                            cols = slice(half * HB, (half + 1) * HB)
                            ins = nc.vector.tensor_tensor(
                                h_sb[:, cols], h_ps[:, cols],
                                b1_sb[:, bass.ds(e, 1), cols].rearrange("p a h -> p (a h)"), ALU.add)
                        ins.then_inc(h_biased, 1)

                    def up(t):
                        e = dve.value_load(tile_ex[0:1, bass.ds(t, 1)], min_val=0, max_val=NX - 1)
                        dve.wait_ge(xs_turned, t + 1)
                        scale_and_bias(t, e)
                        add_b1(t, e)

                    dve.wait_ge(we_in, 16 * (2 * NX + 4))
                    up(0)
                    with dve.Fori(0, TE // UE) as i:
                        for j in range(UE):
                            t = i * UE + j
                            up(t + 1)
                            e = dve.value_load(tile_ex[0:1, bass.ds(t, 1)], min_val=0, max_val=NX - 1)
                            dve.wait_ge(y_made, t + 1)
                            dve.wait_ge(ys_out[j], i * 16 + 16)
                            nc.vector.tensor_tensor(ys[:, j, :], y_ps[:, :], block_of(b2_sb, e),
                                                    ALU.add).then_inc(ys_ready, 1)

                @block.tensor
                def _(pe):
                    def turn_rows(t, slot, in_round):
                        pe.wait_ge(xs_in[slot], in_round)
                        for c in range(KC):
                            ins = nc.tensor.transpose(xsT_ps[:, c, :], xs[:, slot, c * P:(c + 1) * P], ident[:, :])
                        ins.then_inc(xs_turned, 1)

                    def first_layer(t):
                        e = pe.value_load(tile_ex[0:1, bass.ds(t, 1)], min_val=0, max_val=NX - 1)
                        pe.wait_ge(xeT_ready, t + 1)
                        for half in range(H // HB):
                            cols = slice(half * HB, (half + 1) * HB)
                            for c in range(KC):
                                ins = nc.tensor.matmul(
                                    h_ps[:, cols], xeT[:, c, :],
                                    w1_sb[:, bass.ds(e, 1), c, cols].rearrange("p a h -> p (a h)"),
                                    start=(c == 0), stop=(c == KC - 1))
                        ins.then_inc(h_made, 1)

                    def turn_hidden(t):
                        pe.wait_ge(h_ready, t + 1)
                        for k in range(HC):
                            ins = nc.tensor.transpose(hT_ps[:, k, :], h_sb[:, k * P:(k + 1) * P], ident[:, :])
                            if k % (HC // 2) == HC // 2 - 1:
                                ins.then_inc(h_turned, 1)

                    def second_layer(t):
                        e = pe.value_load(tile_ex[0:1, bass.ds(t, 1)], min_val=0, max_val=NX - 1)
                        for k in range(HC):
                            if k % (HC // 2) == 0:
                                pe.wait_ge(hT_ready, t * 2 + k // (HC // 2) + 1)
                            ins = nc.tensor.matmul(y_ps[:, :], hT[:, k, :],
                                                   w2_sb[:, bass.ds(e, 1), k, :].rearrange("p a d -> p (a d)"),
                                                   start=(k == 0), stop=(k == HC - 1))
                        ins.then_inc(y_made, 1)

                    pe.wait_ge(we_in, 16 * (2 * NX + 4))
                    turn_rows(0, 0, 16)
                    first_layer(0)
                    with pe.Fori(0, TE // UE) as i:
                        for j in range(UE):
                            t = i * UE + j
                            turn_rows(t + 1, (j + 1) % UE, i * 16 + 16 + 16 * ((j + 1) // UE))
                            turn_hidden(t)
                            first_layer(t + 1)
                            second_layer(t)

        with ExitStack() as st:
            R = 8
            x1 = sb("x1", [P, NBR, D], F32, st)
            yk = sb("yk", [P, NBR, 2, D], F32, st)
            x1_in = sem("x1_in")
            y_in = [sem(f"y_in{r}") for r in range(R)]
            half_sum = sem("half_sum")
            out_ready = sem("out_ready")
            out_stored = sem("out_stored")
            with nc.Block() as block:
                @block.sync
                def _(sp):
                    sp.dma_start(x1[:, :, :], x1_dram[0:NBR * P, :].rearrange("(b p) d -> p b d", p=P)).then_inc(x1_in, 16)
                    for b in range(NBR):
                        live = P if b < NBF else TAIL
                        sp.wait_ge(out_ready, b + 1)
                        sp.dma_start(out[b * P:b * P + live, :], x1[0:live, b, :]).then_inc(out_stored, 16)
                    sp.wait_ge(out_stored, 16 * NBR)

                @block.gpsimd
                def _(pool):
                    for b in range(NBR):
                        live = P if b < NBF else TAIL
                        if b >= R:
                            pool.wait_ge(out_ready, b - R + 1)
                        for k in range(2):
                            nc.gpsimd.indirect_dma_start(
                                yk[0:live, b, k, :], None, ys_dram,
                                bass.IndirectOffsetOnAxis(row_i[0:live, k, b:b + 1].bitcast(U32), 0)
                            ).then_inc(y_in[b % R], 16)

                @block.vector
                def _(dve):
                    dve.wait_ge(x1_in, 16)
                    for b in range(NBR):
                        live = P if b < NBF else TAIL
                        dve.wait_ge(y_in[b % R], 32 * (b // R + 1))
                        for k, signal in enumerate((half_sum, out_ready)):
                            nc.vector.scalar_tensor_tensor(out=x1[0:live, b, :], in0=yk[0:live, b, k, :],
                                                           scalar=wts[0:live, k, b:b + 1], in1=x1[0:live, b, :],
                                                           op0=ALU.mult, op1=ALU.add).then_inc(signal, 1)
                            dve.wait_ge(signal, b + 1)


_GNN = ["Wq", "bq", "Wk", "bk", "Wv", "bv", "Wo", "bo"]
_FFN = ["Wr", "br", "ln_g", "ln_b", "W1", "b1", "W2", "b2"]
_INS = ["x", "src", "dst"] + ["L0_gnn_" + n for n in _GNN] + ["L0_ffn_" + n for n in _FFN]


def kernel(**inputs):
    import numpy as _np
    import concourse.bacc as _bacc
    from concourse import mybir as _mybir
    from concourse.bass_utils import run_bass_kernel_spmd as _run

    nc = _bacc.Bacc("TRN2", target_bir_lowering=False, num_devices=1)
    arrays, args = {}, []
    for name in _INS:
        a = _np.ascontiguousarray(inputs[name])
        arrays[f"in_{name}_dram"] = a
        args.append(nc.dram_tensor(f"in_{name}_dram", a.shape, _mybir.dt.from_np(a.dtype), kind="ExternalInput").ap())
    out = nc.dram_tensor("out_dram", inputs["x"].shape, _mybir.dt.float32, kind="ExternalOutput").ap()
    gnn_moe_kernel(nc, *args, out)
    r = _run(nc, [arrays], core_ids=[0])
    return r.results[0]["out_dram"]
```

```python
from contextlib import ExitStack

import numpy as np

import concourse.bass as bass
from concourse import mybir

F32 = mybir.dt.float32
BF16 = mybir.dt.bfloat16
I32 = mybir.dt.int32
U32 = mybir.dt.uint32
ALU = mybir.AluOpType
ACT = mybir.ActivationFunctionType
AX = mybir.AxisListType

P = 128
BIG = 1.0e30
EPS = 1e-5


def gnn_moe_kernel(nc, x, src, dst, Wq, bq, Wk, bk, Wv, bv, Wo, bo, Wr, br, ln_g, ln_b, W1, b1, W2, b2, out):
    N, D = x.shape
    E = src.shape[0]
    NX, H = W1.shape[0], W1.shape[2]
    HEADS, HD = 8, D // 8
    KC = D // P
    HC = H // P
    SCALE = float(HD) ** -0.5

    NBF = N // P
    TAIL = N - NBF * P
    NBR = NBF + 1
    NB = NBR + 1
    NT = 416
    assert NT % 16 == 0 and NT * P >= E + NBR * (P - 1) and NB % 2 == 0
    SORT = 1 << 16
    SC = SORT // P
    LOGN, LOGP = 16, 7
    SHIFT = 12
    RADIX = 1 << SHIFT
    PAD_DST = RADIX - 1
    FILL = ((NB - 1) * P + P - 1) * RADIX + PAD_DST
    assert N < PAD_DST and FILL < 1 << 24 and SORT >= NT * P
    ER = 125
    EC = E // ER
    assert ER * EC == E and EC + NBR <= SC

    TE = (2 * N + NX * (P - 1)) // P
    UE = 4
    NS = (TE + UE) * P
    assert TE % UE == 0

    ctx = ExitStack()
    with ctx:
        def sem(name):
            return ctx.enter_context(nc.semaphore(name))

        def dram(name, shape):
            return nc.dram_tensor(name, shape, F32, kind="Internal").ap()

        k_table = dram("k_table", [NB * P, D])
        v_table = dram("v_table", [NB * P, D])

        def sb(name, shape, dt=F32, c=ctx):
            return c.enter_context(nc.sbuf_tensor(name, shape, dt))

        def psum(name, shape, c, dt=F32):
            return c.enter_context(nc.psum_tensor(name, shape, dt))

        ident = sb("ident", [P, P])
        ones = sb("ones", [P, P])
        ones_row = ones[0:1, :]
        wts = sb("wts", [P, 2, NB])
        row_i = sb("row_i", [P, 2, NB], I32)
        tile_ex = sb("tile_ex", [P, NS // P], I32)
        lane = sb("lane", [P, 1], I32)
        lane_f = sb("lane_f", [P, 1])
        stats = sb("stats", [P, NB, 6])
        mean = sb("mean", [P, NB])
        var = sb("var", [P, NB])
        half_diff = sb("half_diff", [P, NB])
        rstd = sb("rstd", [P, NB])
        minus_half = sb("minus_half", [P, NB])

        def block_of(table, b):
            return table[:, bass.ds(b, 1), :].rearrange("p a d -> p (a d)")

        def mean_and_variance(link):
            link(nc.vector.tensor_tensor(mean[:, :], stats[:, :, 1], stats[:, :, 4], ALU.add))
            link(nc.vector.tensor_tensor(half_diff[:, :], stats[:, :, 1], stats[:, :, 4], ALU.subtract))
            link(nc.vector.tensor_tensor(var[:, :], stats[:, :, 2], stats[:, :, 5], ALU.add))
            link(nc.vector.tensor_scalar(mean[:, :], mean[:, :], 0.5, None, ALU.mult))
            link(nc.vector.tensor_scalar(half_diff[:, :], half_diff[:, :], 0.5, None, ALU.mult))
            link(nc.vector.tensor_scalar(var[:, :], var[:, :], 1.0 / D, EPS, ALU.mult, ALU.add))
            link(nc.vector.tensor_tensor(half_diff[:, :], half_diff[:, :], half_diff[:, :], ALU.mult))
            link(nc.vector.tensor_tensor(var[:, :], var[:, :], half_diff[:, :], ALU.add))

        ffn = ExitStack()
        ffn.__enter__()
        w1_sb = sb("w1_sb", [P, NX, KC, H], F32, ffn)
        w2_sb = sb("w2_sb", [P, NX, HC, D], F32, ffn)
        b1_sb = sb("b1_sb", [P, NX, H], F32, ffn)

        class Loan:

            def __init__(self, region):
                self.region, self.at = region, 0

            def take(self, shape, dt=F32):
                words = int(np.prod(shape)) * mybir.dt.size(dt) // 4
                cols = self.region[:, self.at:self.at + words]
                self.at += words
                assert self.at <= self.region.shape[1]
                if dt is not F32:
                    cols = cols.bitcast(dt)
                names = "abc"[:len(shape)]
                return cols.rearrange(f"p ({' '.join(names)}) -> p {' '.join(names)}", **dict(zip(names, shape)))

        w1_words = w1_sb[:, :, :, :].rearrange("p e c h -> p (e c h)")
        w2_words = w2_sb[:, :, :, :].rearrange("p e c d -> p (e c d)")
        b1_words = b1_sb[:, :, :].rearrange("p e h -> p (e h)")

        gnn = ExitStack()
        gnn.__enter__()
        xres = sb("xres", [P, NB, D], F32, gnn)
        U = 16
        loan = Loan(w2_words)
        q_parts = loan.take((3, NB, D), BF16)
        scores = loan.take((NT, HEADS))
        key_i = loan.take((SC,), I32)
        dst_i = loan.take((SC,), I32)
        src_f = loan.take((SC,))
        rel_f = loan.take((SC,))
        real_f = loan.take((SC,))
        blk_i = loan.take((SC,), I32)
        with ExitStack() as st:
            srcs = sb("srcs", [ER, EC], I32, st)
            dsts = sb("dsts", [ER, EC], I32, st)
            blkf = sb("blkf", [ER, EC], F32, st)
            tmp_i = sb("tmp_i", [P, SC], I32, st)
            tmp_f = sb("tmp_f", [P, SC], F32, st)
            blkno_i = sb("blkno_i", [P, NBR], I32, st)
            blkno = sb("blkno", [P, NBR], F32, st)
            loan = Loan(w1_words)
            xhat = loan.take((NB, D))
            inblk = loan.take((NBR, EC), BF16)[0:ER]
            loan = Loan(b1_words)
            cnt = sb("cnt", [ER, NBR], F32, st)
            need_i = sb("need_i", [P, NBR], I32, st)
            need = sb("need", [P, NBR], F32, st)
            padkey = sb("padkey", [P, NBR], F32, st)
            dir_i = sb("dir_i", [P, LOGP], I32, st)
            dirs = sb("dirs", [P, LOGP], F32, st)
            keys = [loan.take((SC,)) for i in range(2)]
            half = loan.take((SC // 2,))
            xin = loan.take((2, D))
            xT = loan.take((2, KC, P))
            wq_sb = loan.take((KC, D))
            wkv_sb = loan.take((KC, 2 * D))
            bq_sb = sb("bq_sb", [1, D], F32, st)
            bkv_sb = sb("bkv_sb", [1, 2 * D], F32, st)
            kv_out = loan.take((2, 2 * D))
            q_full = loan.take((2, D))
            q_rest = loan.take((2, D))
            xT_ps = psum("xT_ps", [P, 2, KC, P], st)
            q_ps = psum("q_ps", [P, 2, D], st)
            kv_ps = [psum(f"kv_ps{i}", [P, 2 * D], st) for i in range(2)]
            cnt_ps = psum("cnt_ps", [P, NBR], st)
            swap_ps = [psum(f"swap_ps{i}", [P, SC], st) for i in range(2)]

            edges_in = sem("edges_in")
            x_in = sem("x_in")
            w_in = sem("w_in")
            consts = sem("consts")
            cdone = sem("cdone")
            cleared = sem("cleared")
            counted = sem("counted")
            cnt_sum = sem("cnt_sum")
            stats_made = sem("stats_made")
            var_ready = sem("var_ready")
            rstd_ready = sem("rstd_ready")
            xhat_ready = sem("xhat_ready")
            xin_ready = sem("xin_ready")
            xin_free = sem("xin_free")
            xT_made = sem("xT_made")
            xT_ready = sem("xT_ready")
            q_made = sem("q_made")
            kv_made = sem("kv_made")
            q_kept = sem("q_kept")
            q_turns = sem("q_turns")
            q_cut = sem("q_cut")
            kv_ready = sem("kv_ready")
            k_stored = [sem(f"k_stored{i}") for i in range(2)]
            sort_step = sem("sort_step")
            to_swap = sem("to_swap")
            swapped = sem("swapped")
            decoded = sem("decoded")

            with nc.Block() as block:
                @block.sync
                def _(sp):
                    for j in range(2):
                        sp.sem_inc(k_stored[j], 32)
                    sp.dma_start(srcs[:, :], src.rearrange("(p t) -> p t", p=ER)).then_inc(edges_in, 16)
                    sp.dma_start(dsts[:, :], dst.rearrange("(p t) -> p t", p=ER)).then_inc(edges_in, 16)
                    sp.wait_ge(cleared, 1)
                    sp.dma_start(xres[:, 0:NBF, :],
                                 x[0:NBF * P, :].rearrange("(b p) d -> p b d", p=P)).then_inc(x_in, 16)
                    sp.dma_start(xres[0:TAIL, NBF, :], x[NBF * P:N, :]).then_inc(x_in, 16)
                    sp.dma_start(wq_sb[:, :, :], Wq.rearrange("(c p) n -> p c n", p=P)).then_inc(w_in, 16)
                    sp.dma_start(wkv_sb[:, :, 0:D], Wk.rearrange("(c p) n -> p c n", p=P)).then_inc(w_in, 16)
                    sp.dma_start(wkv_sb[:, :, D:2 * D], Wv.rearrange("(c p) n -> p c n", p=P)).then_inc(w_in, 16)
                    sp.dma_start(bq_sb[:, :], bq.rearrange("(a n) -> a n", a=1)).then_inc(w_in, 16)
                    sp.dma_start(bkv_sb[:, 0:D], bk.rearrange("(a n) -> a n", a=1)).then_inc(w_in, 16)
                    sp.dma_start(bkv_sb[:, D:2 * D], bv.rearrange("(a n) -> a n", a=1)).then_inc(w_in, 16)
                    with sp.Fori(0, NB // 2) as i:
                        for j in range(2):
                            rows = bass.ds((i * 2 + j) * P, P)
                            sp.wait_ge(kv_ready, i * 2 + j + 1)
                            sp.dma_start(k_table[rows, :], kv_out[:, j, 0:D]).then_inc(k_stored[j], 16)
                            sp.dma_start(v_table[rows, :], kv_out[:, j, D:2 * D]).then_inc(k_stored[j], 16)
                    for j in range(2):
                        sp.wait_ge(k_stored[j], 16 * NB + 32)

                @block.gpsimd
                def _(pool):
                    nc.gpsimd.memset(ident[:, :], 0.0).then_inc(consts, 1)
                    nc.gpsimd.memset(ones[:, :], 1.0).then_inc(consts, 1)
                    pool.wait_ge(consts, 2)
                    nc.gpsimd.affine_select(out=ident[:, :], in_=ident[:, :], compare_op=ALU.not_equal, fill=1.0,
                                            base=0, pattern=[[-1, P]], channel_multiplier=1).then_inc(consts, 1)
                    nc.gpsimd.iota(lane[:, :], [[0, 1]], base=0, channel_multiplier=1).then_inc(consts, 1)
                    nc.gpsimd.iota(blkno_i[:, :], [[1, NBR]], base=0, channel_multiplier=0).then_inc(consts, 1)
                    nc.gpsimd.memset(minus_half[:, :], -0.5).then_inc(consts, 1)
                    pool.wait_ge(consts, 6)
                    pool.wait_ge(var_ready, 1)
                    nc.gpsimd.tensor_tensor(rstd[:, :], var[:, :], minus_half[:, :], ALU.pow).then_inc(rstd_ready, 1)

                    def hand_over(b, j):
                        pool.wait_ge(xhat_ready, b + 1)
                        pool.wait_ge(xin_free, b + 1)
                        nc.gpsimd.tensor_copy(xin[:, j, :], block_of(xhat, b)).then_inc(xin_ready, 1)

                    def split_q(b, j):
                        first, second, third = (block_of(q_parts[:, k], b) for k in range(3))
                        pool.wait_ge(q_kept, b + 1)
                        nc.gpsimd.tensor_copy(first, q_full[:, j, :]).then_inc(q_cut, 1)
                        pool.wait_ge(q_cut, b * 4 + 8 + 1)
                        pool.sem_inc(q_turns, 1)
                        nc.gpsimd.tensor_tensor(q_rest[:, j, :], q_full[:, j, :], first, ALU.subtract).then_inc(q_cut, 1)
                        pool.wait_ge(q_cut, b * 4 + 8 + 2)
                        nc.gpsimd.tensor_copy(second, q_rest[:, j, :]).then_inc(q_cut, 1)
                        pool.wait_ge(q_cut, b * 4 + 8 + 3)
                        pool.sem_inc(q_turns, 1)
                        nc.gpsimd.tensor_tensor(third, q_rest[:, j, :], second, ALU.subtract).then_inc(q_cut, 1)

                    pool.sem_inc(q_cut, 8)
                    hand_over(0, 0)
                    hand_over(1, 1)
                    with pool.Fori(1, NB // 2) as i:
                        for j in range(2):
                            hand_over(i * 2 + j, j)
                            split_q(i * 2 + j - 2, j)
                    split_q(NB - 2, 0)
                    split_q(NB - 1, 1)

                @block.vector
                def _(dve):
                    steps = [0]

                    def link(ins):
                        steps[0] += 1
                        ins.then_inc(cdone, 1)
                        dve.wait_ge(cdone, steps[0])

                    nc.vector.memset(xres[:, NBF:NB, :], 0.0).then_inc(cleared, 1)
                    dve.wait_ge(x_in, 32)
                    with dve.Fori(0, NB // 2) as i:
                        for j in range(2):
                            b = i * 2 + j
                            nc.vector.bn_stats(stats[:, bass.ds(b, 1), :].rearrange("p a s -> p (a s)"),
                                               block_of(xres, b)).then_inc(stats_made, 1)
                    dve.wait_ge(stats_made, NB)
                    mean_and_variance(link)
                    nc.vector.tensor_copy(var[:, :], var[:, :]).then_inc(var_ready, 1)
                    dve.wait_ge(rstd_ready, 1)
                    with dve.Fori(0, NB // 2) as i:
                        for j in range(2):
                            b = i * 2 + j
                            nc.vector.tensor_scalar(block_of(xhat, b), block_of(xres, b), mean[:, bass.ds(b, 1)],
                                                    rstd[:, bass.ds(b, 1)], ALU.subtract,
                                                    ALU.mult).then_inc(xhat_ready, 1)

                    dve.wait_ge(edges_in, 32)
                    dve.wait_ge(consts, 5)
                    link(nc.vector.tensor_copy(lane_f[:, :], lane[:, :]))
                    link(nc.vector.tensor_copy(blkno[:, :], blkno_i[:, :]))
                    link(nc.vector.tensor_scalar(tmp_i[0:ER, 0:EC], srcs[:, :], LOGP, None, ALU.logical_shift_right))
                    link(nc.vector.tensor_copy(blkf[:, :], tmp_i[0:ER, 0:EC]))
                    for b in range(NBR):
                        nc.vector.tensor_scalar(inblk[:, b, :], blkf[:, :], float(b), None, ALU.is_equal)
                    link(nc.vector.tensor_scalar(padkey[:, :], blkno[:, :], float(P * RADIX),
                                                 float((P - 1) * RADIX + PAD_DST - FILL), ALU.mult, ALU.add))
                    nc.vector.tensor_reduce(cnt[:, :], inblk[:, :, :], AX.X, ALU.add).then_inc(counted, 1)
                    for j in range(LOGP):
                        nc.vector.tensor_scalar(dir_i[:, j:j + 1], lane[:, :], j, 1, ALU.logical_shift_right,
                                                ALU.bitwise_and)
                    link(nc.vector.memset(keys[1][:, :], float(FILL)))
                    link(nc.vector.tensor_copy(dirs[:, :], dir_i[:, :]))
                    link(nc.vector.tensor_scalar(dirs[:, :], dirs[:, :], -2.0, 1.0, ALU.mult, ALU.add))
                    link(nc.vector.scalar_tensor_tensor(out=keys[1][0:ER, 0:EC], in0=srcs[:, :], scalar=float(RADIX),
                                                        in1=dsts[:, :], op0=ALU.mult, op1=ALU.add))
                    dve.wait_ge(cnt_sum, 1)
                    link(nc.vector.tensor_scalar(need[:, :], cnt_ps[:, :], -1.0, float(SORT), ALU.mult, ALU.add))
                    link(nc.vector.tensor_copy(need_i[:, :], need[:, :]))
                    link(nc.vector.tensor_scalar(need_i[:, :], need_i[:, :], P - 1, None, ALU.bitwise_and))
                    link(nc.vector.tensor_copy(need[:, :], need_i[:, :]))
                    link(nc.vector.scalar_tensor_tensor(out=need[:, :], in0=need[:, :], scalar=lane_f[:, 0:1],
                                                        in1=padkey[:, :], op0=ALU.is_gt, op1=ALU.mult))
                    link(nc.vector.tensor_scalar(keys[1][:, EC:EC + NBR], need[:, :], float(FILL), None, ALU.add))

                    n, swaps = 0, 0
                    source = keys[1]

                    def column_bit(bit, low):
                        if low:
                            return bit if bit < LOGP else (bit - LOGP if bit >= 2 * LOGP else None)
                        return bit - LOGP

                    def settle(ins):
                        nonlocal n
                        n += 1
                        ins.then_inc(sort_step, 1)
                        dve.wait_ge(sort_step, n)

                    def exchanges(bits, low, after_swap, swap_next, to_come=0):
                        nonlocal n, source
                        for left, bit in zip(range(len(bits) - 1, -1, -1), bits):
                            w = 1 << column_bit(bit, low)
                            target = keys[1 - (left + to_come) % 2]
                            s = source[:, :].rearrange("p (h t w) -> p h t w", t=2, w=w)
                            d = target[:, :].rearrange("p (h t w) -> p h t w", t=2, w=w)
                            first, second = s[:, :, 0, :], s[:, :, 1, :]
                            if left == len(bits) - 1 and after_swap:
                                second = half[:, :].rearrange("p (h w) -> p h w", w=w)
                                settle(nc.vector.tensor_copy(second, s[:, :, 1, :]))
                            lesser = nc.vector.tensor_tensor(d[:, :, 0, :], first, second, ALU.min)
                            if left == 0 and swap_next:
                                settle(lesser)
                            greater = nc.vector.tensor_tensor(d[:, :, 1, :], first, second, ALU.max)
                            if left == 0 and swap_next:
                                greater.then_inc(to_swap, 1)
                            else:
                                settle(greater)
                            source = target

                    def negate(bit, swap_next=False):
                        col = column_bit(bit, True)
                        s = source[:, :]
                        by = dirs[:, bit - LOGP:bit - LOGP + 1] if col is None else -1.0
                        if col is not None:
                            s = s.rearrange("p (h t w) -> p h t w", t=2, w=1 << col)[:, :, 1, :]
                        ins = nc.vector.tensor_scalar(s, s, by, None, ALU.mult)
                        if swap_next:
                            ins.then_inc(to_swap, 1)
                        else:
                            settle(ins)

                    def swap_layout():
                        nonlocal swaps, source
                        swaps += 1
                        dve.wait_ge(swapped, swaps)
                        source = swap_ps[(swaps - 1) % 2]

                    low_bits = list(range(LOGP - 1, -1, -1))
                    for k in range(1, LOGP + 1):
                        if k > 1:
                            negate(k - 1)
                        negate(k)
                        exchanges(list(range(k - 1, -1, -1)), True, False, False,
                                  to_come=sum(range(k + 1, LOGP + 1)))
                    for k in range(LOGP + 1, LOGN + 1):
                        negate(k - 1, swap_next=(k == LOGN))
                        if k < LOGN:
                            negate(k, swap_next=True)
                        swap_layout()
                        exchanges(list(range(k - 1, LOGP - 1, -1)), False, True, True)
                        swap_layout()
                        exchanges(low_bits, True, True, k == LOGN)
                    swap_layout()

                    n = 0

                    def then(ins):
                        nonlocal n
                        n += 1
                        ins.then_inc(decoded, 1)
                        dve.wait_ge(decoded, n)

                    then(nc.vector.tensor_copy(key_i[:, :], source[:, :]))
                    then(nc.vector.tensor_scalar(tmp_i[:, :], key_i[:, :], SHIFT, None, ALU.logical_shift_right))
                    then(nc.vector.tensor_copy(src_f[:, :], tmp_i[:, :]))
                    then(nc.vector.tensor_scalar(blk_i[:, :], tmp_i[:, :], LOGP, None, ALU.logical_shift_right))
                    then(nc.vector.tensor_scalar(tmp_i[:, :], tmp_i[:, :], P - 1, None, ALU.bitwise_and))
                    then(nc.vector.tensor_copy(rel_f[:, :], tmp_i[:, :]))
                    then(nc.vector.tensor_scalar(tmp_i[:, :], key_i[:, :], RADIX - 1, None, ALU.bitwise_and))
                    then(nc.vector.tensor_copy(tmp_f[:, :], tmp_i[:, :]))
                    then(nc.vector.tensor_scalar(real_f[:, :], tmp_f[:, :], float(PAD_DST), None, ALU.is_lt))
                    then(nc.vector.tensor_scalar(dst_i[:, :], tmp_f[:, :], float(N - 1), None, ALU.min))

                @block.tensor
                def _(pe):
                    pe.wait_ge(consts, 3)
                    pe.sem_inc(xin_free, 2)

                    def project(b, j):
                        pe.wait_ge(xin_ready, b + 1)
                        for c in range(KC):
                            ins = nc.tensor.transpose(xT_ps[:, j, c, :], xin[:, j, c * P:(c + 1) * P], ident[:, :])
                        ins.then_inc(xT_made, 1)
                        pe.wait_ge(xT_ready, b + 1)
                        pe.wait_ge(w_in, 96)
                        for c in range(KC):
                            nc.tensor.matmul(q_ps[:, j, :], xT[:, j, c, :], wq_sb[:, c, :], start=(c == 0), stop=False)
                        nc.tensor.matmul(q_ps[:, j, :], ones_row, bq_sb[:, :], start=False, stop=True).then_inc(q_made, 1)
                        for c in range(KC):
                            ins = nc.tensor.matmul(kv_ps[j][:, :], xT[:, j, c, :], wkv_sb[:, c, :], start=(c == 0), stop=False)
                        ins.then_inc(xin_free, 1)
                        nc.tensor.matmul(kv_ps[j][:, :], ones_row, bkv_sb[:, :], start=False, stop=True).then_inc(kv_made, 1)

                    def swap(i, j):
                        pe.wait_ge(to_swap, i + 1)
                        for g in range(SC // P):
                            ins = nc.tensor.transpose(swap_ps[j][:, g * P:(g + 1) * P], keys[1][:, g * P:(g + 1) * P], ident[:, :])
                        ins.then_inc(swapped, 1)

                    HEAD = NB - 2 * (LOGN - LOGP)
                    with pe.Fori(0, HEAD // 2) as i:
                        project(i * 2, 0)
                        project(i * 2 + 1, 1)
                    pe.wait_ge(counted, 1)
                    nc.tensor.matmul(cnt_ps[:, :], ones[0:ER, :], cnt[:, :], start=True, stop=True).then_inc(cnt_sum, 1)
                    with pe.Fori(0, LOGN - LOGP) as i:
                        swap(i * 2, 0)
                        project(i * 2 + HEAD, 0)
                        swap(i * 2 + 1, 1)
                        project(i * 2 + HEAD + 1, 1)
                    swap(2 * (LOGN - LOGP), 0)

                @block.scalar
                def _(act):
                    with act.Fori(0, NB // 2) as i:
                        for j in range(2):
                            b = i * 2 + j
                            act.wait_ge(xT_made, b + 1)
                            nc.scalar.activation(xT[:, j, :, :], xT_ps[:, j, :, :], ACT.Copy).then_inc(xT_ready, 1)
                            act.wait_ge(q_made, b + 1)
                            act.wait_ge(q_cut, b * 4 + 2)
                            nc.scalar.activation(q_full[:, j, :], q_ps[:, j, :], ACT.Copy,
                                                 scale=SCALE).then_inc(q_kept, 1)
                            act.wait_ge(kv_made, b + 1)
                            act.wait_ge(k_stored[j], i * 32 + 32)
                            nc.scalar.activation(kv_out[:, j, :], kv_ps[j][:, :], ACT.Copy).then_inc(kv_ready, 1)

        TR = NT // U
        lane_row = sb("lane_row", [P, P], F32, gnn)
        lane_row_i = sb("lane_row_i", [P, P], I32, gnn)
        idx_ring = sb("idx_ring", [P, 2, U // 2], I32, gnn)
        att_st = ExitStack()
        att_st.__enter__()
        weights = sb("weights", [P, NT + 4, HEADS], F32, att_st)
        H8 = U // 2

        def load_blocks(eng, name, i):
            regs = [eng.alloc_register(f"{name}{k}") for k in range(U)]
            eng.reg_load(regs, blk_i[0:1, bass.ds(i * U, U)])
            return [eng.snap(reg, donate=True, min_val=0, max_val=NB - 1) for reg in regs]

        def gather_rows(pool, table, row_ring, fetched, used, copied, turns, extra):
            def copy_indices(first, s):
                nc.gpsimd.tensor_copy(idx_ring[:, s, :], dst_i[:, bass.ds(first, H8)]).then_inc(copied, 1)

            def gather(slot, free):
                pool.wait_ge(used, free)
                pool.sem_inc(turns, 1)
                nc.gpsimd.indirect_dma_start(
                    row_ring[:, slot, :], None, table,
                    bass.IndirectOffsetOnAxis(idx_ring[:, slot // H8, slot % H8:slot % H8 + 1].bitcast(U32), 0)).then_inc(fetched[slot // 2], 16)

            nc.gpsimd.tensor_copy(idx_ring[:, 0, :], dst_i[:, 0:H8]).then_inc(copied, 1)
            with pool.Fori(0, TR) as i:
                for half in range(2):
                    pool.wait_ge(copied, i * 2 + half + 1)
                    for j in range(H8):
                        gather(half * H8 + j, i * H8 + (half * H8 + j) // 2 + 1)
                        if j == H8 - 2:
                            pool.wait_ge(used, i * H8 + half * H8 // 2 + H8)
                            copy_indices(i * U + (half + 1) * H8, 1 - half)
            pool.wait_ge(copied, TR * 2 + 1)
            for slot in range(extra):
                gather(slot, NT // 2 + slot // 2 + 1)
            for pair in range(H8):
                pool.wait_ge(fetched[pair], 32 * (TR + (pair < extra // 2)))

        with ExitStack() as st:
            loan = Loan(w1_words)
            k_ring = loan.take((U, D))
            onehot = loan.take((8, P), BF16)
            onehotT = loan.take((2, 2, P), BF16)
            ident_h = loan.take((P,), BF16)
            prod = loan.take((2, 2, D))
            oT_ps = [psum(f"oT_ps{i}", [P, 2, P], st, BF16) for i in range(2)]
            qe_ps = [psum(f"qe_ps{i}", [P, 2, D], st) for i in range(4)]
            k_in = [sem(f"k_in{i}") for i in range(H8)]
            k_copied = sem("k_copied")
            k_turns = sem("k_turns")
            lane_made = sem("lane_made")
            hot_ready = sem("hot_ready")
            hotT_made = sem("hotT_made")
            hotT_ready = sem("hotT_ready")
            qe_made = sem("qe_made")
            qk_done = sem("qk_done")
            scored = sem("scored")
            with nc.Block() as block:
                @block.gpsimd
                def _(pool):
                    nc.gpsimd.iota(lane_row_i[:, :], [[1, P]], base=0, channel_multiplier=0).then_inc(lane_made, 1)
                    gather_rows(pool, k_table, k_ring, k_in, qk_done, k_copied, k_turns, 0)

                @block.vector
                def _(dve):
                    dve.sem_inc(qk_done, H8)
                    nc.vector.tensor_copy(ident_h[:, :], ident[:, :]).then_inc(lane_made, 1)
                    dve.wait_ge(lane_made, 2)
                    nc.vector.tensor_copy(lane_row[:, :], lane_row_i[:, :]).then_inc(lane_made, 1)
                    dve.wait_ge(lane_made, 3)

                    def hots(p, slot):
                        nc.vector.tensor_tensor(onehot[:, slot * 2:slot * 2 + 2, :],
                                                lane_row[:, :].unsqueeze(1).to_broadcast([P, 2, P]),
                                                rel_f[:, bass.ds(p * 2, 2)].unsqueeze(2).to_broadcast([P, 2, P]),
                                                ALU.is_equal).then_inc(hot_ready, 1)

                    for p in range(3):
                        hots(p, p)
                    with dve.Fori(0, TR) as i:
                        for j in range(H8):
                            p = i * H8 + j
                            dve.wait_ge(k_in[j], i * 32 + 32)
                            dve.wait_ge(qe_made, p + 1)
                            nc.vector.tensor_tensor(prod[:, j % 2], qe_ps[j % 4][:, :, :],
                                                    k_ring[:, j * 2:j * 2 + 2, :], ALU.mult).then_inc(qk_done, 1)
                            hots(p + 3, (j + 3) % 4)
                            dve.wait_ge(qk_done, p + 1 + H8)
                            nc.vector.tensor_reduce(scores[:, bass.ds(p * 2, 2), :],
                                                    prod[:, j % 2].rearrange("p t (d h) -> p t h d", h=HEADS),
                                                    AX.X, ALU.add).then_inc(scored, 1)

                @block.tensor
                def _(pe):
                    def turn(p, j):
                        pe.wait_ge(hot_ready, p + 1)
                        for k in range(2):
                            ins = nc.tensor.transpose(oT_ps[j % 2][:, k, :], onehot[:, j % 4 * 2 + k, :], ident_h[:, :])
                        ins.then_inc(hotT_made, 1)

                    turn(0, 0)
                    with pe.Fori(0, TR) as i:
                        regs = load_blocks(pe, "q_block", i)
                        for j in range(H8):
                            p = i * H8 + j
                            turn(p + 1, j + 1)
                            pe.wait_ge(hotT_ready, p + 1)
                            pe.wait_ge(qk_done, p + H8 - 3)
                            for k, b in enumerate(regs[j * 2:j * 2 + 2]):
                                for part in range(3):
                                    ins = nc.tensor.matmul(qe_ps[j % 4][:, k, :], onehotT[:, j % 2, k, :],
                                                           block_of(q_parts[:, part], b), start=(part == 0),
                                                           stop=(part == 2))
                            ins.then_inc(qe_made, 1)

                @block.scalar
                def _(act):
                    def keep(p, j):
                        act.wait_ge(hotT_made, p + 1)
                        nc.scalar.activation(onehotT[:, j % 2], oT_ps[j % 2][:, :, :], ACT.Copy).then_inc(hotT_ready, 1)

                    with act.Fori(0, TR) as i:
                        for j in range(H8):
                            keep(i * H8 + j, j)
                    keep(NT // 2, 0)

        W = TR * P
        PER = 4
        with ExitStack() as st:
            loan = Loan(w1_words)
            perm = loan.take((TR, U, HEADS))
            sT = loan.take((W,))
            off = loan.take((W + 1,))
            fwd = loan.take((W,))
            bwd = scores.rearrange("p t h -> p (t h)")
            loan = Loan(b1_words)
            pen = loan.take((NT,))
            ends = loan.take((4,))
            rows = loan.take((4, HEADS, U))[0:1]
            f_row, l_row, lf_row, lb_row = (rows[:, k] for k in range(4))
            whole = loan.take((HEADS, U))[0:1]
            cont = loan.take((2, HEADS, U))[0:1]
            step_off = loan.take((HEADS, U))[0:1]
            run = loan.take((2, HEADS, U))[0:1]
            carry = loan.take((2, U, HEADS))[0:1]
            carry_col = loan.take((2,))
            turn_ps = [psum(f"turn_ps{i}", [P, PER * P], st) for i in range(4)]
            small_ps = psum("small_ps", [1, 4, P], st)
            carry_ps = psum("carry_ps", [P, 2], st)
            GROUPS = [list(range(g, min(g + PER, TR))) for g in range(0, TR, PER)]
            NG = len(GROUPS)
            sm = sem("sm")
            perm_ready = sem("perm_ready")
            turned = sem("turned")
            evacuated = sem("evacuated")
            ends_ready = sem("ends_ready")
            rows_made = sem("rows_made")
            carry_ready = sem("carry_ready")
            carry_made = sem("carry_made")
            diff_ready = sem("diff_ready")
            exp_ready = sem("exp_ready")
            with nc.Block() as block:
                @block.vector
                def _(dve):
                    n = [0]

                    def then(ins):
                        n[0] += 1
                        ins.then_inc(sm, 1)
                        dve.wait_ge(sm, n[0])

                    by_row = scores[:, :, :].rearrange("p (r q) h -> p q r h", q=TR)
                    then(nc.vector.tensor_scalar(pen[:, :], real_f[:, 0:NT], BIG, -BIG, ALU.mult, ALU.add))
                    pens = pen[:, :].rearrange("p (r q) -> p q r", q=TR).unsqueeze(3).to_broadcast([P, TR, U, HEADS])
                    for q in range(TR):
                        ins = nc.vector.tensor_tensor(perm[:, q], by_row[:, q], pens[:, q], ALU.add)
                    ins.then_inc(perm_ready, 1)
                    dve.wait_ge(turned, NG)
                    srcs_by_row = src_f[:, 0:NT].rearrange("p (r q) -> p q r", q=TR).unsqueeze(3)\
                        .to_broadcast([P, TR, U, HEADS])
                    for q in range(TR):
                        ins = nc.vector.tensor_copy(perm[:, q], srcs_by_row[:, q])
                    ins.then_inc(perm_ready, 1)
                    dve.wait_ge(evacuated, 2 * NG)
                    then(nc.vector.tensor_copy(ends[:, 0:1], fwd[:, 0:1]))
                    then(nc.vector.tensor_copy(ends[:, 1:2], fwd[:, W - 1:W]))
                    then(nc.vector.tensor_tensor(off[:, 1:W], fwd[:, 1:W], fwd[:, 0:W - 1], ALU.not_equal))
                    then(nc.vector.memset(off[:, 0:1], 0.0))
                    then(nc.vector.memset(off[:, W:W + 1], 0.0))
                    then(nc.vector.tensor_scalar(off[:, 1:W], off[:, 1:W], -BIG, None, ALU.mult))

                    def scans(first_f, first_b):
                        then(nc.vector.tensor_tensor_scan(fwd[:, :], off[:, 0:W], sT[:, :], first_f, ALU.add, ALU.max))
                        then(nc.vector.tensor_tensor_scan(bwd[:, ::-1], off[:, W:0:-1], sT[:, ::-1], first_b,
                                                          ALU.add, ALU.max))

                    scans(-BIG, -BIG)
                    then(nc.vector.tensor_copy(ends[:, 2:3], fwd[:, W - 1:W]))
                    nc.vector.tensor_copy(ends[:, 3:4], bwd[:, 0:1]).then_inc(ends_ready, 1)
                    dve.wait_ge(rows_made, 1)
                    then(nc.vector.tensor_copy(rows[:, :, :, :],
                                               small_ps[:, :, :].rearrange("a k (r h) -> a k h r", h=HEADS)))
                    then(nc.vector.tensor_tensor(whole[:, :, :], f_row, l_row, ALU.is_equal))
                    then(nc.vector.memset(cont[:, :, :, :], 0.0))
                    then(nc.vector.tensor_tensor(cont[:, 0, :, 1:U], f_row[:, :, 1:U], l_row[:, :, 0:U - 1],
                                                 ALU.is_equal))
                    then(nc.vector.tensor_tensor(cont[:, 1, :, 0:U - 1], l_row[:, :, 0:U - 1], f_row[:, :, 1:U],
                                                 ALU.is_equal))

                    def flat(ap):
                        return ap.rearrange("a h r -> a (h r)")

                    for k, last in ((0, lf_row), (1, lb_row)):
                        back = slice(None) if k == 0 else slice(None, None, -1)
                        then(nc.vector.tensor_tensor(step_off[:, :, :], cont[:, k], whole[:, :, :], ALU.mult))
                        then(nc.vector.tensor_scalar(step_off[:, :, :], step_off[:, :, :], BIG, -BIG, ALU.mult, ALU.add))
                        then(nc.vector.tensor_tensor_scan(flat(run[:, k])[:, back], flat(step_off[:, :, :])[:, back],
                                                          flat(last)[:, back], -BIG, ALU.add, ALU.max))
                        then(nc.vector.tensor_scalar(cont[:, k], cont[:, k], BIG, -BIG, ALU.mult, ALU.add))
                    then(nc.vector.memset(carry[:, :, :, :], -BIG))
                    fc = carry[:, 0].rearrange("a r h -> a h r")
                    bc = carry[:, 1].rearrange("a r h -> a h r")
                    then(nc.vector.tensor_tensor(fc[:, :, 1:U], run[:, 0, :, 0:U - 1], cont[:, 0, :, 1:U], ALU.add))
                    nc.vector.tensor_tensor(bc[:, :, 0:U - 1], run[:, 1, :, 1:U], cont[:, 1, :, 0:U - 1],
                                            ALU.add).then_inc(carry_ready, 1)
                    dve.wait_ge(carry_made, 1)
                    then(nc.vector.tensor_copy(carry_col[:, :], carry_ps[:, :]))
                    scans(carry_col[:, 0:1], carry_col[:, 1:2])
                    for g, qs in enumerate(GROUPS):
                        cols = slice(qs[0] * P, (qs[-1] + 1) * P)
                        then(nc.vector.tensor_tensor(fwd[:, cols], fwd[:, cols], bwd[:, cols], ALU.max))
                        nc.vector.tensor_tensor(sT[:, cols], sT[:, cols], fwd[:, cols], ALU.subtract).then_inc(diff_ready, 1)
                    then(nc.vector.memset(weights[:, NT:NT + 4, :], 0.0))
                    w_rows = weights[:, 0:NT, :].rearrange("p (r q) h -> p q r h", q=TR)
                    real_rows = real_f[:, 0:NT].rearrange("p (r q) -> p q r", q=TR).unsqueeze(3)\
                        .to_broadcast([P, TR, U, HEADS])
                    for g, qs in enumerate(GROUPS):
                        dve.wait_ge(turned, 2 * NG + g + 1)
                        for k, q in enumerate(qs):
                            nc.vector.tensor_tensor(
                                w_rows[:, q], turn_ps[g % 4][:, k * P:(k + 1) * P].rearrange("p (r h) -> p r h", h=HEADS),
                                real_rows[:, q], ALU.mult).then_inc(evacuated, 1)

                @block.tensor
                def _(pe):
                    for what in range(2):
                        pe.wait_ge(perm_ready, what + 1)
                        for g, qs in enumerate(GROUPS):
                            bank = what * NG + g
                            if bank >= 4:
                                pe.wait_ge(evacuated, bank - 3)
                            for k, q in enumerate(qs):
                                ins = nc.tensor.transpose(turn_ps[bank % 4][:, k * P:(k + 1) * P],
                                                          perm[:, q].rearrange("p r h -> p (r h)"), ident[:, :])
                            ins.then_inc(turned, 1)
                    pe.wait_ge(ends_ready, 1)
                    for k in range(4):
                        ins = nc.tensor.transpose(small_ps[:, k, :], ends[:, k:k + 1], ident[:, :])
                    ins.then_inc(rows_made, 1)
                    pe.wait_ge(carry_ready, 1)
                    for k in range(2):
                        ins = nc.tensor.transpose(carry_ps[:, k:k + 1], carry[:, k].rearrange("a r h -> a (r h)"),
                                                  ident[0:1, 0:1])
                    ins.then_inc(carry_made, 1)
                    for g, qs in enumerate(GROUPS):
                        pe.wait_ge(exp_ready, g + 1)
                        if g >= 4:
                            pe.wait_ge(evacuated, 2 * NG + (g - 3) * PER)
                        for k, q in enumerate(qs):
                            ins = nc.tensor.transpose(turn_ps[g % 4][:, k * P:(k + 1) * P], sT[:, q * P:(q + 1) * P],
                                                      ident[:, :])
                        ins.then_inc(turned, 1)

                @block.scalar
                def _(act):
                    for what, target in enumerate((sT, fwd)):
                        for g, qs in enumerate(GROUPS):
                            act.wait_ge(turned, what * NG + g + 1)
                            nc.scalar.activation(target[:, qs[0] * P:(qs[-1] + 1) * P],
                                                 turn_ps[(what * NG + g) % 4][:, 0:len(qs) * P],
                                                 ACT.Copy).then_inc(evacuated, 1)
                    for g, qs in enumerate(GROUPS):
                        act.wait_ge(diff_ready, g + 1)
                        cols = slice(qs[0] * P, (qs[-1] + 1) * P)
                        nc.scalar.activation(sT[:, cols], sT[:, cols], ACT.Exp).then_inc(exp_ready, 1)

        DZ = D + HEADS
        acc = Loan(b1_words).take((NB + 1, DZ))
        with ExitStack() as st:
            loan = Loan(w2_words)
            v_ring = loan.take((U, D))
            onehot = loan.take((8, P))
            pv = loan.take((8, DZ))
            agg_ps = [psum(f"agg_ps{i}", [P, 512], st) for i in range(8)]
            v_in = [sem(f"v_in{i}") for i in range(H8)]
            v_copied = sem("v_copied")
            v_turns = sem("v_turns")
            acc_clear = sem("acc_clear")
            pv_ready = sem("pv_ready")
            w_ready = sem("w_ready")
            agg_made = sem("agg_made")
            acc_done = sem("acc_done")
            w1_in = sem("w1_in")
            with nc.Block() as block:
                @block.sync
                def _(sp):
                    for e in range(NX):
                        sp.dma_start(w1_sb[:, e], W1[e].rearrange("(c p) h -> p c h", p=P)).then_inc(w1_in, 16)
                    sp.wait_ge(w1_in, 16 * NX)

                @block.gpsimd
                def _(pool):
                    gather_rows(pool, v_table, v_ring, v_in, pv_ready, v_copied, v_turns, 4)

                @block.vector
                def _(dve):
                    dve.sem_inc(pv_ready, H8)
                    dve.sem_inc(acc_done, 1)
                    nc.vector.memset(acc[:, :, :], 0.0).then_inc(acc_clear, 1)

                    def hots(p, slot):
                        nc.vector.tensor_tensor(onehot[:, slot * 2:slot * 2 + 2, :],
                                                lane_row[:, :].unsqueeze(1).to_broadcast([P, 2, P]),
                                                rel_f[:, bass.ds(p * 2, 2)].unsqueeze(2).to_broadcast([P, 2, P]),
                                                ALU.is_equal)

                    def weigh(p, j, in_round):
                        dve.wait_ge(v_in[j], in_round)
                        w = weights[:, bass.ds(p * 2, 2), :].unsqueeze(2).to_broadcast([P, 2, HD, HEADS])
                        at = j % 4 * 2
                        nc.vector.tensor_tensor(pv[:, at:at + 2, 0:D].rearrange("p t (d h) -> p t d h", h=HEADS),
                                                v_ring[:, j * 2:j * 2 + 2, :].rearrange("p t (d h) -> p t d h", h=HEADS),
                                                w, ALU.mult).then_inc(pv_ready, 1)

                    def accumulate(p, j, k, b):
                        dve.wait_ge(acc_done, p * 2 + k + 1)
                        nc.vector.tensor_tensor(block_of(acc, b), block_of(acc, b), agg_ps[j % 4 * 2 + k][:, 0:DZ],
                                                ALU.add).then_inc(acc_done, 1)

                    for p in range(2):
                        hots(p, p)
                        weigh(p, p, 32)
                    hots(2, 2)
                    dve.wait_ge(acc_clear, 1)
                    with dve.Fori(0, TR) as i:
                        regs = load_blocks(dve, "v_block", i)
                        for j in range(H8):
                            p = i * H8 + j
                            weigh(p + 2, (j + 2) % H8, i * 32 + 32 + 32 * ((j + 2) // H8))
                            dve.wait_ge(agg_made, p + 1 + 4)
                            accumulate(p, j, 0, regs[j * 2])
                            hots(p + 3, (j + 3) % 4)
                            accumulate(p, j, 1, regs[j * 2 + 1])

                @block.tensor
                def _(pe):
                    pe.sem_inc(agg_made, 4)

                    def aggregate(p, j):
                        pe.wait_ge(w_ready, p + 1)
                        pe.wait_ge(pv_ready, p + 1 + H8)
                        for k in range(2):
                            at = j % 4 * 2 + k
                            ins = nc.tensor.matmul(agg_ps[at][:, 0:DZ], onehot[:, at, :], pv[:, at, :],
                                                   start=True, stop=True)
                        ins.then_inc(agg_made, 1)

                    with pe.Fori(0, TR) as i:
                        for j in range(H8):
                            aggregate(i * H8 + j, j)
                    aggregate(NT // 2, 0)
                    aggregate(NT // 2 + 1, 1)

                @block.scalar
                def _(act):
                    def put_weights(p, j):
                        act.wait_ge(agg_made, p + 1)
                        at = j % 4 * 2
                        nc.scalar.activation(pv[:, at:at + 2, D:DZ], weights[:, bass.ds(p * 2, 2), :],
                                             ACT.Copy).then_inc(w_ready, 1)

                    with act.Fori(0, TR) as i:
                        for j in range(H8):
                            put_weights(i * H8 + j, j)
                    put_weights(NT // 2, 0)
                    put_weights(NT // 2 + 1, 1)

        att_st.close()

        x1_dram = dram("x1_dram", [NB * P, D])
        xs_dram = dram("xs_dram", [NS, D])
        ys_dram = dram("ys_dram", [TE * P, D])
        logits = sb("logits", [P, NB, NX], F32, gnn)
        xn = xres
        with ExitStack() as st:
            att = sb("att", [P, 2, D], F32, st)
            attT = sb("attT", [P, 2, KC, P], F32, st)
            zinv = sb("zinv", [P, NB + 1, HEADS], F32, st)
            wo_sb = sb("wo_sb", [P, KC, D], F32, st)
            bo_sb = sb("bo_sb", [1, D], F32, st)
            wr_sb = sb("wr_sb", [P, KC, NX], F32, st)
            br_sb = sb("br_sb", [1, NX], F32, st)
            uin = sb("uin", [P, 2, D], F32, st)
            uT = sb("uT", [P, 2, KC, P], F32, st)
            zeros = sb("zeros", [P, D], F32, st)
            aT_ps = [psum(f"aT_ps{i}", [P, KC, P], st) for i in range(2)]
            o_ps = [psum(f"o_ps{i}", [P, D], st) for i in range(2)]
            uT_ps = [psum(f"uT_ps{i}", [P, KC, P], st) for i in range(2)]
            lg_ps = psum("lg_ps", [P, 2, NX], st)
            wo_in = sem("wo_in")
            zeroed = sem("zeroed")
            xs_zero = sem("xs_zero")
            nd = sem("nd")
            att_ready = sem("att_ready")
            att_turned = sem("att_turned")
            attT_ready = sem("attT_ready")
            o_made = sem("o_made")
            x1_ready = sem("x1_ready")
            x1_stored = sem("x1_stored")
            stats1 = sem("stats1")
            var1 = sem("var1")
            rstd1 = sem("rstd1")
            u_ready = sem("u_ready")
            uin_ready = sem("uin_ready")
            uin_free = sem("uin_free")
            u_turned = sem("u_turned")
            uT_ready = sem("uT_ready")
            lg_made = sem("lg_made")
            lg_kept = sem("lg_kept")
            w2_in = sem("w2_in")
            xn_ready = sem("xn_ready")
            with nc.Block() as block:
                @block.sync
                def _(sp):
                    sp.dma_start(wo_sb[:, :, :], Wo.rearrange("(c p) n -> p c n", p=P)).then_inc(wo_in, 16)
                    sp.dma_start(bo_sb[:, :], bo.rearrange("(a n) -> a n", a=1)).then_inc(wo_in, 16)
                    sp.dma_start(wr_sb[:, :, :], Wr.rearrange("(c p) n -> p c n", p=P)).then_inc(wo_in, 16)
                    sp.dma_start(br_sb[:, :], br.rearrange("(a n) -> a n", a=1)).then_inc(wo_in, 16)
                    sp.wait_ge(zeroed, 1)
                    sp.dma_start(xs_dram.rearrange("(t p) d -> p t d", p=P),
                                 zeros[:, :].unsqueeze(1).to_broadcast([P, NS // P, D])).then_inc(xs_zero, 16)
                    with sp.Fori(0, NB) as b:
                        sp.wait_ge(x1_ready, b + 1)
                        sp.dma_start(x1_dram[bass.ds(b * P, P), :], block_of(xres, b)).then_inc(x1_stored, 16)
                    sp.wait_ge(x1_stored, 16 * NB)
                    sp.wait_ge(xs_zero, 16)

                @block.gpsimd
                def _(pool):
                    nc.gpsimd.memset(zeros[:, :], 0.0).then_inc(zeroed, 1)
                    pool.wait_ge(var1, 1)
                    nc.gpsimd.tensor_tensor(rstd[:, :], var[:, :], minus_half[:, :], ALU.pow).then_inc(rstd1, 1)
                    with pool.Fori(0, NB // 2) as i:
                        for j in range(2):
                            b = i * 2 + j
                            pool.wait_ge(u_ready, b + 1)
                            pool.wait_ge(uin_free, b + 1)
                            nc.gpsimd.tensor_copy(uin[:, j, :], block_of(xn, b)).then_inc(uin_ready, 1)
                    pool.wait_ge(var1, 2)
                    pool.wait_ge(uin_ready, NB)
                    nc.gpsimd.tensor_tensor(rstd[:, :], var[:, :], minus_half[:, :], ALU.pow).then_inc(rstd1, 1)

                @block.vector
                def _(dve):
                    n = [0]

                    def link(ins):
                        n[0] += 1
                        ins.then_inc(nd, 1)
                        dve.wait_ge(nd, n[0])

                    link(nc.vector.tensor_scalar(zinv[:, :, :], acc[:, :, D:DZ], 0.5, None, ALU.max))
                    link(nc.vector.reciprocal(zinv[:, :, :], zinv[:, :, :]))

                    def normalise(b, j):
                        z = zinv[:, bass.ds(b, 1), :].to_broadcast([P, HD, HEADS])
                        sums = acc[:, bass.ds(b, 1), 0:D].rearrange("p a (d h) -> p (a d) h", h=HEADS)
                        nc.vector.tensor_tensor(att[:, j, :].rearrange("p (d h) -> p d h", h=HEADS), sums, z,
                                                ALU.mult).then_inc(att_ready, 1)

                    normalise(0, 0)
                    with dve.Fori(0, NB // 2) as i:
                        for j in range(2):
                            b = i * 2 + j
                            normalise(b + 1, 1 - j)
                            dve.wait_ge(o_made, b + 1)
                            nc.vector.tensor_tensor(block_of(xres, b), block_of(xres, b), o_ps[j][:, :],
                                                    ALU.add).then_inc(x1_ready, 1)
                            dve.wait_ge(x1_ready, b + 1)
                            nc.vector.bn_stats(stats[:, bass.ds(b, 1), :].rearrange("p a s -> p (a s)"),
                                               block_of(xres, b)).then_inc(stats1, 1)
                    dve.wait_ge(stats1, NB)
                    mean_and_variance(link)
                    nc.vector.tensor_copy(var[:, :], var[:, :]).then_inc(var1, 1)
                    dve.wait_ge(rstd1, 1)
                    dve.wait_ge(x1_stored, 16 * NB)
                    with dve.Fori(0, NB // 2) as i:
                        for j in range(2):
                            b = i * 2 + j
                            nc.vector.tensor_scalar(block_of(xn, b), block_of(xres, b), mean[:, bass.ds(b, 1)],
                                                    rstd[:, bass.ds(b, 1)], ALU.subtract, ALU.mult).then_inc(u_ready, 1)
                            dve.wait_ge(u_ready, b + 1)
                            nc.vector.bn_stats(stats[:, bass.ds(b, 1), :].rearrange("p a s -> p (a s)"),
                                               block_of(xn, b)).then_inc(stats1, 1)
                    dve.wait_ge(stats1, 2 * NB)
                    mean_and_variance(link)
                    nc.vector.tensor_copy(var[:, :], var[:, :]).then_inc(var1, 1)
                    dve.wait_ge(rstd1, 2)
                    with dve.Fori(0, NB // 2) as i:
                        for j in range(2):
                            b = i * 2 + j
                            nc.vector.tensor_scalar(block_of(xn, b), block_of(xn, b), mean[:, bass.ds(b, 1)],
                                                    rstd[:, bass.ds(b, 1)], ALU.subtract, ALU.mult).then_inc(xn_ready, 1)

                @block.tensor
                def _(pe):
                    pe.sem_inc(uin_free, 2)
                    pe.wait_ge(wo_in, 64)
                    with pe.Fori(0, NB // 2) as i:
                        for j in range(2):
                            b = i * 2 + j
                            pe.wait_ge(att_ready, b + 1)
                            for c in range(KC):
                                ins = nc.tensor.transpose(aT_ps[j][:, c, :], att[:, j, c * P:(c + 1) * P], ident[:, :])
                            ins.then_inc(att_turned, 1)
                            pe.wait_ge(attT_ready, b + 1)
                            for c in range(KC):
                                nc.tensor.matmul(o_ps[j][:, :], attT[:, j, c, :], wo_sb[:, c, :], start=(c == 0),
                                                 stop=False)
                            nc.tensor.matmul(o_ps[j][:, :], ones_row, bo_sb[:, :], start=False,
                                             stop=True).then_inc(o_made, 1)
                    with pe.Fori(0, NB // 2) as i:
                        for j in range(2):
                            b = i * 2 + j
                            pe.wait_ge(uin_ready, b + 1)
                            for c in range(KC):
                                ins = nc.tensor.transpose(uT_ps[j][:, c, :], uin[:, j, c * P:(c + 1) * P], ident[:, :])
                            ins.then_inc(u_turned, 1)
                            pe.wait_ge(uT_ready, b + 1)
                            for c in range(KC):
                                ins = nc.tensor.matmul(lg_ps[:, j, :], uT[:, j, c, :], wr_sb[:, c, :], start=(c == 0),
                                                       stop=False)
                            ins.then_inc(uin_free, 1)
                            nc.tensor.matmul(lg_ps[:, j, :], ones_row, br_sb[:, :], start=False,
                                             stop=True).then_inc(lg_made, 1)

                @block.scalar
                def _(act):
                    for e in range(NX):
                        act.dma_start(w2_sb[:, e], W2[e].rearrange("(c p) d -> p c d", p=P)).then_inc(w2_in, 16)
                    with act.Fori(0, NB // 2) as i:
                        for j in range(2):
                            act.wait_ge(att_turned, i * 2 + j + 1)
                            nc.scalar.activation(attT[:, j, :, :], aT_ps[j][:, :, :], ACT.Copy).then_inc(attT_ready, 1)
                    with act.Fori(0, NB // 2) as i:
                        for j in range(2):
                            b = i * 2 + j
                            act.wait_ge(u_turned, b + 1)
                            nc.scalar.activation(uT[:, j, :, :], uT_ps[j][:, :, :], ACT.Copy).then_inc(uT_ready, 1)
                            act.wait_ge(lg_made, b + 1)
                            nc.scalar.activation(block_of(logits, b), lg_ps[:, j, :], ACT.Copy).then_inc(lg_kept, 1)
                    act.wait_ge(w2_in, 16 * NX)

        with ExitStack() as st:
            top = sb("top", [P, NB, 8], F32, st)
            top_i = sb("top_i", [P, NB, 8], U32, st)
            ids = sb("ids", [P, 2, NB], F32, st)
            ex_no = sb("ex_no", [P, NX], F32, st)
            ex_no_i = sb("ex_no_i", [P, NX], I32, st)
            token_i = sb("token_i", [P, NB], I32, st)
            token_ok = sb("token_ok", [P, NB], F32, st)
            tile_no_i = sb("tile_no_i", [P, NS // P], I32, st)
            tile_no = sb("tile_no", [P, NS // P], F32, st)
            pick = sb("pick", [P, 2, NB, NX], F32, st)
            both = sb("both", [P, NB, NX], F32, st)
            before = sb("before", [P, P], F32, st)
            inc = sb("inc", [P, NX, NB], F32, st)
            keep = sb("keep", [P, NX, NB], F32, st)
            total = sb("total", [P, NX, NB], F32, st)
            tiles_i = sb("tiles_i", [P, NX], I32, st)
            tiles = sb("tiles", [P, NX], F32, st)
            tile_end = sb("tile_end", [P, NX], F32, st)
            base = sb("base", [P, NX], F32, st)
            one_x = sb("one_x", [P, NX], F32, st)
            place = sb("place", [P, NB, NX], F32, st)
            picked = sb("picked", [P, 2, NB, NX], F32, st)
            rowf = sb("rowf", [P, 2, NB], F32, st)
            ended = sb("ended", [P, NS // P, NX], F32, st)
            tile_f = sb("tile_f", [P, NS // P], F32, st)
            low = sb("low", [P, 2, NB], F32, st)
            pre_ps = psum("pre_ps", [P, NB, NX], st)
            tot_ps = psum("tot_ps", [P, NB, NX], st)
            rt = sem("rt")
            r_const = sem("r_const")
            gap_ready = sem("gap_ready")
            gap_exp = sem("gap_exp")
            both_ready = sem("both_ready")
            pre_made = sem("pre_made")
            rows_ready = sem("rows_ready")
            scattered = sem("scattered")
            b1_in = sem("b1_in")
            with nc.Block() as block:
                @block.sync
                def _(sp):
                    sp.dma_start(b1_sb[:, :, :], b1.unsqueeze(0).to_broadcast([P, NX, H])).then_inc(b1_in, 16)
                    sp.wait_ge(b1_in, 16)

                @block.gpsimd
                def _(pool):
                    nc.gpsimd.iota(ex_no_i[:, :], [[1, NX]], base=0, channel_multiplier=0).then_inc(r_const, 1)
                    nc.gpsimd.iota(token_i[:, :], [[P, NB]], base=0, channel_multiplier=1).then_inc(r_const, 1)
                    nc.gpsimd.iota(tile_no_i[:, :], [[1, NS // P]], base=0, channel_multiplier=0).then_inc(r_const, 1)
                    nc.gpsimd.affine_select(out=before[:, :], in_=ones[:, :], compare_op=ALU.is_gt, fill=0.0,
                                            base=0, pattern=[[1, P]], channel_multiplier=-1).then_inc(r_const, 1)
                    pool.wait_ge(rows_ready, 1)
                    for b in range(NBR):
                        live = P if b < NBF else TAIL
                        for k in range(2):
                            nc.gpsimd.indirect_dma_start(
                                xs_dram, bass.IndirectOffsetOnAxis(row_i[0:live, k, b:b + 1].bitcast(U32), 0),
                                xn[0:live, b, :], None).then_inc(scattered, 16)
                    pool.wait_ge(scattered, 32 * NBR)

                @block.vector
                def _(dve):
                    n = [0]

                    def link(ins):
                        n[0] += 1
                        ins.then_inc(rt, 1)
                        dve.wait_ge(rt, n[0])

                    dve.wait_ge(r_const, 3)
                    nc.vector.tensor_copy(ex_no[:, :], ex_no_i[:, :])
                    nc.vector.tensor_copy(tile_no[:, :], tile_no_i[:, :])
                    link(nc.vector.tensor_copy(token_ok[:, :], token_i[:, :]))
                    link(nc.vector.tensor_scalar(token_ok[:, :], token_ok[:, :], float(N), None, ALU.is_lt))
                    for b in range(NB):
                        ins = nc.vector.max(top[:, b, :], logits[:, b, :])
                    link(ins)
                    for b in range(NB):
                        ins = nc.vector.max_index(top_i[:, b, :], top[:, b, :], logits[:, b, :])
                    link(ins)
                    nc.vector.tensor_tensor(low[:, 0, :], top[:, :, 1], top[:, :, 0], ALU.subtract).then_inc(gap_ready, 1)
                    for k in range(2):
                        link(nc.vector.tensor_copy(ids[:, k, :], top_i[:, :, k]))
                    for k in range(2):
                        for b in range(NB):
                            ins = nc.vector.tensor_scalar(pick[:, k, b, :], ex_no[:, :], ids[:, k, b:b + 1],
                                                          token_ok[:, b:b + 1], ALU.is_equal, ALU.mult)
                    link(ins)
                    nc.vector.tensor_tensor(both[:, :, :], pick[:, 0], pick[:, 1], ALU.add).then_inc(both_ready, 1)
                    dve.wait_ge(gap_exp, 1)
                    link(nc.vector.tensor_scalar(wts[:, 0, :], low[:, 1, :], 1.0, None, ALU.add))
                    link(nc.vector.reciprocal(wts[:, 0, :], wts[:, 0, :]))
                    link(nc.vector.tensor_tensor(wts[:, 1, :], wts[:, 0, :], low[:, 1, :], ALU.mult))
                    link(nc.vector.memset(keep[:, :, :], 1.0))
                    link(nc.vector.memset(keep[:, :, 0:1], 0.0))
                    link(nc.vector.memset(one_x[:, :], 1.0))
                    dve.wait_ge(pre_made, 1)
                    link(nc.vector.tensor_copy(total[:, :, :], tot_ps[:, :, :].rearrange("p b e -> p e b")))
                    link(nc.vector.tensor_tensor_scan(inc[:, :, :].rearrange("p e b -> p (e b)"),
                                                      keep[:, :, :].rearrange("p e b -> p (e b)"),
                                                      total[:, :, :].rearrange("p e b -> p (e b)"), 0.0,
                                                      ALU.mult, ALU.add))
                    link(nc.vector.tensor_scalar(tiles[:, :], inc[:, :, NB - 1], float(P - 1), None, ALU.add))
                    link(nc.vector.tensor_copy(tiles_i[:, :], tiles[:, :]))
                    link(nc.vector.tensor_scalar(tiles_i[:, :], tiles_i[:, :], LOGP, None, ALU.logical_shift_right))
                    link(nc.vector.tensor_copy(tiles[:, :], tiles_i[:, :]))
                    link(nc.vector.tensor_tensor_scan(tile_end[:, :], one_x[:, :], tiles[:, :], 0.0, ALU.mult, ALU.add))
                    link(nc.vector.tensor_tensor(base[:, :], tile_end[:, :], tiles[:, :], ALU.subtract))
                    link(nc.vector.tensor_scalar(base[:, :], base[:, :], float(P), None, ALU.mult))
                    link(nc.vector.tensor_tensor(inc[:, :, :], inc[:, :, :], total[:, :, :], ALU.subtract))
                    link(nc.vector.tensor_tensor(inc[:, :, :], inc[:, :, :],
                                                 base[:, :].unsqueeze(2).to_broadcast([P, NX, NB]), ALU.add))
                    link(nc.vector.tensor_tensor(place[:, :, :], inc[:, :, :].rearrange("p e b -> p b e"),
                                                 pre_ps[:, :, :], ALU.add))
                    for k in range(2):
                        link(nc.vector.tensor_tensor(picked[:, k], pick[:, k], place[:, :, :], ALU.mult))
                        link(nc.vector.tensor_reduce(rowf[:, k], picked[:, k], AX.X, ALU.add))
                    nc.vector.tensor_copy(row_i[:, :, :], rowf[:, :, :]).then_inc(rows_ready, 1)
                    for e in range(NX):
                        ins = nc.vector.tensor_scalar(ended[:, :, e], tile_no[:, :], tile_end[:, e:e + 1], None,
                                                      ALU.is_ge)
                    link(ins)
                    link(nc.vector.tensor_reduce(tile_f[:, :], ended[:, :, :], AX.X, ALU.add))
                    link(nc.vector.tensor_scalar(tile_f[:, :], tile_f[:, :], float(NX - 1), None, ALU.min))
                    link(nc.vector.tensor_copy(tile_ex[:, :], tile_f[:, :]))

                @block.scalar
                def _(act):
                    act.wait_ge(gap_ready, 1)
                    nc.scalar.activation(low[:, 1, :], low[:, 0, :], ACT.Exp).then_inc(gap_exp, 1)

                @block.tensor
                def _(pe):
                    pe.wait_ge(both_ready, 1)
                    pe.wait_ge(r_const, 4)
                    nc.tensor.matmul(pre_ps[:, :, :].rearrange("p b e -> p (b e)"), before[:, :],
                                     both[:, :, :].rearrange("p b e -> p (b e)"), start=True, stop=True)
                    nc.tensor.matmul(tot_ps[:, :, :].rearrange("p b e -> p (b e)"), ones[:, :],
                                     both[:, :, :].rearrange("p b e -> p (b e)"), start=True,
                                     stop=True).then_inc(pre_made, 1)

        gnn.close()
        with ExitStack() as st:
            b2_sb = sb("b2_sb", [P, NX, D], F32, st)
            g_sb = sb("g_sb", [P, NX * KC], F32, st)
            be_sb = sb("be_sb", [P, NX * KC], F32, st)
            xs = sb("xs", [P, UE, D], F32, st)
            xeT = sb("xeT", [P, 2, KC, P], F32, st)
            h_sb = sb("h_sb", [P, H], F32, st)
            hT = sb("hT", [P, HC, P], F32, st)
            ys = sb("ys", [P, UE, D], F32, st)
            xsT_ps = psum("xsT_ps", [P, KC, P], st)
            h_ps = psum("h_ps", [P, H], st)
            hT_ps = psum("hT_ps", [P, HC, P], st)
            y_ps = [psum(f"y_ps{i}", [P, D], st) for i in range(2)]
            HB = 512
            we_in = sem("we_in")
            xs_in = [sem(f"xs_in{j}") for j in range(UE)]
            ys_out = [sem(f"ys_out{j}") for j in range(UE)]
            xs_turned = sem("xs_turned")
            xeT_ready = sem("xeT_ready")
            h_made = sem("h_made")
            h_biased = sem("h_biased")
            h_ready = sem("h_ready")
            h_turned = sem("h_turned")
            hT_ready = sem("hT_ready")
            y_made = sem("y_made")
            ys_ready = sem("ys_ready")

            def load_experts(eng, name, first, count):
                regs = [eng.alloc_register(f"{name}{k}") for k in range(count)]
                eng.reg_load(regs, tile_ex[0:1, bass.ds(first, count)])
                return [eng.snap(reg, donate=True, min_val=0, max_val=NX - 1) for reg in regs]

            with nc.Block() as block:
                @block.sync
                def _(sp):
                    for j in range(UE):
                        sp.sem_inc(ys_out[j], 16)
                        sp.dma_start(xs[:, j, :], xs_dram[j * P:(j + 1) * P, :]).then_inc(xs_in[j], 16)
                    with sp.Fori(0, TE // UE) as i:
                        for j in range(UE):
                            t = i * UE + j
                            sp.wait_ge(xs_turned, t + 1)
                            sp.dma_start(xs[:, j, :], xs_dram[bass.ds((t + UE) * P, P), :]).then_inc(xs_in[j], 16)
                            sp.wait_ge(ys_ready, t + 1)
                            sp.dma_start(ys_dram[bass.ds(t * P, P), :], ys[:, j, :]).then_inc(ys_out[j], 16)
                    for j in range(UE):
                        sp.wait_ge(xs_in[j], 16 * (TE // UE + 1))
                        sp.wait_ge(ys_out[j], 16 * (TE // UE + 1))

                @block.scalar
                def _(act):
                    act.dma_start(g_sb[:, :], ln_g.rearrange("e (c p) -> p (e c)", p=P),
                                  allow_slow_non_contiguous=True).then_inc(we_in, 16)
                    act.dma_start(be_sb[:, :], ln_b.rearrange("e (c p) -> p (e c)", p=P),
                                  allow_slow_non_contiguous=True).then_inc(we_in, 16)
                    act.dma_start(b2_sb[:, :, :], b2.unsqueeze(0).to_broadcast([P, NX, D])).then_inc(we_in, 16)

                    with act.Fori(0, TE // UE) as i:
                        for j in range(UE):
                            t = i * UE + j
                            act.wait_ge(h_biased, t + 1)
                            nc.scalar.activation(h_sb[:, :], h_sb[:, :], ACT.Gelu).then_inc(h_ready, 1)
                            for half in range(2):
                                ks = slice(half * HC // 2, (half + 1) * HC // 2)
                                act.wait_ge(h_turned, t * 2 + half + 1)
                                nc.scalar.activation(hT[:, ks, :], hT_ps[:, ks, :], ACT.Copy).then_inc(hT_ready, 1)

                @block.vector
                def _(dve):
                    def scale_and_bias(t, j, e):
                        dve.wait_ge(xs_turned, t + 1)
                        for c in range(KC):
                            at = bass.ds(e * KC + c, 1)
                            ins = nc.vector.tensor_scalar(xeT[:, j % 2, c, :], xsT_ps[:, c, :], g_sb[:, at],
                                                          be_sb[:, at], ALU.mult, ALU.add)
                        ins.then_inc(xeT_ready, 1)

                    def add_b1(t, e):
                        dve.wait_ge(h_made, t + 1)
                        for half in range(H // HB):
                            cols = slice(half * HB, (half + 1) * HB)
                            ins = nc.vector.tensor_tensor(
                                h_sb[:, cols], h_ps[:, cols],
                                b1_sb[:, bass.ds(e, 1), cols].rearrange("p a h -> p (a h)"), ALU.add)
                        ins.then_inc(h_biased, 1)

                    dve.wait_ge(we_in, 16 * 3)
                    first = load_experts(dve, "v_first", 0, 2)
                    scale_and_bias(0, 0, first[0])
                    scale_and_bias(1, 1, first[1])
                    add_b1(0, first[0])
                    with dve.Fori(0, TE // UE) as i:
                        e = load_experts(dve, "v_expert", i * UE, UE + 2)
                        for j in range(UE):
                            t = i * UE + j
                            scale_and_bias(t + 2, j, e[j + 2])
                            add_b1(t + 1, e[j + 1])
                            dve.wait_ge(y_made, t + 1)
                            dve.wait_ge(ys_out[j], i * 16 + 16)
                            nc.vector.tensor_tensor(ys[:, j, :], y_ps[j % 2][:, :], block_of(b2_sb, e[j]),
                                                    ALU.add).then_inc(ys_ready, 1)

                @block.tensor
                def _(pe):
                    def turn_rows(t, slot, in_round):
                        pe.wait_ge(xs_in[slot], in_round)
                        for c in range(KC):
                            ins = nc.tensor.transpose(xsT_ps[:, c, :], xs[:, slot, c * P:(c + 1) * P], ident[:, :])
                        ins.then_inc(xs_turned, 1)

                    def first_layer(t, j, e):
                        pe.wait_ge(xeT_ready, t + 1)
                        for half in range(H // HB):
                            cols = slice(half * HB, (half + 1) * HB)
                            for c in range(KC):
                                ins = nc.tensor.matmul(
                                    h_ps[:, cols], xeT[:, j % 2, c, :],
                                    w1_sb[:, bass.ds(e, 1), c, cols].rearrange("p a h -> p (a h)"),
                                    start=(c == 0), stop=(c == KC - 1))
                        ins.then_inc(h_made, 1)

                    def turn_hidden(t):
                        pe.wait_ge(h_ready, t + 1)
                        for k in range(HC):
                            ins = nc.tensor.transpose(hT_ps[:, k, :], h_sb[:, k * P:(k + 1) * P], ident[:, :])
                            if k % (HC // 2) == HC // 2 - 1:
                                ins.then_inc(h_turned, 1)

                    def second_layer(t, j, e):
                        for k in range(HC):
                            if k % (HC // 2) == 0:
                                pe.wait_ge(hT_ready, t * 2 + k // (HC // 2) + 1)
                            ins = nc.tensor.matmul(y_ps[j % 2][:, :], hT[:, k, :],
                                                   w2_sb[:, bass.ds(e, 1), k, :].rearrange("p a d -> p (a d)"),
                                                   start=(k == 0), stop=(k == HC - 1))
                        ins.then_inc(y_made, 1)

                    turn_rows(0, 0, 16)
                    pe.wait_ge(xeT_ready, 1)
                    turn_rows(1, 1, 16)
                    first_layer(0, 0, load_experts(pe, "p_first", 0, 1)[0])
                    pe.wait_ge(xeT_ready, 2)
                    turn_rows(2, 2, 16)
                    with pe.Fori(0, TE // UE) as i:
                        e = load_experts(pe, "p_expert", i * UE, UE + 1)
                        for j in range(UE):
                            t = i * UE + j
                            turn_hidden(t)
                            first_layer(t + 1, j + 1, e[j + 1])
                            second_layer(t, j, e[j])
                            pe.wait_ge(xeT_ready, t + 3)
                            turn_rows(t + 3, (j + 3) % UE, i * 16 + 16 + 16 * ((j + 3) // UE))

        ffn.close()
        with ExitStack() as st:
            R = 8
            x1 = sb("x1", [P, NBR, D], F32, st)
            yk = sb("yk", [P, NBR, 2, D], F32, st)
            x1_in = sem("x1_in")
            y_in = [sem(f"y_in{r}") for r in range(R)]
            half_sum = sem("half_sum")
            out_ready = sem("out_ready")
            out_stored = sem("out_stored")
            with nc.Block() as block:
                @block.sync
                def _(sp):
                    sp.dma_start(x1[:, :, :], x1_dram[0:NBR * P, :].rearrange("(b p) d -> p b d", p=P)).then_inc(x1_in, 16)
                    for b in range(NBR):
                        live = P if b < NBF else TAIL
                        sp.wait_ge(out_ready, b + 1)
                        sp.dma_start(out[b * P:b * P + live, :], x1[0:live, b, :]).then_inc(out_stored, 16)
                    sp.wait_ge(out_stored, 16 * NBR)

                @block.gpsimd
                def _(pool):
                    for b in range(NBR):
                        live = P if b < NBF else TAIL
                        if b >= R:
                            pool.wait_ge(out_ready, b - R + 1)
                        for k in range(2):
                            nc.gpsimd.indirect_dma_start(
                                yk[0:live, b, k, :], None, ys_dram,
                                bass.IndirectOffsetOnAxis(row_i[0:live, k, b:b + 1].bitcast(U32), 0)
                            ).then_inc(y_in[b % R], 16)

                @block.vector
                def _(dve):
                    dve.wait_ge(x1_in, 16)
                    for b in range(NBR):
                        live = P if b < NBF else TAIL
                        dve.wait_ge(y_in[b % R], 32 * (b // R + 1))
                        for k, signal in enumerate((half_sum, out_ready)):
                            nc.vector.scalar_tensor_tensor(out=x1[0:live, b, :], in0=yk[0:live, b, k, :],
                                                           scalar=wts[0:live, k, b:b + 1], in1=x1[0:live, b, :],
                                                           op0=ALU.mult, op1=ALU.add).then_inc(signal, 1)
                            dve.wait_ge(signal, b + 1)


_GNN = ["Wq", "bq", "Wk", "bk", "Wv", "bv", "Wo", "bo"]
_FFN = ["Wr", "br", "ln_g", "ln_b", "W1", "b1", "W2", "b2"]
_INS = ["x", "src", "dst"] + ["L0_gnn_" + n for n in _GNN] + ["L0_ffn_" + n for n in _FFN]


def kernel(**inputs):
    import numpy as _np
    import concourse.bacc as _bacc
    from concourse import mybir as _mybir
    from concourse.bass_utils import run_bass_kernel_spmd as _run

    nc = _bacc.Bacc("TRN2", target_bir_lowering=False, num_devices=1)
    arrays, args = {}, []
    for name in _INS:
        a = _np.ascontiguousarray(inputs[name])
        arrays[f"in_{name}_dram"] = a
        args.append(nc.dram_tensor(f"in_{name}_dram", a.shape, _mybir.dt.from_np(a.dtype), kind="ExternalInput").ap())
    out = nc.dram_tensor("out_dram", inputs["x"].shape, _mybir.dt.float32, kind="ExternalOutput").ap()
    gnn_moe_kernel(nc, *args, out)
    r = _run(nc, [arrays], core_ids=[0])
    return r.results[0]["out_dram"]
```

```python
from contextlib import ExitStack

import numpy as np

import concourse.bass as bass
from concourse import mybir

F32 = mybir.dt.float32
BF16 = mybir.dt.bfloat16
I32 = mybir.dt.int32
U32 = mybir.dt.uint32
ALU = mybir.AluOpType
ACT = mybir.ActivationFunctionType
AX = mybir.AxisListType

P = 128
BIG = 1.0e30
EPS = 1e-5


def gnn_moe_kernel(nc, x, src, dst, Wq, bq, Wk, bk, Wv, bv, Wo, bo, Wr, br, ln_g, ln_b, W1, b1, W2, b2, out):
    N, D = x.shape
    E = src.shape[0]
    NX, H = W1.shape[0], W1.shape[2]
    HEADS, HD = 8, D // 8
    KC = D // P
    HC = H // P
    SCALE = float(HD) ** -0.5

    NBF = N // P
    TAIL = N - NBF * P
    NBR = NBF + 1
    NB = NBR + 1
    NT = 416
    assert NT % 32 == 0 and NT * P >= E + NBR * (P - 1) and NB % 2 == 0
    SORT = 1 << 16
    SC = SORT // P
    LOGN, LOGP = 16, 7
    SHIFT = 12
    RADIX = 1 << SHIFT
    PAD_DST = RADIX - 1
    FILL = ((NB - 1) * P + P - 1) * RADIX + PAD_DST
    assert N < PAD_DST and FILL < 1 << 24 and SORT >= NT * P
    ER = 125
    EC = E // ER
    assert ER * EC == E and EC + NBR <= SC

    TE = (2 * N + NX * (P - 1)) // P
    UE = 4
    NS = (TE + UE) * P
    assert TE % UE == 0

    ctx = ExitStack()
    with ctx:
        def sem(name):
            return ctx.enter_context(nc.semaphore(name))

        def dram(name, shape):
            return nc.dram_tensor(name, shape, F32, kind="Internal").ap()

        k_table = dram("k_table", [NB * P, D])
        v_table = dram("v_table", [NB * P, D])

        def sb(name, shape, dt=F32, c=ctx):
            return c.enter_context(nc.sbuf_tensor(name, shape, dt))

        def psum(name, shape, c, dt=F32):
            return c.enter_context(nc.psum_tensor(name, shape, dt))

        ident = sb("ident", [P, P])
        ones = sb("ones", [P, P])
        ones_row = ones[0:1, :]
        wts = sb("wts", [P, 2, NB])
        token_of = sb("token_of", [P, NS // P], I32)
        place_of = sb("place_of", [P, NS // P], I32)
        tile_ex = sb("tile_ex", [P, NS // P], I32)
        lane = sb("lane", [P, 1], I32)
        lane_f = sb("lane_f", [P, 1])
        stats = sb("stats", [P, NB, 6])
        mean = sb("mean", [P, NB])
        var = sb("var", [P, NB])
        half_diff = sb("half_diff", [P, NB])
        rstd = sb("rstd", [P, NB])
        minus_half = sb("minus_half", [P, NB])

        def block_of(table, b):
            return table[:, bass.ds(b, 1), :].rearrange("p a d -> p (a d)")

        def mean_and_variance(link):
            link(nc.vector.tensor_tensor(mean[:, :], stats[:, :, 1], stats[:, :, 4], ALU.add))
            link(nc.vector.tensor_tensor(half_diff[:, :], stats[:, :, 1], stats[:, :, 4], ALU.subtract))
            link(nc.vector.tensor_tensor(var[:, :], stats[:, :, 2], stats[:, :, 5], ALU.add))
            link(nc.vector.tensor_scalar(mean[:, :], mean[:, :], 0.5, None, ALU.mult))
            link(nc.vector.tensor_scalar(half_diff[:, :], half_diff[:, :], 0.5, None, ALU.mult))
            link(nc.vector.tensor_scalar(var[:, :], var[:, :], 1.0 / D, EPS, ALU.mult, ALU.add))
            link(nc.vector.tensor_tensor(half_diff[:, :], half_diff[:, :], half_diff[:, :], ALU.mult))
            link(nc.vector.tensor_tensor(var[:, :], var[:, :], half_diff[:, :], ALU.add))

        ffn = ExitStack()
        ffn.__enter__()
        w1_sb = sb("w1_sb", [P, NX, KC, H], F32, ffn)
        w2_sb = sb("w2_sb", [P, NX, HC, D], F32, ffn)
        w1_now = sb("w1_now", [P, 8192], F32, ffn)
        b2_sb = w1_now[:, 8192 - NX * D:8192].rearrange("p (e d) -> p e d", e=NX)
        g_sb = sb("g_sb", [P, NX * KC], F32, ffn)
        be_sb = sb("be_sb", [P, NX * KC], F32, ffn)
        b1_sb = sb("b1_sb", [P, NX * HC], F32, ffn)

        class Loan:

            def __init__(self, region):
                self.region, self.at = region, 0

            def take(self, shape, dt=F32):
                words = int(np.prod(shape)) * mybir.dt.size(dt) // 4
                cols = self.region[:, self.at:self.at + words]
                self.at += words
                assert self.at <= self.region.shape[1]
                if dt is not F32:
                    cols = cols.bitcast(dt)
                names = "abc"[:len(shape)]
                return cols.rearrange(f"p ({' '.join(names)}) -> p {' '.join(names)}", **dict(zip(names, shape)))

        w1_words = w1_sb[:, :, :, :].rearrange("p e c h -> p (e c h)")
        w2_words = w2_sb[:, :, :, :].rearrange("p e c d -> p (e c d)")
        now_words = w1_now[:, :]

        gnn = ExitStack()
        gnn.__enter__()
        xres = sb("xres", [P, NB, D], F32, gnn)
        U = 16
        UV = 32
        loan = Loan(w2_words)
        q_parts = loan.take((3, NB, D), BF16)
        scores = loan.take((NT, HEADS))
        key_i = loan.take((SC,), I32)
        dst_i = loan.take((SC,), I32)
        src_f = loan.take((SC,))
        rel_f = loan.take((SC,))
        real_f = loan.take((SC,))
        blk_i = loan.take((SC,), I32)
        with ExitStack() as st:
            srcs = sb("srcs", [ER, EC], I32, st)
            dsts = sb("dsts", [ER, EC], I32, st)
            blkf = sb("blkf", [ER, EC], F32, st)
            tmp_i = sb("tmp_i", [P, SC], I32, st)
            tmp_f = sb("tmp_f", [P, SC], F32, st)
            blkno_i = sb("blkno_i", [P, NBR], I32, st)
            blkno = sb("blkno", [P, NBR], F32, st)
            loan = Loan(w1_words)
            xhat = loan.take((NB, D))
            inblk = loan.take((NBR, EC), BF16)[0:ER]
            bias = loan.take((3 * D,))[0:3]
            bias_rest = loan.take((3 * D,))[0:3]
            bias_cut = loan.take((3, 3 * D), BF16)[0:3]
            bias_parts = loan.take((3 * D,), BF16)[0:3]
            ones_h = loan.take((P,), BF16)[0:3]
            loan = Loan(now_words)
            cnt = sb("cnt", [ER, NBR], F32, st)
            need_i = sb("need_i", [P, NBR], I32, st)
            need = sb("need", [P, NBR], F32, st)
            padkey = sb("padkey", [P, NBR], F32, st)
            dir_i = sb("dir_i", [P, LOGP], I32, st)
            dirs = sb("dirs", [P, LOGP], F32, st)
            keys = [loan.take((SC,)) for i in range(2)]
            half = loan.take((SC // 2,))
            xin = loan.take((2, D))
            xT = loan.take((2, KC, P))
            wq_sb = loan.take((KC, D))
            wkv_sb = loan.take((KC, 2 * D))
            kv_out = loan.take((2, 2 * D))
            q_full = loan.take((2, D))
            q_rest = loan.take((2, D))
            xT_ps = psum("xT_ps", [P, 2, KC, P], st)
            q_ps = psum("q_ps", [P, 2, D], st)
            kv_ps = [psum(f"kv_ps{i}", [P, 2 * D], st) for i in range(2)]
            cnt_ps = psum("cnt_ps", [P, NBR], st)
            swap_ps = [psum(f"swap_ps{i}", [P, SC], st) for i in range(2)]

            edges_in = sem("edges_in")
            x_in = sem("x_in")
            w_in = sem("w_in")
            bias_in = sem("bias_in")
            bias_step = sem("bias_step")
            consts = sem("consts")
            cdone = sem("cdone")
            cleared = sem("cleared")
            counted = sem("counted")
            cnt_sum = sem("cnt_sum")
            stats_made = sem("stats_made")
            var_ready = sem("var_ready")
            rstd_ready = sem("rstd_ready")
            xhat_ready = sem("xhat_ready")
            xin_ready = sem("xin_ready")
            xin_free = sem("xin_free")
            xT_made = sem("xT_made")
            xT_ready = sem("xT_ready")
            q_made = sem("q_made")
            kv_made = sem("kv_made")
            q_kept = sem("q_kept")
            q_turns = sem("q_turns")
            q_cut = sem("q_cut")
            kv_ready = sem("kv_ready")
            k_stored = [sem(f"k_stored{i}") for i in range(2)]
            sort_step = sem("sort_step")
            to_swap = sem("to_swap")
            swapped = sem("swapped")
            decoded = sem("decoded")

            with nc.Block() as block:
                @block.sync
                def _(sp):
                    for j in range(2):
                        sp.sem_inc(k_stored[j], 32)
                    sp.dma_start(srcs[:, :], src.rearrange("(p t) -> p t", p=ER)).then_inc(edges_in, 16)
                    sp.dma_start(dsts[:, :], dst.rearrange("(p t) -> p t", p=ER)).then_inc(edges_in, 16)
                    sp.wait_ge(cleared, 1)
                    sp.dma_start(xres[:, 0:NBF, :],
                                 x[0:NBF * P, :].rearrange("(b p) d -> p b d", p=P)).then_inc(x_in, 16)
                    sp.dma_start(xres[0:TAIL, NBF, :], x[NBF * P:N, :]).then_inc(x_in, 16)
                    sp.dma_start(wq_sb[:, :, :], Wq.rearrange("(c p) n -> p c n", p=P)).then_inc(w_in, 16)
                    sp.dma_start(wkv_sb[:, :, 0:D], Wk.rearrange("(c p) n -> p c n", p=P)).then_inc(w_in, 16)
                    sp.dma_start(wkv_sb[:, :, D:2 * D], Wv.rearrange("(c p) n -> p c n", p=P)).then_inc(w_in, 16)
                    for k, b in enumerate((bq, bk, bv)):
                        sp.dma_start(bias[:, k * D:(k + 1) * D],
                                     b.rearrange("(a n) -> a n", a=1).to_broadcast([3, D])).then_inc(bias_in, 16)
                    with sp.Fori(0, NB // 2) as i:
                        for j in range(2):
                            rows = bass.ds((i * 2 + j) * P, P)
                            sp.wait_ge(kv_ready, i * 2 + j + 1)
                            sp.dma_start(k_table[rows, :], kv_out[:, j, 0:D]).then_inc(k_stored[j], 16)
                            sp.dma_start(v_table[rows, :], kv_out[:, j, D:2 * D]).then_inc(k_stored[j], 16)
                    for j in range(2):
                        sp.wait_ge(k_stored[j], 16 * NB + 32)

                @block.gpsimd
                def _(pool):
                    nc.gpsimd.memset(ident[:, :], 0.0).then_inc(consts, 1)
                    nc.gpsimd.memset(ones[:, :], 1.0).then_inc(consts, 1)
                    pool.wait_ge(consts, 2)
                    nc.gpsimd.affine_select(out=ident[:, :], in_=ident[:, :], compare_op=ALU.not_equal, fill=1.0,
                                            base=0, pattern=[[-1, P]], channel_multiplier=1).then_inc(consts, 1)
                    nc.gpsimd.iota(lane[:, :], [[0, 1]], base=0, channel_multiplier=1).then_inc(consts, 1)
                    nc.gpsimd.iota(blkno_i[:, :], [[1, NBR]], base=0, channel_multiplier=0).then_inc(consts, 1)
                    nc.gpsimd.memset(minus_half[:, :], -0.5).then_inc(consts, 1)
                    nc.gpsimd.memset(ones_h[:, :], 1.0).then_inc(consts, 1)
                    pool.wait_ge(consts, 7)
                    pool.wait_ge(var_ready, 1)
                    nc.gpsimd.tensor_tensor(rstd[:, :], var[:, :], minus_half[:, :], ALU.pow).then_inc(rstd_ready, 1)
                    pool.wait_ge(bias_in, 48)
                    steps = [0]

                    def then(ins):
                        steps[0] += 1
                        ins.then_inc(bias_step, 1)
                        pool.wait_ge(bias_step, steps[0])

                    then(nc.gpsimd.tensor_copy(bias_cut[:, 0, :], bias[:, :]))
                    then(nc.gpsimd.tensor_tensor(bias_rest[:, :], bias[:, :], bias_cut[:, 0, :], ALU.subtract))
                    then(nc.gpsimd.tensor_copy(bias_cut[:, 1, :], bias_rest[:, :]))
                    then(nc.gpsimd.tensor_tensor(bias_cut[:, 2, :], bias_rest[:, :], bias_cut[:, 1, :], ALU.subtract))
                    for k in range(3):
                        then(nc.gpsimd.tensor_scalar(bias_cut[:, k, :], bias_cut[:, k, :], ident[0:3, k:k + 1], None,
                                                     ALU.mult))
                    then(nc.gpsimd.tensor_tensor(bias_parts[:, :], bias_cut[:, 0, :], bias_cut[:, 1, :], ALU.add))
                    then(nc.gpsimd.tensor_tensor(bias_parts[:, :], bias_parts[:, :], bias_cut[:, 2, :], ALU.add))

                    def hand_over(b, j):
                        pool.wait_ge(xhat_ready, b + 1)
                        pool.wait_ge(xin_free, b + 1)
                        nc.gpsimd.tensor_copy(xin[:, j, :], block_of(xhat, b)).then_inc(xin_ready, 1)

                    def split_q(b, j):
                        first, second, third = (block_of(q_parts[:, k], b) for k in range(3))
                        pool.wait_ge(q_kept, b + 1)
                        nc.gpsimd.tensor_copy(first, q_full[:, j, :]).then_inc(q_cut, 1)
                        pool.wait_ge(q_cut, b * 4 + 8 + 1)
                        pool.sem_inc(q_turns, 1)
                        nc.gpsimd.tensor_tensor(q_rest[:, j, :], q_full[:, j, :], first, ALU.subtract).then_inc(q_cut, 1)
                        pool.wait_ge(q_cut, b * 4 + 8 + 2)
                        nc.gpsimd.tensor_copy(second, q_rest[:, j, :]).then_inc(q_cut, 1)
                        pool.wait_ge(q_cut, b * 4 + 8 + 3)
                        pool.sem_inc(q_turns, 1)
                        nc.gpsimd.tensor_tensor(third, q_rest[:, j, :], second, ALU.subtract).then_inc(q_cut, 1)

                    pool.sem_inc(q_cut, 8)
                    hand_over(0, 0)
                    hand_over(1, 1)
                    with pool.Fori(1, NB // 2) as i:
                        for j in range(2):
                            hand_over(i * 2 + j, j)
                            split_q(i * 2 + j - 2, j)
                    split_q(NB - 2, 0)
                    split_q(NB - 1, 1)

                @block.vector
                def _(dve):
                    steps = [0]

                    def link(ins):
                        steps[0] += 1
                        ins.then_inc(cdone, 1)
                        dve.wait_ge(cdone, steps[0])

                    nc.vector.memset(xres[:, NBF:NB, :], 0.0).then_inc(cleared, 1)
                    dve.wait_ge(edges_in, 32)
                    dve.wait_ge(consts, 5)
                    link(nc.vector.tensor_copy(lane_f[:, :], lane[:, :]))
                    link(nc.vector.tensor_copy(blkno[:, :], blkno_i[:, :]))
                    link(nc.vector.tensor_scalar(tmp_i[0:ER, 0:EC], srcs[:, :], LOGP, None, ALU.logical_shift_right))
                    link(nc.vector.tensor_copy(blkf[:, :], tmp_i[0:ER, 0:EC]))
                    for b in range(NBR):
                        nc.vector.tensor_scalar(inblk[:, b, :], blkf[:, :], float(b), None, ALU.is_equal)
                    link(nc.vector.tensor_scalar(padkey[:, :], blkno[:, :], float(P * RADIX),
                                                 float((P - 1) * RADIX + PAD_DST - FILL), ALU.mult, ALU.add))
                    for j in range(LOGP):
                        nc.vector.tensor_scalar(dir_i[:, j:j + 1], lane[:, :], j, 1, ALU.logical_shift_right,
                                                ALU.bitwise_and)
                    link(nc.vector.memset(keys[1][:, :], float(FILL)))
                    link(nc.vector.tensor_copy(dirs[:, :], dir_i[:, :]))
                    link(nc.vector.tensor_scalar(dirs[:, :], dirs[:, :], -2.0, 1.0, ALU.mult, ALU.add))
                    link(nc.vector.scalar_tensor_tensor(out=keys[1][0:ER, 0:EC], in0=srcs[:, :], scalar=float(RADIX),
                                                        in1=dsts[:, :], op0=ALU.mult, op1=ALU.add))
                    dve.wait_ge(x_in, 32)
                    for b in range(NB):
                        nc.vector.bn_stats(stats[:, b, :], xres[:, b, :]).then_inc(stats_made, 1)
                    dve.wait_ge(stats_made, NB)
                    mean_and_variance(link)
                    nc.vector.tensor_copy(var[:, :], var[:, :]).then_inc(var_ready, 1)
                    nc.vector.tensor_reduce(cnt[:, :], inblk[:, :, :], AX.X, ALU.add).then_inc(counted, 1)
                    dve.wait_ge(rstd_ready, 1)
                    for b in range(NB):
                        nc.vector.tensor_scalar(xhat[:, b, :], xres[:, b, :], mean[:, b:b + 1], rstd[:, b:b + 1],
                                                ALU.subtract, ALU.mult).then_inc(xhat_ready, 1)
                    dve.wait_ge(cnt_sum, 1)
                    link(nc.vector.tensor_scalar(need[:, :], cnt_ps[:, :], -1.0, float(SORT), ALU.mult, ALU.add))
                    link(nc.vector.tensor_copy(need_i[:, :], need[:, :]))
                    link(nc.vector.tensor_scalar(need_i[:, :], need_i[:, :], P - 1, None, ALU.bitwise_and))
                    link(nc.vector.tensor_copy(need[:, :], need_i[:, :]))
                    link(nc.vector.scalar_tensor_tensor(out=need[:, :], in0=need[:, :], scalar=lane_f[:, 0:1],
                                                        in1=padkey[:, :], op0=ALU.is_gt, op1=ALU.mult))
                    link(nc.vector.tensor_scalar(keys[1][:, EC:EC + NBR], need[:, :], float(FILL), None, ALU.add))

                    n, swaps = 0, 0
                    source = keys[1]

                    def column_bit(bit, low):
                        if low:
                            return bit if bit < LOGP else (bit - LOGP if bit >= 2 * LOGP else None)
                        return bit - LOGP

                    def settle(ins):
                        nonlocal n
                        n += 1
                        ins.then_inc(sort_step, 1)
                        dve.wait_ge(sort_step, n)

                    def exchanges(bits, low, after_swap, swap_next, to_come=0):
                        nonlocal n, source
                        for left, bit in zip(range(len(bits) - 1, -1, -1), bits):
                            w = 1 << column_bit(bit, low)
                            target = keys[1 - (left + to_come) % 2]
                            s = source[:, :].rearrange("p (h t w) -> p h t w", t=2, w=w)
                            d = target[:, :].rearrange("p (h t w) -> p h t w", t=2, w=w)
                            first, second = s[:, :, 0, :], s[:, :, 1, :]
                            if left == len(bits) - 1 and after_swap:
                                second = half[:, :].rearrange("p (h w) -> p h w", w=w)
                                settle(nc.vector.tensor_copy(second, s[:, :, 1, :]))
                            lesser = nc.vector.tensor_tensor(d[:, :, 0, :], first, second, ALU.min)
                            if left == 0 and swap_next:
                                settle(lesser)
                            greater = nc.vector.tensor_tensor(d[:, :, 1, :], first, second, ALU.max)
                            if left == 0 and swap_next:
                                greater.then_inc(to_swap, 1)
                            else:
                                settle(greater)
                            source = target

                    def negate(bit, swap_next=False):
                        col = column_bit(bit, True)
                        s = source[:, :]
                        by = dirs[:, bit - LOGP:bit - LOGP + 1] if col is None else -1.0
                        if col is not None:
                            s = s.rearrange("p (h t w) -> p h t w", t=2, w=1 << col)[:, :, 1, :]
                        ins = nc.vector.tensor_scalar(s, s, by, None, ALU.mult)
                        if swap_next:
                            ins.then_inc(to_swap, 1)
                        else:
                            settle(ins)

                    def swap_layout():
                        nonlocal swaps, source
                        swaps += 1
                        dve.wait_ge(swapped, swaps)
                        source = swap_ps[(swaps - 1) % 2]

                    low_bits = list(range(LOGP - 1, -1, -1))
                    for k in range(1, LOGP + 1):
                        if k > 1:
                            negate(k - 1)
                        negate(k)
                        exchanges(list(range(k - 1, -1, -1)), True, False, False,
                                  to_come=sum(range(k + 1, LOGP + 1)))
                    for k in range(LOGP + 1, LOGN + 1):
                        negate(k - 1, swap_next=(k == LOGN))
                        if k < LOGN:
                            negate(k, swap_next=True)
                        swap_layout()
                        exchanges(list(range(k - 1, LOGP - 1, -1)), False, True, True)
                        swap_layout()
                        exchanges(low_bits, True, True, k == LOGN)
                    swap_layout()

                    n = 0

                    def then(ins):
                        nonlocal n
                        n += 1
                        ins.then_inc(decoded, 1)
                        dve.wait_ge(decoded, n)

                    then(nc.vector.tensor_copy(key_i[:, :], source[:, :]))
                    then(nc.vector.tensor_scalar(tmp_i[:, :], key_i[:, :], SHIFT, None, ALU.logical_shift_right))
                    then(nc.vector.tensor_copy(src_f[:, :], tmp_i[:, :]))
                    then(nc.vector.tensor_scalar(blk_i[:, :], tmp_i[:, :], LOGP, None, ALU.logical_shift_right))
                    then(nc.vector.tensor_scalar(tmp_i[:, :], tmp_i[:, :], P - 1, None, ALU.bitwise_and))
                    then(nc.vector.tensor_copy(rel_f[:, :], tmp_i[:, :]))
                    then(nc.vector.tensor_scalar(tmp_i[:, :], key_i[:, :], RADIX - 1, None, ALU.bitwise_and))
                    then(nc.vector.tensor_copy(tmp_f[:, :], tmp_i[:, :]))
                    then(nc.vector.tensor_scalar(real_f[:, :], tmp_f[:, :], float(PAD_DST), None, ALU.is_lt))
                    then(nc.vector.tensor_scalar(dst_i[:, :], tmp_f[:, :], float(N - 1), None, ALU.min))

                @block.tensor
                def _(pe):
                    pe.wait_ge(consts, 3)
                    pe.sem_inc(xin_free, 2)

                    def project(b, j):
                        pe.wait_ge(xin_ready, b + 1)
                        for c in range(KC):
                            ins = nc.tensor.transpose(xT_ps[:, j, c, :], xin[:, j, c * P:(c + 1) * P], ident[:, :])
                        ins.then_inc(xT_made, 1)
                        pe.wait_ge(xT_ready, b + 1)
                        pe.wait_ge(w_in, 48)
                        for c in range(KC):
                            nc.tensor.matmul(q_ps[:, j, :], xT[:, j, c, :], wq_sb[:, c, :], start=(c == 0), stop=False)
                        nc.tensor.matmul(q_ps[:, j, :], ones_h[:, :], bias_parts[:, 0:D], start=False,
                                         stop=True).then_inc(q_made, 1)
                        for c in range(KC):
                            ins = nc.tensor.matmul(kv_ps[j][:, :], xT[:, j, c, :], wkv_sb[:, c, :], start=(c == 0), stop=False)
                        ins.then_inc(xin_free, 1)
                        nc.tensor.matmul(kv_ps[j][:, :], ones_h[:, :], bias_parts[:, D:3 * D], start=False,
                                         stop=True).then_inc(kv_made, 1)

                    def swap(i, j):
                        pe.wait_ge(to_swap, i + 1)
                        for g in range(SC // P):
                            ins = nc.tensor.transpose(swap_ps[j][:, g * P:(g + 1) * P], keys[1][:, g * P:(g + 1) * P], ident[:, :])
                        ins.then_inc(swapped, 1)

                    pe.wait_ge(counted, 1)
                    nc.tensor.matmul(cnt_ps[:, :], ones[0:ER, :], cnt[:, :], start=True, stop=True).then_inc(cnt_sum, 1)
                    ROUNDS, SHORT, LONG = LOGN - LOGP, 4, 4
                    MIDDLE = ROUNDS - SHORT - LONG
                    HEAD = NB - SHORT - 2 * MIDDLE - 4 * LONG
                    assert HEAD % 2 == 0 and SHORT % 2 == 0
                    pe.wait_ge(bias_step, 9)
                    with pe.Fori(0, HEAD // 2) as i:
                        project(i * 2, 0)
                        project(i * 2 + 1, 1)
                    with pe.Fori(0, SHORT // 2) as i:
                        for j in range(2):
                            swap(i * 4 + j * 2, 0)
                            swap(i * 4 + j * 2 + 1, 1)
                            project(i * 2 + HEAD + j, j)
                    with pe.Fori(0, MIDDLE) as i:
                        for j in range(2):
                            swap(i * 2 + 2 * SHORT + j, j)
                            project(i * 2 + HEAD + SHORT + j, j)
                    with pe.Fori(0, LONG - 1) as i:
                        for j in range(2):
                            swap(i * 2 + 2 * (SHORT + MIDDLE) + j, j)
                            for k in range(2):
                                project(i * 4 + HEAD + SHORT + 2 * MIDDLE + j * 2 + k, k)
                    swap(2 * ROUNDS - 2, 0)
                    project(NB - 4, 0)
                    project(NB - 3, 1)
                    swap(2 * ROUNDS - 1, 1)
                    project(NB - 2, 0)
                    swap(2 * ROUNDS, 0)
                    project(NB - 1, 1)

                @block.scalar
                def _(act):
                    with act.Fori(0, NB // 2) as i:
                        for j in range(2):
                            b = i * 2 + j
                            act.wait_ge(xT_made, b + 1)
                            nc.scalar.activation(xT[:, j, :, :], xT_ps[:, j, :, :], ACT.Copy).then_inc(xT_ready, 1)
                            act.wait_ge(q_made, b + 1)
                            act.wait_ge(q_cut, b * 4 + 2)
                            nc.scalar.activation(q_full[:, j, :], q_ps[:, j, :], ACT.Copy,
                                                 scale=SCALE).then_inc(q_kept, 1)
                            act.wait_ge(kv_made, b + 1)
                            act.wait_ge(k_stored[j], i * 32 + 32)
                            nc.scalar.activation(kv_out[:, j, :], kv_ps[j][:, :], ACT.Copy).then_inc(kv_ready, 1)

        TR = NT // U
        lane_row = sb("lane_row", [P, P], F32, gnn)
        lane_row_i = sb("lane_row_i", [P, P], I32, gnn)
        idx_ring = sb("idx_ring", [P, UV // 8, 8], I32, gnn)
        wo_sb = sb("wo_sb", [P, KC, D], F32, gnn)
        bo_sb = sb("bo_sb", [P, D], F32, gnn)
        wr_sb = sb("wr_sb", [P, KC, NX], F32, gnn)
        br_sb = sb("br_sb", [1, NX], F32, gnn)
        att_st = ExitStack()
        att_st.__enter__()
        weights = sb("weights", [P, NT + 4, HEADS], F32, att_st)
        H8 = U // 2

        def load_blocks(eng, name, first, count):
            regs = [eng.alloc_register(f"{name}{k}") for k in range(count)]
            eng.reg_load(regs, blk_i[0:1, bass.ds(first, count)])
            return [eng.snap(reg, donate=True, min_val=0, max_val=NB - 1) for reg in regs]

        def gather_rows(pool, table, row_ring, fetched, used, copied, turns, extra):
            tiles = row_ring.shape[1]
            sets = tiles // idx_ring.shape[2]
            I8 = idx_ring.shape[2]

            def copy_indices(first, s):
                nc.gpsimd.tensor_copy(idx_ring[:, s, :], dst_i[:, bass.ds(first, I8)]).then_inc(copied, 1)

            def gather(slot, free):
                if slot % 2 == 0:
                    pool.wait_ge(used, free)
                    pool.sem_inc(turns, 1)
                at = slot % I8
                nc.gpsimd.indirect_dma_start(
                    row_ring[:, slot, :], None, table,
                    bass.IndirectOffsetOnAxis(idx_ring[:, slot // I8, at:at + 1].bitcast(U32), 0)
                ).then_inc(fetched[slot // 2], 16)

            nc.gpsimd.tensor_copy(idx_ring[:, 0, :], dst_i[:, 0:I8]).then_inc(copied, 1)
            with pool.Fori(0, NT // tiles) as i:
                for g in range(tiles // I8):
                    pool.wait_ge(copied, i * (tiles // I8) + g + 1)
                    for j in range(I8):
                        slot = g * I8 + j
                        gather(slot, i * (tiles // 2) + slot // 2 + 1)
                        if j == I8 - 2:
                            pool.wait_ge(used, i * (tiles // 2) + (g + 2) * I8 // 2)
                            copy_indices(i * tiles + (g + 1) * I8, (g + 1) % sets)
            pool.wait_ge(copied, NT // I8 + 1)
            for slot in range(extra):
                gather(slot, NT // 2 + slot // 2 + 1)
            for pair in range(tiles // 2):
                pool.wait_ge(fetched[pair], 32 * (NT // tiles + (pair < extra // 2)))

        W = TR * P
        PER = 4
        GROUPS = [list(range(g, min(g + PER, TR))) for g in range(0, TR, PER)]
        NG = len(GROUPS)

        def softmax_marks(loan):
            return loan.take((W + 1,)), loan.take((4,))

        with ExitStack() as st:
            loan = Loan(w1_words)
            off, ends = softmax_marks(loan)
            src_perm = loan.take((TR, U, HEADS))
            src_rows = loan.take((W,))
            src_ps = [psum(f"src_ps{i}", [P, PER * P], st) for i in range(2)]
            src_ready = sem("src_ready")
            src_turned = sem("src_turned")
            src_kept = sem("src_kept")
            mark = sem("mark")
            k_ring = loan.take((U, D))
            onehot = loan.take((8, P), BF16)
            onehotT = loan.take((2, 2, P), BF16)
            ident_h = loan.take((P,), BF16)
            prod = loan.take((2, 2, D))
            oT_ps = [psum(f"oT_ps{i}", [P, 2, P], st, BF16) for i in range(2)]
            qe_ps = [psum(f"qe_ps{i}", [P, 2, D], st) for i in range(4)]
            k_in = [sem(f"k_in{i}") for i in range(H8)]
            k_copied = sem("k_copied")
            k_turns = sem("k_turns")
            lane_made = sem("lane_made")
            hot_ready = sem("hot_ready")
            hotT_made = sem("hotT_made")
            hotT_ready = sem("hotT_ready")
            qe_made = sem("qe_made")
            qk_done = sem("qk_done")
            scored = sem("scored")
            with nc.Block() as block:
                @block.gpsimd
                def _(pool):
                    nc.gpsimd.iota(lane_row_i[:, :], [[1, P]], base=0, channel_multiplier=0).then_inc(lane_made, 1)
                    gather_rows(pool, k_table, k_ring, k_in, qk_done, k_copied, k_turns, 0)

                @block.vector
                def _(dve):
                    dve.sem_inc(qk_done, H8)
                    nc.vector.tensor_copy(ident_h[:, :], ident[:, :]).then_inc(lane_made, 1)
                    dve.wait_ge(lane_made, 2)
                    nc.vector.tensor_copy(lane_row[:, :], lane_row_i[:, :]).then_inc(lane_made, 1)
                    dve.wait_ge(lane_made, 3)

                    def hots(p, slot):
                        nc.vector.tensor_tensor(onehot[:, slot * 2:slot * 2 + 2, :],
                                                lane_row[:, :].unsqueeze(1).to_broadcast([P, 2, P]),
                                                rel_f[:, bass.ds(p * 2, 2)].unsqueeze(2).to_broadcast([P, 2, P]),
                                                ALU.is_equal).then_inc(hot_ready, 1)

                    for p in range(3):
                        hots(p, p)
                    srcs_by_row = src_f[:, 0:NT].rearrange("p (r q) -> p q r", q=TR).unsqueeze(3)\
                        .to_broadcast([P, TR, U, HEADS])
                    for q in range(TR):
                        ins = nc.vector.tensor_copy(src_perm[:, q], srcs_by_row[:, q])
                    ins.then_inc(src_ready, 1)

                    def score_step(i):
                        for j in range(H8):
                            p = i * H8 + j
                            dve.wait_ge(k_in[j], i * 32 + 32)
                            dve.wait_ge(qe_made, p + 1)
                            nc.vector.tensor_tensor(prod[:, j % 2], qe_ps[j % 4][:, :, :],
                                                    k_ring[:, j * 2:j * 2 + 2, :], ALU.mult).then_inc(qk_done, 1)
                            hots(p + 3, (j + 3) % 4)
                            dve.wait_ge(qk_done, p + 1 + H8)
                            nc.vector.tensor_reduce(scores[:, bass.ds(p * 2, 2), :],
                                                    prod[:, j % 2].rearrange("p t (d h) -> p t h d", h=HEADS),
                                                    AX.X, ALU.add).then_inc(scored, 1)

                    with dve.Fori(0, TR // 2) as i:
                        score_step(i)
                    dve.wait_ge(src_kept, NG)
                    nc.vector.tensor_copy(ends[:, 0:1], src_rows[:, 0:1])
                    nc.vector.tensor_copy(ends[:, 1:2], src_rows[:, W - 1:W])
                    nc.vector.memset(off[:, 0:1], 0.0)
                    nc.vector.memset(off[:, W:W + 1], 0.0)
                    nc.vector.tensor_tensor(off[:, 1:W], src_rows[:, 1:W], src_rows[:, 0:W - 1],
                                            ALU.not_equal).then_inc(mark, 1)
                    dve.wait_ge(mark, 1)
                    nc.vector.tensor_scalar(off[:, 1:W], off[:, 1:W], -BIG, None, ALU.mult)
                    with dve.Fori(TR // 2, TR) as i:
                        score_step(i)

                @block.tensor
                def _(pe):
                    def turn(p, j):
                        pe.wait_ge(hot_ready, p + 1)
                        for k in range(2):
                            ins = nc.tensor.transpose(oT_ps[j % 2][:, k, :], onehot[:, j % 4 * 2 + k, :], ident_h[:, :])
                        ins.then_inc(hotT_made, 1)

                    turn(0, 0)
                    pe.wait_ge(src_ready, 1)
                    for g, qs in enumerate(GROUPS):
                        if g >= 2:
                            pe.wait_ge(src_kept, g - 1)
                        for k, q in enumerate(qs):
                            ins = nc.tensor.transpose(src_ps[g % 2][:, k * P:(k + 1) * P],
                                                      src_perm[:, q].rearrange("p r h -> p (r h)"), ident[:, :])
                        ins.then_inc(src_turned, 1)
                    with pe.Fori(0, TR) as i:
                        regs = load_blocks(pe, "q_block", i * U, U)
                        for j in range(H8):
                            p = i * H8 + j
                            turn(p + 1, j + 1)
                            pe.wait_ge(hotT_ready, p + 1)
                            pe.wait_ge(qk_done, p + H8 - 3)
                            for k, b in enumerate(regs[j * 2:j * 2 + 2]):
                                for part in range(3):
                                    ins = nc.tensor.matmul(qe_ps[j % 4][:, k, :], onehotT[:, j % 2, k, :],
                                                           block_of(q_parts[:, part], b), start=(part == 0),
                                                           stop=(part == 2))
                            ins.then_inc(qe_made, 1)

                @block.scalar
                def _(act):
                    def keep(p, j):
                        act.wait_ge(hotT_made, p + 1)
                        nc.scalar.activation(onehotT[:, j % 2], oT_ps[j % 2][:, :, :], ACT.Copy).then_inc(hotT_ready, 1)

                    for g, qs in enumerate(GROUPS):
                        act.wait_ge(src_turned, g + 1)
                        nc.scalar.activation(src_rows[:, qs[0] * P:(qs[-1] + 1) * P], src_ps[g % 2][:, 0:len(qs) * P],
                                             ACT.Copy).then_inc(src_kept, 1)
                    with act.Fori(0, TR) as i:
                        for j in range(H8):
                            keep(i * H8 + j, j)
                    keep(NT // 2, 0)

        DZ = D + HEADS
        HV = UV // 2
        acc = Loan(now_words).take((NB + 2, DZ))
        with ExitStack() as st:
            banks = [psum(f"att_bank{i}", [P, 512], st) for i in range(8)]
            loan = Loan(w2_words)
            v_ring = loan.take((UV, D))
            onehot = loan.take((8, P))
            pv = Loan(scores.rearrange("p t h -> p (t h)")).take((8, DZ))
            v_in = [sem(f"v_in{i}") for i in range(UV // 2)]
            v_copied = sem("v_copied")
            v_turns = sem("v_turns")
            acc_clear = sem("acc_clear")
            pv_ready = sem("pv_ready")
            w_ready = sem("w_ready")
            agg_made = sem("agg_made")
            acc_done = sem("acc_done")
            w1_in = sem("w1_in")
            wo_in = sem("wo_in")
            loan = Loan(w1_words)
            off, ends = softmax_marks(loan)
            perm = loan.take((TR, U, HEADS))
            sT = loan.take((W,))
            fwd = loan.take((W,))
            bwd = scores.rearrange("p t h -> p (t h)")
            pen = loan.take((NT,))
            rows = loan.take((4, HEADS, U))[0:1]
            f_row, l_row, lf_row, lb_row = (rows[:, k] for k in range(4))
            whole = loan.take((HEADS, U))[0:1]
            cont = loan.take((2, HEADS, U))[0:1]
            step_off = loan.take((HEADS, U))[0:1]
            run = loan.take((2, HEADS, U))[0:1]
            carry = loan.take((2, U, HEADS))[0:1]
            carry_col = loan.take((2,))
            turn_ps = banks[0:4]
            small_ps = banks[4][0:1, :].rearrange("a (k p) -> a k p", p=P)
            carry_ps = banks[5][:, 0:2]
            agg_ps = banks
            sm = sem("sm")
            perm_ready = sem("perm_ready")
            turned = sem("turned")
            evacuated = sem("evacuated")
            ends_ready = sem("ends_ready")
            rows_made = sem("rows_made")
            carry_ready = sem("carry_ready")
            carry_made = sem("carry_made")
            diff_ready = sem("diff_ready")
            exp_ready = sem("exp_ready")
            DONE = NG + TR
            with nc.Block() as block:
                @block.sync
                def _(sp):
                    sp.dma_start(wo_sb[:, :, :], Wo.rearrange("(c p) n -> p c n", p=P)).then_inc(wo_in, 16)
                    sp.dma_start(bo_sb[:, :], bo.rearrange("(a n) -> a n", a=1).to_broadcast([P, D])).then_inc(wo_in, 16)
                    sp.dma_start(wr_sb[:, :, :], Wr.rearrange("(c p) n -> p c n", p=P)).then_inc(wo_in, 16)
                    sp.dma_start(br_sb[:, :], br.rearrange("(a n) -> a n", a=1)).then_inc(wo_in, 16)
                    sp.wait_ge(wo_in, 64)
                    sp.wait_ge(evacuated, DONE)
                    for e in range(NX):
                        sp.dma_start(w1_sb[:, e], W1[e].rearrange("(c p) h -> p c h", p=P)).then_inc(w1_in, 16)
                    sp.wait_ge(w1_in, 16 * NX)

                @block.gpsimd
                def _(pool):
                    nc.gpsimd.memset(acc, 0.0).then_inc(acc_clear, 1)
                    gather_rows(pool, v_table, v_ring, v_in, pv_ready, v_copied, v_turns, 4)

                @block.vector
                def _(dve):
                    dve.sem_inc(pv_ready, HV)
                    n = [0]

                    def then(ins):
                        n[0] += 1
                        ins.then_inc(sm, 1)
                        dve.wait_ge(sm, n[0])

                    by_row = scores[:, :, :].rearrange("p (r q) h -> p q r h", q=TR)
                    then(nc.vector.tensor_scalar(pen[:, :], real_f[:, 0:NT], BIG, -BIG, ALU.mult, ALU.add))
                    pens = pen[:, :].rearrange("p (r q) -> p q r", q=TR).unsqueeze(3).to_broadcast([P, TR, U, HEADS])
                    for q in range(TR):
                        nc.vector.tensor_tensor(perm[:, q], by_row[:, q], pens[:, q], ALU.add).then_inc(perm_ready, 1)
                    dve.wait_ge(evacuated, NG)

                    def scans(first_f, first_b):
                        then(nc.vector.tensor_tensor_scan(fwd[:, :], off[:, 0:W], sT[:, :], first_f, ALU.add, ALU.max))
                        then(nc.vector.tensor_tensor_scan(bwd[:, ::-1], off[:, W:0:-1], sT[:, ::-1], first_b,
                                                          ALU.add, ALU.max))

                    scans(-BIG, -BIG)
                    then(nc.vector.tensor_copy(ends[:, 2:3], fwd[:, W - 1:W]))
                    nc.vector.tensor_copy(ends[:, 3:4], bwd[:, 0:1]).then_inc(ends_ready, 1)
                    dve.wait_ge(rows_made, 1)
                    then(nc.vector.tensor_copy(rows[:, :, :, :],
                                               small_ps[:, :, :].rearrange("a k (r h) -> a k h r", h=HEADS)))
                    then(nc.vector.tensor_tensor(whole[:, :, :], f_row, l_row, ALU.is_equal))
                    then(nc.vector.memset(cont[:, :, :, :], 0.0))
                    then(nc.vector.tensor_tensor(cont[:, 0, :, 1:U], f_row[:, :, 1:U], l_row[:, :, 0:U - 1],
                                                 ALU.is_equal))
                    then(nc.vector.tensor_tensor(cont[:, 1, :, 0:U - 1], l_row[:, :, 0:U - 1], f_row[:, :, 1:U],
                                                 ALU.is_equal))

                    def flat(ap):
                        return ap.rearrange("a h r -> a (h r)")

                    for k, last in ((0, lf_row), (1, lb_row)):
                        back = slice(None) if k == 0 else slice(None, None, -1)
                        then(nc.vector.tensor_tensor(step_off[:, :, :], cont[:, k], whole[:, :, :], ALU.mult))
                        then(nc.vector.tensor_scalar(step_off[:, :, :], step_off[:, :, :], BIG, -BIG, ALU.mult, ALU.add))
                        then(nc.vector.tensor_tensor_scan(flat(run[:, k])[:, back], flat(step_off[:, :, :])[:, back],
                                                          flat(last)[:, back], -BIG, ALU.add, ALU.max))
                        then(nc.vector.tensor_scalar(cont[:, k], cont[:, k], BIG, -BIG, ALU.mult, ALU.add))
                    then(nc.vector.memset(carry[:, :, :, :], -BIG))
                    fc = carry[:, 0].rearrange("a r h -> a h r")
                    bc = carry[:, 1].rearrange("a r h -> a h r")
                    then(nc.vector.tensor_tensor(fc[:, :, 1:U], run[:, 0, :, 0:U - 1], cont[:, 0, :, 1:U], ALU.add))
                    nc.vector.tensor_tensor(bc[:, :, 0:U - 1], run[:, 1, :, 1:U], cont[:, 1, :, 0:U - 1],
                                            ALU.add).then_inc(carry_ready, 1)
                    dve.wait_ge(carry_made, 1)
                    then(nc.vector.tensor_copy(carry_col[:, :], carry_ps[:, :]))
                    scans(carry_col[:, 0:1], carry_col[:, 1:2])
                    for g, qs in enumerate(GROUPS):
                        cols = slice(qs[0] * P, (qs[-1] + 1) * P)
                        then(nc.vector.tensor_tensor(fwd[:, cols], fwd[:, cols], bwd[:, cols], ALU.max))
                        nc.vector.tensor_tensor(sT[:, cols], sT[:, cols], fwd[:, cols], ALU.subtract).then_inc(diff_ready, 1)
                    then(nc.vector.memset(weights[:, NT:NT + 4, :], 0.0))
                    w_rows = weights[:, 0:NT, :].rearrange("p (r q) h -> p q r h", q=TR)
                    real_rows = real_f[:, 0:NT].rearrange("p (r q) -> p q r", q=TR).unsqueeze(3)\
                        .to_broadcast([P, TR, U, HEADS])
                    for g, qs in enumerate(GROUPS):
                        dve.wait_ge(turned, NG + g + 1)
                        for k, q in enumerate(qs):
                            nc.vector.tensor_tensor(
                                w_rows[:, q], turn_ps[g % 4][:, k * P:(k + 1) * P].rearrange("p (r h) -> p r h", h=HEADS),
                                real_rows[:, q], ALU.mult).then_inc(evacuated, 1)

                    dve.wait_ge(evacuated, DONE)
                    dve.sem_inc(acc_done, 1)

                    def hots(p, slot):
                        nc.vector.tensor_tensor(onehot[:, slot * 2:slot * 2 + 2, :],
                                                lane_row[:, :].unsqueeze(1).to_broadcast([P, 2, P]),
                                                rel_f[:, bass.ds(p * 2, 2)].unsqueeze(2).to_broadcast([P, 2, P]),
                                                ALU.is_equal)

                    def weigh(p, j, in_round):
                        dve.wait_ge(v_in[j], in_round)
                        w = weights[:, bass.ds(p * 2, 2), :].unsqueeze(2).to_broadcast([P, 2, HD, HEADS])
                        at = j % 4 * 2
                        nc.vector.tensor_tensor(pv[:, at:at + 2, 0:D].rearrange("p t (d h) -> p t d h", h=HEADS),
                                                v_ring[:, j * 2:j * 2 + 2, :].rearrange("p t (d h) -> p t d h", h=HEADS),
                                                w, ALU.mult).then_inc(pv_ready, 1)

                    def accumulate(p, j, k, b):
                        dve.wait_ge(acc_done, p * 2 + k + 1)
                        nc.vector.tensor_tensor(block_of(acc, b), block_of(acc, b), agg_ps[j % 4 * 2 + k][:, 0:DZ],
                                                ALU.add).then_inc(acc_done, 1)

                    for p in range(2):
                        hots(p, p)
                        weigh(p, p, 32)
                    hots(2, 2)
                    dve.wait_ge(acc_clear, 1)
                    with dve.Fori(0, NT // UV) as i:
                        regs = load_blocks(dve, "v_block", i * UV, UV)
                        for j in range(HV):
                            p = i * HV + j
                            weigh(p + 2, (j + 2) % HV, i * 32 + 32 + 32 * ((j + 2) // HV))
                            dve.wait_ge(agg_made, p + 1 + 4)
                            accumulate(p, j, 0, regs[j * 2])
                            hots(p + 3, (j + 3) % 4)
                            accumulate(p, j, 1, regs[j * 2 + 1])

                @block.tensor
                def _(pe):
                    for g, qs in enumerate(GROUPS):
                        if g >= 4:
                            pe.wait_ge(evacuated, g - 3)
                        for k, q in enumerate(qs):
                            pe.wait_ge(perm_ready, q + 1)
                            ins = nc.tensor.transpose(turn_ps[g % 4][:, k * P:(k + 1) * P],
                                                      perm[:, q].rearrange("p r h -> p (r h)"), ident[:, :])
                        ins.then_inc(turned, 1)
                    pe.wait_ge(ends_ready, 1)
                    for k in range(4):
                        ins = nc.tensor.transpose(small_ps[:, k, :], ends[:, k:k + 1], ident[:, :])
                    ins.then_inc(rows_made, 1)
                    pe.wait_ge(carry_ready, 1)
                    for k in range(2):
                        ins = nc.tensor.transpose(carry_ps[:, k:k + 1], carry[:, k].rearrange("a r h -> a (r h)"),
                                                  ident[0:1, 0:1])
                    ins.then_inc(carry_made, 1)
                    for g, qs in enumerate(GROUPS):
                        pe.wait_ge(exp_ready, g + 1)
                        if g >= 4:
                            pe.wait_ge(evacuated, NG + (g - 3) * PER)
                        for k, q in enumerate(qs):
                            ins = nc.tensor.transpose(turn_ps[g % 4][:, k * P:(k + 1) * P], sT[:, q * P:(q + 1) * P],
                                                      ident[:, :])
                        ins.then_inc(turned, 1)

                    pe.sem_inc(agg_made, 4)

                    def aggregate(p, j):
                        pe.wait_ge(w_ready, p + 1)
                        pe.wait_ge(pv_ready, p + 1 + HV)
                        for k in range(2):
                            at = j % 4 * 2 + k
                            ins = nc.tensor.matmul(agg_ps[at][:, 0:DZ], onehot[:, at, :], pv[:, at, :],
                                                   start=True, stop=True)
                        ins.then_inc(agg_made, 1)

                    with pe.Fori(0, NT // UV) as i:
                        for j in range(HV):
                            aggregate(i * HV + j, j)
                    aggregate(NT // 2, 0)
                    aggregate(NT // 2 + 1, 1)

                @block.scalar
                def _(act):
                    for g, qs in enumerate(GROUPS):
                        act.wait_ge(turned, g + 1)
                        nc.scalar.activation(sT[:, qs[0] * P:(qs[-1] + 1) * P], turn_ps[g % 4][:, 0:len(qs) * P],
                                             ACT.Copy).then_inc(evacuated, 1)
                    for g, qs in enumerate(GROUPS):
                        act.wait_ge(diff_ready, g + 1)
                        cols = slice(qs[0] * P, (qs[-1] + 1) * P)
                        nc.scalar.activation(sT[:, cols], sT[:, cols], ACT.Exp).then_inc(exp_ready, 1)
                    act.wait_ge(evacuated, DONE)
                    def put_weights(p, j):
                        act.wait_ge(agg_made, p + 1)
                        at = j % 4 * 2
                        nc.scalar.activation(pv[:, at:at + 2, D:DZ], weights[:, bass.ds(p * 2, 2), :],
                                             ACT.Copy).then_inc(w_ready, 1)

                    with act.Fori(0, NT // UV) as i:
                        for j in range(HV):
                            put_weights(i * HV + j, j)
                    put_weights(NT // 2, 0)
                    put_weights(NT // 2 + 1, 1)

        att_st.close()

        x1_dram = dram("x1_dram", [(NB + 1) * P, D])
        xn_dram = dram("xn_dram", [NB * P, D + NX])
        logits = sb("logits", [P, NB, NX], F32, gnn)
        xn = xres
        with ExitStack() as st:
            att = sb("att", [P, 2, D], F32, st)
            attT = sb("attT", [P, 2, KC, P], F32, st)
            zinv = sb("zinv", [P, NB + 2, HEADS], F32, st)
            uin = sb("uin", [P, 2, D], F32, st)
            uT = sb("uT", [P, 2, KC, P], F32, st)
            aT_ps = [psum(f"aT_ps{i}", [P, KC, P], st) for i in range(2)]
            o_ps = [psum(f"o_ps{i}", [P, D], st) for i in range(2)]
            uT_ps = [psum(f"uT_ps{i}", [P, KC, P], st) for i in range(2)]
            lg_ps = [psum(f"lg_ps{i}", [P, 512], st) for i in range(2)]
            bo_added = sem("bo_added")
            nd = sem("nd")
            att_ready = sem("att_ready")
            att_turned = sem("att_turned")
            attT_ready = sem("attT_ready")
            o_made = sem("o_made")
            x1_ready = sem("x1_ready")
            x1_stored = sem("x1_stored")
            stats1 = sem("stats1")
            var1 = sem("var1")
            rstd1 = sem("rstd1")
            u_ready = sem("u_ready")
            u_kept = sem("u_kept")
            u_turned = sem("u_turned")
            uT_ready = sem("uT_ready")
            lg_made = sem("lg_made")
            lg_kept = sem("lg_kept")
            w2_in = sem("w2_in")
            with nc.Block() as block:
                @block.sync
                def _(sp):
                    with sp.Fori(0, NB) as b:
                        sp.wait_ge(x1_ready, b + 1)
                        sp.dma_start(x1_dram[bass.ds(b * P, P), :], block_of(xres, b)).then_inc(x1_stored, 16)
                    sp.wait_ge(x1_stored, 16 * NB)

                @block.gpsimd
                def _(pool):
                    with pool.Fori(0, NB) as b:
                        nc.gpsimd.tensor_tensor(block_of(xres, b), block_of(xres, b), bo_sb[:, :],
                                                ALU.add).then_inc(bo_added, 1)
                    pool.wait_ge(var1, 1)
                    nc.gpsimd.tensor_tensor(rstd[:, :], var[:, :], minus_half[:, :], ALU.pow).then_inc(rstd1, 1)
                    pool.sem_inc(u_kept, 1)
                    with pool.Fori(0, NB // 2) as i:
                        for j in range(2):
                            b = i * 2 + j
                            pool.wait_ge(u_ready, b + 1)
                            nc.gpsimd.tensor_copy(block_of(xn, b), uin[:, j, :]).then_inc(u_kept, 1)

                @block.vector
                def _(dve):
                    n = [0]

                    def link(ins):
                        n[0] += 1
                        ins.then_inc(nd, 1)
                        dve.wait_ge(nd, n[0])

                    link(nc.vector.tensor_scalar(zinv[:, :, :], acc[:, :, D:DZ], 0.5, None, ALU.max))
                    link(nc.vector.reciprocal(zinv[:, :, :], zinv[:, :, :]))

                    def normalise(b, j):
                        z = zinv[:, bass.ds(b, 1), :].to_broadcast([P, HD, HEADS])
                        sums = acc[:, bass.ds(b, 1), 0:D].rearrange("p a (d h) -> p (a d) h", h=HEADS)
                        nc.vector.tensor_tensor(att[:, j, :].rearrange("p (d h) -> p d h", h=HEADS), sums, z,
                                                ALU.mult).then_inc(att_ready, 1)

                    def row_stats(b, rows):
                        nc.vector.bn_stats(stats[:, bass.ds(b, 1), :].rearrange("p a s -> p (a s)"),
                                           rows).then_inc(stats1, 1)

                    def add_attention(b, j):
                        dve.wait_ge(o_made, b + 1)
                        dve.wait_ge(bo_added, b + 1)
                        nc.vector.tensor_tensor(block_of(xres, b), block_of(xres, b), o_ps[j][:, :],
                                                ALU.add).then_inc(x1_ready, 1)

                    normalise(0, 0)
                    normalise(1, 1)
                    with dve.Fori(0, NB // 2) as i:
                        for j in range(2):
                            b = i * 2 + j
                            dve.wait_ge(att_turned, b + 1)
                            normalise(b + 2, j)
                            add_attention(b, j)
                            dve.wait_ge(x1_ready, b + 1)
                            row_stats(b, block_of(xres, b))
                    dve.wait_ge(stats1, NB)
                    mean_and_variance(link)
                    nc.vector.tensor_copy(var[:, :], var[:, :]).then_inc(var1, 1)
                    dve.wait_ge(rstd1, 1)
                    dve.wait_ge(x1_stored, 16 * NB)

                    def first_norm(b, j):
                        nc.vector.tensor_scalar(uin[:, j, :], block_of(xres, b), mean[:, bass.ds(b, 1)],
                                                rstd[:, bass.ds(b, 1)], ALU.subtract, ALU.mult).then_inc(u_ready, 1)

                    first_norm(0, 0)
                    with dve.Fori(0, NB // 2 - 1) as i:
                        for j in range(2):
                            b = i * 2 + j
                            dve.wait_ge(u_kept, b + 1)
                            dve.wait_ge(u_turned, b + 1)
                            dve.wait_ge(stats1, NB + b)
                            first_norm(b + 1, 1 - j)
                            dve.wait_ge(u_ready, b + 1)
                            row_stats(b, uin[:, j, :])
                    last = NB - 2
                    dve.wait_ge(u_kept, last + 1)
                    dve.wait_ge(u_turned, last + 1)
                    dve.wait_ge(stats1, NB + last)
                    first_norm(last + 1, 1)
                    row_stats(last, uin[:, 0, :])
                    dve.wait_ge(u_ready, NB)
                    row_stats(last + 1, uin[:, 1, :])
                    dve.wait_ge(stats1, 2 * NB)
                    mean_and_variance(link)

                @block.tensor
                def _(pe):
                    def turn_att(b, j):
                        pe.wait_ge(att_ready, b + 1)
                        for c in range(KC):
                            ins = nc.tensor.transpose(aT_ps[j][:, c, :], att[:, j, c * P:(c + 1) * P], ident[:, :])
                        ins.then_inc(att_turned, 1)

                    turn_att(0, 0)
                    with pe.Fori(0, NB // 2) as i:
                        for j in range(2):
                            b = i * 2 + j
                            turn_att(b + 1, 1 - j)
                            pe.wait_ge(attT_ready, b + 1)
                            for c in range(KC):
                                ins = nc.tensor.matmul(o_ps[j][:, :], attT[:, j, c, :], wo_sb[:, c, :],
                                                       start=(c == 0), stop=(c == KC - 1))
                            ins.then_inc(o_made, 1)

                    def turn_u(b, j):
                        pe.wait_ge(u_ready, b + 1)
                        for c in range(KC):
                            ins = nc.tensor.transpose(uT_ps[j][:, c, :], uin[:, j, c * P:(c + 1) * P], ident[:, :])
                        ins.then_inc(u_turned, 1)

                    def form_logits(b, j):
                        pe.wait_ge(uT_ready, b + 1)
                        for c in range(KC):
                            nc.tensor.matmul(lg_ps[j][:, 0:NX], uT[:, j, c, :], wr_sb[:, c, :], start=(c == 0), stop=False)
                        nc.tensor.matmul(lg_ps[j][:, 0:NX], ones_row, br_sb[:, :], start=False,
                                         stop=True).then_inc(lg_made, 1)

                    pe.sem_inc(u_turned, 1)
                    turn_u(0, 0)
                    with pe.Fori(0, NB // 2 - 1) as i:
                        for j in range(2):
                            b = i * 2 + j
                            turn_u(b + 1, 1 - j)
                            form_logits(b, j)
                    turn_u(NB - 1, 1)
                    form_logits(NB - 2, 0)
                    form_logits(NB - 1, 1)

                @block.scalar
                def _(act):
                    for e in range(NX):
                        act.dma_start(w2_sb[:, e], W2[e].rearrange("(c p) d -> p c d", p=P)).then_inc(w2_in, 16)
                    def keep_attT(b, j):
                        act.wait_ge(att_turned, b + 1)
                        nc.scalar.activation(attT[:, j, :, :], aT_ps[j][:, :, :], ACT.Copy).then_inc(attT_ready, 1)

                    with act.Fori(0, NB // 2) as i:
                        for j in range(2):
                            keep_attT(i * 2 + j, j)
                    keep_attT(NB, 0)

                    def keep_uT(b, j):
                        act.wait_ge(u_turned, b + 2)
                        nc.scalar.activation(uT[:, j, :, :], uT_ps[j][:, :, :], ACT.Copy).then_inc(uT_ready, 1)

                    def keep_logits(b, j):
                        act.wait_ge(lg_made, b + 1)
                        nc.scalar.activation(block_of(logits, b), lg_ps[j][:, 0:NX], ACT.Copy).then_inc(lg_kept, 1)

                    keep_uT(0, 0)
                    with act.Fori(0, NB // 2 - 1) as i:
                        for j in range(2):
                            keep_uT(i * 2 + j + 1, 1 - j)
                            keep_logits(i * 2 + j, j)
                    keep_uT(NB - 1, 1)
                    keep_logits(NB - 2, 0)
                    keep_logits(NB - 1, 1)
                    act.wait_ge(w2_in, 16 * NX)

        with ExitStack() as st:
            ids = sb("ids", [P, 2, NB], F32, st)
            ex_no = sb("ex_no", [P, NX], F32, st)
            ex_no_i = sb("ex_no_i", [P, NX], I32, st)
            token_i = sb("token_i", [P, NB], I32, st)
            token_ok = sb("token_ok", [P, NB], F32, st)
            tile_no_i = sb("tile_no_i", [P, NS // P], I32, st)
            tile_no = sb("tile_no", [P, NS // P], F32, st)
            both = sb("both", [P, NB, NX], F32, st)
            before = sb("before", [P, P], F32, st)
            inc = sb("inc", [P, NX, NB], F32, st)
            keep = sb("keep", [P, NX, NB], F32, st)
            total = sb("total", [P, NX, NB], F32, st)
            tiles_i = sb("tiles_i", [P, NX], I32, st)
            tiles = sb("tiles", [P, NX], F32, st)
            tile_end = sb("tile_end", [P, NX], F32, st)
            base = sb("base", [P, NX], F32, st)
            one_x = sb("one_x", [P, NX], F32, st)
            place = sb("place", [P, NB, NX], F32, st)
            rowf = sb("rowf", [P, 2, NB], F32, st)
            ended = sb("ended", [P, NS // P, NX], F32, st)
            tile_f = sb("tile_f", [P, NS // P], F32, st)
            low = sb("low", [P, 2, NB], F32, st)
            pre_ps = psum("pre_ps", [P, NB, NX], st)
            tot_ps = psum("tot_ps", [P, NB, NX], st)
            HB = NB // 2
            row_i = sb("row_i", [P, 2, NB], I32, st)
            low_i = sb("low_i", [P, 2, NB], I32, st)
            by_ex = sb("by_ex", [P, NB, NX], F32, st)
            spare_row = sb("spare_row", [P, 1], F32, st)
            spare = sb("spare", [P, NS // P], F32, st)
            row_lo = sb("row_lo", [P, 2, NB], F32, st)
            row_hi = sb("row_hi", [P, 2, NB], F32, st)
            tile_no1 = sb("tile_no1", [P, NS // P], F32, st)
            block_no1 = sb("block_no1", [P, NB], F32, st)
            loan = Loan(now_words)
            hot_lo = loan.take((2, HB * P), BF16).rearrange("p g (b l) -> p g b l", l=P)
            number = loan.take((2, HB * 2 * (NS // P)), BF16).rearrange("p g (b w t) -> p g b w t", b=HB, w=2)
            hot_hi = loan.take((HB, NS // P), BF16)
            top = loan.take((NB, 8))
            top_i = loan.take((NB, 8), U32)
            pick = loan.take((2, NB * NX)).rearrange("p k (b e) -> p k b e", e=NX)
            picked = loan.take((2, NB * NX)).rearrange("p k (b e) -> p k b e", e=NX)
            number_ps = psum("number_ps", [P, 2, NS // P], st)
            rt = sem("rt")
            r_const = sem("r_const")
            gap_ready = sem("gap_ready")
            gap_exp = sem("gap_exp")
            both_ready = sem("both_ready")
            pre_made = sem("pre_made")
            numbers_ready = sem("numbers_ready")
            numbers_made = sem("numbers_made")
            b1_in = sem("b1_in")
            g_in = sem("g_in")
            xn_stored = sem("xn_stored")
            by_ex_ready = sem("by_ex_ready")
            xn_ready = sem("xn_ready")
            xn_ready_v = sem("xn_ready_v")
            rstd2 = sem("rstd2")
            POOL_B = 16

            def second_norm(eng, b, ready):
                eng.tensor_scalar(xn[:, b, :], xn[:, b, :], mean[:, b:b + 1], rstd[:, b:b + 1],
                                  ALU.subtract, ALU.mult).then_inc(ready, 1)

            with nc.Block() as block:
                @block.sync
                def _(sp):
                    sp.dma_start(b1_sb[:, :], b1.rearrange("e (k p) -> p (e k)", p=P),
                                 allow_slow_non_contiguous=True).then_inc(b1_in, 16)
                    for bs, ready in ((slice(POOL_B, NB), xn_ready_v), (slice(0, POOL_B // 2), xn_ready),
                                      (slice(POOL_B // 2, POOL_B), xn_ready)):
                        sp.wait_ge(ready, bs.stop - (POOL_B if ready is xn_ready_v else 0))
                        sp.dma_start(xn_dram.rearrange("(b p) d -> p b d", p=P)[:, bs, 0:D],
                                     xn[:, bs, :]).then_inc(xn_stored, 16)
                    sp.wait_ge(by_ex_ready, 1)
                    sp.dma_start(xn_dram.rearrange("(b p) d -> p b d", p=P)[:, :, D:D + NX],
                                 by_ex[:, :, :]).then_inc(xn_stored, 16)
                    sp.wait_ge(b1_in, 16)
                    sp.wait_ge(xn_stored, 64)

                @block.gpsimd
                def _(pool):
                    nc.gpsimd.iota(ex_no_i[:, :], [[1, NX]], base=0, channel_multiplier=0).then_inc(r_const, 1)
                    nc.gpsimd.iota(token_i[:, :], [[P, NB]], base=0, channel_multiplier=1).then_inc(r_const, 1)
                    nc.gpsimd.iota(tile_no_i[:, :], [[1, NS // P]], base=0, channel_multiplier=0).then_inc(r_const, 1)
                    nc.gpsimd.affine_select(out=before[:, :], in_=ones[:, :], compare_op=ALU.is_gt, fill=0.0,
                                            base=0, pattern=[[1, P]], channel_multiplier=-1).then_inc(r_const, 1)
                    nc.gpsimd.tensor_tensor(rstd[:, :], var[:, :], minus_half[:, :], ALU.pow).then_inc(rstd2, 1)
                    pool.wait_ge(rstd2, 1)
                    for b in range(POOL_B):
                        second_norm(nc.gpsimd, b, xn_ready)

                @block.vector
                def _(dve):
                    n = [0]

                    def link(ins):
                        n[0] += 1
                        ins.then_inc(rt, 1)
                        dve.wait_ge(rt, n[0])

                    dve.wait_ge(r_const, 3)
                    nc.vector.tensor_copy(ex_no[:, :], ex_no_i[:, :])
                    nc.vector.tensor_copy(tile_no[:, :], tile_no_i[:, :])
                    link(nc.vector.tensor_copy(token_ok[:, :], token_i[:, :]))
                    link(nc.vector.tensor_scalar(block_no1[:, :], token_ok[:, :], lane_f[:, 0:1], None, ALU.subtract))
                    link(nc.vector.tensor_scalar(token_ok[:, :], token_ok[:, :], float(N), None, ALU.is_lt))
                    for b in range(NB):
                        ins = nc.vector.max(top[:, b, :], logits[:, b, :])
                    link(ins)
                    for b in range(NB):
                        ins = nc.vector.max_index(top_i[:, b, :], top[:, b, :], logits[:, b, :])
                    link(ins)
                    nc.vector.tensor_tensor(low[:, 0, :], top[:, :, 1], top[:, :, 0], ALU.subtract).then_inc(gap_ready, 1)
                    for k in range(2):
                        link(nc.vector.tensor_copy(ids[:, k, :], top_i[:, :, k]))
                    for k in range(2):
                        ins = nc.vector.tensor_tensor(pick[:, k], ex_no[:, :].unsqueeze(1).to_broadcast([P, NB, NX]),
                                                      ids[:, k, :].unsqueeze(2).to_broadcast([P, NB, NX]), ALU.is_equal)
                    link(ins)
                    for k in range(2):
                        ins = nc.vector.tensor_tensor(pick[:, k], pick[:, k],
                                                      token_ok[:, :].unsqueeze(2).to_broadcast([P, NB, NX]), ALU.mult)
                    link(ins)
                    nc.vector.tensor_tensor(both[:, :, :], pick[:, 0], pick[:, 1], ALU.add).then_inc(both_ready, 1)
                    dve.wait_ge(rstd2, 1)
                    for b in range(POOL_B, NB):
                        second_norm(nc.vector, b, xn_ready_v)
                    dve.wait_ge(gap_exp, 1)
                    link(nc.vector.tensor_scalar(wts[:, 0, :], low[:, 1, :], 1.0, None, ALU.add))
                    link(nc.vector.reciprocal(wts[:, 0, :], wts[:, 0, :]))
                    link(nc.vector.tensor_tensor(wts[:, 1, :], wts[:, 0, :], low[:, 1, :], ALU.mult))
                    for k in range(2):
                        ins = nc.vector.tensor_tensor(picked[:, k], pick[:, k],
                                                      wts[:, k, :].unsqueeze(2).to_broadcast([P, NB, NX]), ALU.mult)
                    link(ins)
                    nc.vector.tensor_tensor(by_ex[:, :, :], picked[:, 0], picked[:, 1], ALU.add).then_inc(by_ex_ready, 1)
                    dve.wait_ge(by_ex_ready, 1)
                    link(nc.vector.memset(keep[:, :, :], 1.0))
                    link(nc.vector.memset(keep[:, :, 0:1], 0.0))
                    link(nc.vector.memset(one_x[:, :], 1.0))
                    dve.wait_ge(pre_made, 1)
                    link(nc.vector.tensor_copy(total[:, :, :], tot_ps[:, :, :].rearrange("p b e -> p e b")))
                    link(nc.vector.tensor_tensor_scan(inc[:, :, :].rearrange("p e b -> p (e b)"),
                                                      keep[:, :, :].rearrange("p e b -> p (e b)"),
                                                      total[:, :, :].rearrange("p e b -> p (e b)"), 0.0,
                                                      ALU.mult, ALU.add))
                    link(nc.vector.tensor_scalar(tiles[:, :], inc[:, :, NB - 1], float(P - 1), None, ALU.add))
                    link(nc.vector.tensor_copy(tiles_i[:, :], tiles[:, :]))
                    link(nc.vector.tensor_scalar(tiles_i[:, :], tiles_i[:, :], LOGP, None, ALU.logical_shift_right))
                    link(nc.vector.tensor_copy(tiles[:, :], tiles_i[:, :]))
                    link(nc.vector.tensor_tensor_scan(tile_end[:, :], one_x[:, :], tiles[:, :], 0.0, ALU.mult, ALU.add))
                    link(nc.vector.tensor_tensor(base[:, :], tile_end[:, :], tiles[:, :], ALU.subtract))
                    link(nc.vector.tensor_scalar(base[:, :], base[:, :], float(P), None, ALU.mult))
                    link(nc.vector.tensor_tensor(inc[:, :, :], inc[:, :, :], total[:, :, :], ALU.subtract))
                    link(nc.vector.tensor_tensor(inc[:, :, :], inc[:, :, :],
                                                 base[:, :].unsqueeze(2).to_broadcast([P, NX, NB]), ALU.add))
                    link(nc.vector.tensor_tensor(place[:, :, :], inc[:, :, :].rearrange("p e b -> p b e"),
                                                 pre_ps[:, :, :], ALU.add))
                    for k in range(2):
                        link(nc.vector.tensor_tensor(picked[:, k], pick[:, k], place[:, :, :], ALU.mult))
                        link(nc.vector.tensor_reduce(rowf[:, k], picked[:, k], AX.X, ALU.add))
                    link(nc.vector.tensor_copy(row_i[:, :, :], rowf[:, :, :]))
                    link(nc.vector.tensor_scalar(low_i[:, :, :], row_i[:, :, :], P - 1, None, ALU.bitwise_and))
                    link(nc.vector.tensor_copy(row_lo[:, :, :], low_i[:, :, :]))
                    link(nc.vector.tensor_scalar(low_i[:, :, :], row_i[:, :, :], LOGP, None, ALU.logical_shift_right))
                    link(nc.vector.tensor_copy(row_hi[:, :, :], low_i[:, :, :]))
                    link(nc.vector.tensor_scalar(row_hi[:, :, :], row_hi[:, :, :], 1.0, None, ALU.add))
                    link(nc.vector.tensor_tensor(row_hi[:, :, :], row_hi[:, :, :],
                                                 token_ok[:, :].unsqueeze(1).to_broadcast([P, 2, NB]), ALU.mult))
                    link(nc.vector.tensor_scalar(tile_no1[:, :], tile_no[:, :], 1.0, None, ALU.add))
                    link(nc.vector.tensor_scalar(block_no1[:, :], block_no1[:, :], 1.0 / P, None, ALU.mult))
                    link(nc.vector.tensor_scalar(block_no1[:, :], block_no1[:, :], 1.0, None, ALU.add))
                    for g in range(4):
                        k, bs = g // 2, slice(g % 2 * HB, (g % 2 + 1) * HB)
                        if g >= 2:
                            dve.wait_ge(numbers_made, g - 1)
                        nc.vector.tensor_tensor(hot_lo[:, g % 2], lane_row[:, :].unsqueeze(1).to_broadcast([P, HB, P]),
                                                row_lo[:, k, bs].unsqueeze(2).to_broadcast([P, HB, P]), ALU.is_equal)
                        link(nc.vector.tensor_tensor(hot_hi[:, :, :],
                                                     tile_no1[:, :].unsqueeze(1).to_broadcast([P, HB, NS // P]),
                                                     row_hi[:, k, bs].unsqueeze(2).to_broadcast([P, HB, NS // P]),
                                                     ALU.is_equal))
                        nc.vector.tensor_scalar(number[:, g % 2, :, 0, :], hot_hi[:, :, :], lane_f[:, 0:1], None, ALU.mult)
                        nc.vector.tensor_tensor(number[:, g % 2, :, 1, :], hot_hi[:, :, :],
                                                block_no1[:, bs].unsqueeze(2).to_broadcast([P, HB, NS // P]),
                                                ALU.mult).then_inc(numbers_ready, 1)
                        dve.wait_ge(numbers_ready, g + 1)
                    for e in range(NX):
                        ins = nc.vector.tensor_scalar(ended[:, :, e], tile_no[:, :], tile_end[:, e:e + 1], None,
                                                      ALU.is_ge)
                    link(ins)
                    link(nc.vector.tensor_reduce(tile_f[:, :], ended[:, :, :], AX.X, ALU.add))
                    link(nc.vector.tensor_scalar(tile_f[:, :], tile_f[:, :], float(NX - 1), None, ALU.min))
                    link(nc.vector.tensor_copy(tile_ex[:, :], tile_f[:, :]))
                    dve.wait_ge(numbers_made, 4)
                    link(nc.vector.tensor_scalar(tile_f[:, :], number_ps[:, 1, :], float(P), -float(P), ALU.mult, ALU.add))
                    link(nc.vector.tensor_scalar(tile_f[:, :], tile_f[:, :], 0.0, None, ALU.max))
                    link(nc.vector.tensor_tensor(tile_f[:, :], tile_f[:, :], number_ps[:, 0, :], ALU.add))
                    nc.vector.tensor_copy(token_of[:, :], tile_f[:, :])
                    link(nc.vector.tensor_scalar(spare_row[:, :], lane_f[:, :], float(NB * P), None, ALU.add))
                    link(nc.vector.tensor_scalar(spare[:, :], number_ps[:, 1, :], 0.0, spare_row[:, 0:1],
                                                 ALU.is_equal, ALU.mult))
                    link(nc.vector.tensor_tensor(tile_f[:, :], tile_f[:, :], spare[:, :], ALU.add))
                    link(nc.vector.tensor_copy(place_of[:, :], tile_f[:, :]))

                @block.scalar
                def _(act):
                    act.dma_start(g_sb[:, :], ln_g.rearrange("e (c p) -> p (e c)", p=P),
                                  allow_slow_non_contiguous=True).then_inc(g_in, 16)
                    act.dma_start(be_sb[:, :], ln_b.rearrange("e (c p) -> p (e c)", p=P),
                                  allow_slow_non_contiguous=True).then_inc(g_in, 16)
                    act.dma_start(b2_sb, b2.unsqueeze(0).to_broadcast([P, NX, D])).then_inc(g_in, 16)
                    act.wait_ge(gap_ready, 1)
                    nc.scalar.activation(low[:, 1, :], low[:, 0, :], ACT.Exp).then_inc(gap_exp, 1)
                    act.wait_ge(g_in, 48)

                @block.tensor
                def _(pe):
                    pe.wait_ge(both_ready, 1)
                    pe.wait_ge(r_const, 4)
                    nc.tensor.matmul(pre_ps[:, :, :].rearrange("p b e -> p (b e)"), before[:, :],
                                     both[:, :, :].rearrange("p b e -> p (b e)"), start=True, stop=True)
                    nc.tensor.matmul(tot_ps[:, :, :].rearrange("p b e -> p (b e)"), ones[:, :],
                                     both[:, :, :].rearrange("p b e -> p (b e)"), start=True,
                                     stop=True).then_inc(pre_made, 1)
                    for g in range(4):
                        pe.wait_ge(numbers_ready, g + 1)
                        for b in range(HB):
                            ins = nc.tensor.matmul(number_ps[:, :, :].rearrange("p w t -> p (w t)"), hot_lo[:, g % 2, b, :],
                                                   number[:, g % 2, b].rearrange("p w t -> p (w t)"),
                                                   start=(g == 0 and b == 0), stop=(g == 3 and b == HB - 1))
                        ins.then_inc(numbers_made, 1)

        gnn.close()
        with ExitStack() as st:
            xs = sb("xs", [P, UE, D + NX], F32, st)
            zeros = sb("zeros", [P, D], F32, st)
            w_now = sb("w_now", [P, UE], F32, st)
            xeT = sb("xeT", [P, 2, KC, P], F32, st)
            w1_ring = w1_now[:, 0:2 * KC * H].rearrange("p (s c h) -> p s c h", s=2, c=KC)
            hT = sb("hT", [P, 2, HC, P], F32, st)
            ys = sb("ys", [P, UE, D], F32, st)
            xsT_ps = psum("xsT_ps", [P, KC, P], st)
            hT_ps = [psum(f"hT_ps{i}", [P, HC // 2, P], st) for i in range(2)]
            y_ps = [psum(f"y_ps{i}", [P, D], st) for i in range(2)]
            HH = HC // 2
            token_now = sb("token_now", [P, UE], I32, st)
            place_now = sb("place_now", [P, UE], I32, st)
            put = sem("put")
            added = sem("added")
            ys_free = sem("ys_free")
            ys_biased = sem("ys_biased")
            spare_clear = sem("spare_clear")
            out_stored = sem("out_stored")
            turns = sem("turns")
            xs_in = [sem(f"xs_in{j}") for j in range(UE)]
            xs_turned = sem("xs_turned")
            xeT_ready = sem("xeT_ready")
            w1_ready = sem("w1_ready")
            h_made = sem("h_made")
            hT_ready = sem("hT_ready")
            y_made = sem("y_made")
            ys_ready = sem("ys_ready")

            def load_experts(eng, name, first, count):
                regs = [eng.alloc_register(f"{name}{k}") for k in range(count)]
                eng.reg_load(regs, tile_ex[0:1, bass.ds(first, count)])
                return [eng.snap(reg, donate=True, min_val=0, max_val=NX - 1) for reg in regs]

            with nc.Block() as block:
                @block.sync
                def _(sp):
                    sp.wait_ge(added, 16 * (TE + 1))
                    sp.dma_start(out.rearrange("n d -> (n d)").rearrange("(a m) -> a m", a=P),
                                 x1_dram[0:N, :].rearrange("n d -> (n d)").rearrange("(a m) -> a m", a=P)
                                 ).then_inc(out_stored, 16)
                    sp.wait_ge(out_stored, 16)

                @block.gpsimd
                def _(pool):
                    def fetch(j):
                        nc.gpsimd.indirect_dma_start(
                            xs[:, j, :], None, xn_dram,
                            bass.IndirectOffsetOnAxis(token_now[:, j:j + 1].bitcast(U32), 0)).then_inc(xs_in[j], 16)

                    nc.gpsimd.memset(zeros[:, :], 0.0).then_inc(spare_clear, 1)
                    nc.gpsimd.tensor_copy(token_now[:, :], token_of[:, 0:UE]).then_inc(put, 1)
                    pool.wait_ge(put, 1)
                    for j in range(UE):
                        fetch(j)
                    pool.wait_ge(spare_clear, 1)
                    pool.dma_start(x1_dram[NB * P:(NB + 1) * P, :], zeros[:, :]).then_inc(added, 16)
                    with pool.Fori(0, TE // UE) as i:
                        for j in range(UE):
                            t = i * UE + j
                            pool.wait_ge(xeT_ready, t + 1)
                            nc.gpsimd.tensor_copy(token_now[:, j:j + 1],
                                                  token_of[:, bass.ds(t + UE, 1)]).then_inc(put, 1)
                            nc.gpsimd.tensor_copy(place_now[:, j:j + 1], place_of[:, bass.ds(t, 1)]).then_inc(put, 1)
                            pool.wait_ge(put, t * 2 + 3)
                            pool.sem_inc(turns, 1)
                            fetch(j)
                            pool.wait_ge(added, (t + 1) * 16)
                            pool.sem_inc(ys_free, 1)
                            pool.wait_ge(ys_ready, t + 3)
                            pool.sem_inc(turns, 1)
                            nc.gpsimd.indirect_dma_start(
                                x1_dram, bass.IndirectOffsetOnAxis(place_now[:, j:j + 1].bitcast(U32), 0),
                                ys[:, j, :], None, compute_op=ALU.add).then_inc(added, 16)
                    for j in range(UE):
                        pool.wait_ge(xs_in[j], 16 * (TE // UE + 1))
                    pool.wait_ge(added, 16 * (TE + 1))

                @block.scalar
                def _(act):

                    def gelu(t, j, e):
                        act.wait_ge(y_made, t + 1)
                        for half in range(2):
                            act.wait_ge(h_made, t * 2 + half + 1)
                            for k in range(HH):
                                at = half * HH + k
                                ins = nc.scalar.activation(hT[:, j % 2, at, :], hT_ps[half][:, k, :], ACT.Gelu,
                                                           bias=b1_sb[:, bass.ds(e * HC + at, 1)])
                            ins.then_inc(hT_ready, 1)

                    with act.Fori(0, TE // UE) as i:
                        e = load_experts(act, "a_expert", i * UE, UE)
                        for j in range(UE):
                            gelu(i * UE + j, j, e[j])

                @block.vector
                def _(dve):
                    def scale_and_bias(t, j, e):
                        dve.wait_ge(xs_turned, t + 1)
                        for c in range(KC):
                            at = bass.ds(e * KC + c, 1)
                            ins = nc.vector.tensor_scalar(xeT[:, j % 2, c, :], xsT_ps[:, c, :], g_sb[:, at],
                                                          be_sb[:, at], ALU.mult, ALU.add)
                        slot = j % UE
                        ins = nc.vector.tensor_copy(w_now[:, slot:slot + 1], xs[:, slot, bass.ds(e + D, 1)])
                        ins.then_inc(xeT_ready, 1)

                    def fetch_w1(j, e):
                        nc.vector.tensor_copy(w1_ring[:, j % 2],
                                              w1_sb[:, bass.ds(e, 1), :, :].rearrange("p a c h -> p (a c) h")
                                              ).then_inc(w1_ready, 1)

                    dve.sem_inc(ys_ready, 2)
                    dve.sem_inc(ys_free, 3)
                    first = load_experts(dve, "v_first", 0, 2)
                    for t in range(2):
                        fetch_w1(t, first[t])
                    for t in range(2):
                        scale_and_bias(t, t, first[t])
                    with dve.Fori(0, TE // UE) as i:
                        e = load_experts(dve, "v_expert", i * UE, UE + 2)
                        for j in range(UE):
                            t = i * UE + j
                            dve.wait_ge(ys_ready, t + 1)
                            scale_and_bias(t + 2, j + 2, e[j + 2])
                            dve.wait_ge(h_made, t * 2 + 2)
                            fetch_w1(j, e[j + 2])
                            dve.wait_ge(y_made, t + 3)
                            dve.wait_ge(ys_free, t + 1)
                            nc.vector.tensor_tensor(ys[:, j, :], y_ps[j % 2][:, :], block_of(b2_sb, e[j]),
                                                    ALU.add).then_inc(ys_biased, 1)
                            dve.wait_ge(ys_biased, t + 1)
                            nc.vector.tensor_scalar(ys[:, j, :], ys[:, j, :], w_now[:, j:j + 1], None,
                                                    ALU.mult).then_inc(ys_ready, 1)

                @block.tensor
                def _(pe):
                    def turn_rows(t, slot, in_round):
                        pe.wait_ge(xs_in[slot], in_round)
                        for c in range(KC):
                            ins = nc.tensor.transpose(xsT_ps[:, c, :], xs[:, slot, c * P:(c + 1) * P], ident[:, :])
                        ins.then_inc(xs_turned, 1)

                    def first_layer(t, j):
                        pe.wait_ge(xeT_ready, t + 1)
                        pe.wait_ge(w1_ready, t + 1)
                        for half in range(2):
                            pe.wait_ge(hT_ready, t * 2 + half + 1)
                            for k in range(HH):
                                cols = slice((half * HH + k) * P, (half * HH + k + 1) * P)
                                for c in range(KC):
                                    ins = nc.tensor.matmul(hT_ps[half][:, k, :], w1_ring[:, j % 2, c, cols],
                                                           xeT[:, j % 2, c, :], start=(c == 0), stop=(c == KC - 1))
                            ins.then_inc(h_made, 1)

                    def second_layer(t, j, e):
                        for k in range(HC):
                            ins = nc.tensor.matmul(y_ps[j % 2][:, :], hT[:, j % 2, k, :],
                                                   w2_sb[:, bass.ds(e, 1), k, :].rearrange("p a d -> p (a d)"),
                                                   start=(k == 0), stop=(k == HC - 1))
                        ins.then_inc(y_made, 1)

                    pe.sem_inc(y_made, 2)
                    pe.sem_inc(hT_ready, 2)
                    turn_rows(0, 0, 16)
                    pe.wait_ge(xeT_ready, 1)
                    turn_rows(1, 1, 16)
                    first_layer(0, 0)
                    pe.wait_ge(xeT_ready, 2)
                    turn_rows(2, 2, 16)
                    with pe.Fori(0, TE // UE) as i:
                        e = load_experts(pe, "p_expert", i * UE, UE)
                        for j in range(UE):
                            t = i * UE + j
                            first_layer(t + 1, j + 1)
                            pe.wait_ge(xeT_ready, t + 3)
                            turn_rows(t + 3, (j + 3) % UE, i * 16 + 16 + 16 * ((j + 3) // UE))
                            second_layer(t, j, e[j])

        ffn.close()


_GNN = ["Wq", "bq", "Wk", "bk", "Wv", "bv", "Wo", "bo"]
_FFN = ["Wr", "br", "ln_g", "ln_b", "W1", "b1", "W2", "b2"]
_INS = ["x", "src", "dst"] + ["L0_gnn_" + n for n in _GNN] + ["L0_ffn_" + n for n in _FFN]


def kernel(**inputs):
    import numpy as _np
    import concourse.bacc as _bacc
    from concourse import mybir as _mybir
    from concourse.bass_utils import run_bass_kernel_spmd as _run

    nc = _bacc.Bacc("TRN2", target_bir_lowering=False, num_devices=1)
    arrays, args = {}, []
    for name in _INS:
        a = _np.ascontiguousarray(inputs[name])
        arrays[f"in_{name}_dram"] = a
        args.append(nc.dram_tensor(f"in_{name}_dram", a.shape, _mybir.dt.from_np(a.dtype), kind="ExternalInput").ap())
    out = nc.dram_tensor("out_dram", inputs["x"].shape, _mybir.dt.float32, kind="ExternalOutput").ap()
    gnn_moe_kernel(nc, *args, out)
    r = _run(nc, [arrays], core_ids=[0])
    return r.results[0]["out_dram"]
```
